# Optimizing a Trainium2 kernel written in Bass

```python
import numpy as np
import jax
import jax.numpy as jnp

def _softmax(x, axis=-1):
    return jax.nn.softmax(x, axis=axis)

def _gelu(x):
    return jax.nn.gelu(x, approximate=True)

def _silu(x):
    return jax.nn.silu(x)

def _sigmoid(x):
    return jax.nn.sigmoid(x)

def _layernorm(x, axis=-1, eps=1e-05):
    m = jnp.mean(x, axis=axis, keepdims=True)
    v = jnp.var(x, axis=axis, keepdims=True)
    return (x - m) / jnp.sqrt(v + eps)

def _scatter_add(tgt, idx, src, axis=0):
    return tgt.at[idx].add(src)

def _segment_sum(src, seg, n):
    return jax.ops.segment_sum(src, seg, n)
kernel_name = 'mk_sandwich_d1_jaxref_r4_12094c'

def setup_inputs(seed: int=0):
    np.random.seed(seed)
    _w = jnp.asarray

    def _L0_attn_setup():
        import jax, jax.numpy as jnp
        import numpy as np
        N_HEAD = 16
        HEAD_SIZE = 256
        EMBED = 256
        MULTI_HEAD_SIZE = HEAD_SIZE // N_HEAD
        B, S = (4, 512)
        key = jax.random.key(seed)
        k1, k2, k3, k4 = jax.random.split(key, 4)
        x = jax.random.normal(k1, (B, S, EMBED), dtype=jnp.float32)
        w_qkv = jax.random.normal(k2, (3 * HEAD_SIZE, EMBED), dtype=jnp.float32) * 0.02
        w_proj = jax.random.normal(k3, (EMBED, HEAD_SIZE), dtype=jnp.float32) * 0.02
        b_proj = jax.random.normal(k4, (EMBED,), dtype=jnp.float32) * 0.02
        return {'x': x, 'w_qkv': w_qkv, 'w_proj': w_proj, 'b_proj': b_proj}
    _L0_attn_in = _L0_attn_setup()

    def _L0_ffn_setup():
        import jax, jax.numpy as jnp
        import numpy as np
        E = 16
        F_C = 2.0
        D = 256
        I = 4 * D
        IS = 2 * D
        B, S = (4, 256)
        key = jax.random.key(seed)
        ks = jax.random.split(key, 8)
        w = 0.02
        return {'hidden_states': jax.random.normal(ks[0], (B, S, D), dtype=jnp.float32), 'gate_w': jax.random.normal(ks[1], (E, D), dtype=jnp.float32) * w, 'Wg': jax.random.normal(ks[2], (E, I, D), dtype=jnp.float32) * w, 'Wu': jax.random.normal(ks[3], (E, I, D), dtype=jnp.float32) * w, 'Wd': jax.random.normal(ks[4], (E, D, I), dtype=jnp.float32) * w, 'Sg': jax.random.normal(ks[5], (IS, D), dtype=jnp.float32) * w, 'Su': jax.random.normal(ks[6], (IS, D), dtype=jnp.float32) * w, 'Sd': jax.random.normal(ks[7], (D, IS), dtype=jnp.float32) * w}
    _L0_ffn_in = _L0_ffn_setup()
    _d = {'L0_attn_x': _L0_attn_in['x'], 'L0_attn_w_qkv': _L0_attn_in['w_qkv'], 'L0_attn_w_proj': _L0_attn_in['w_proj'], 'L0_attn_b_proj': _L0_attn_in['b_proj'], 'L0_ffn_gate_w': _L0_ffn_in['gate_w'], 'L0_ffn_Wg': _L0_ffn_in['Wg'], 'L0_ffn_Wu': _L0_ffn_in['Wu'], 'L0_ffn_Wd': _L0_ffn_in['Wd'], 'L0_ffn_Sg': _L0_ffn_in['Sg'], 'L0_ffn_Su': _L0_ffn_in['Su'], 'L0_ffn_Sd': _L0_ffn_in['Sd']}
    _x0 = _d['L0_attn_x']
    _d['L0_attn_x'] = jax.random.normal(jax.random.fold_in(jax.random.key(seed), 1), (8, 1024, 256), dtype=_x0.dtype)
    del _x0
    return _d

def reference(L0_attn_x, L0_attn_w_qkv, L0_attn_w_proj, L0_attn_b_proj, L0_ffn_gate_w, L0_ffn_Wg, L0_ffn_Wu, L0_ffn_Wd, L0_ffn_Sg, L0_ffn_Su, L0_ffn_Sd):

    def _L0_attn_ref(x, w_qkv, w_proj, b_proj):
        import jax, jax.numpy as jnp
        import numpy as np
        N_HEAD = 16
        HEAD_SIZE = 256
        EMBED = 256
        MULTI_HEAD_SIZE = HEAD_SIZE // N_HEAD
        B, S = (4, 512)
        qkv = jnp.einsum('bse,he->bsh', x, w_qkv)
        q, k, v = jnp.split(qkv, 3, axis=-1)
        scale = 1.0 / np.sqrt(MULTI_HEAD_SIZE).astype(np.float32)
        scores = jnp.einsum('bqh,bkh->bqk', q, k) * scale
        probs = jax.nn.softmax(scores, axis=-1)
        out = jnp.einsum('bqk,bkh->bqh', probs, v)
        Bn, Sn, H = out.shape
        out = jnp.swapaxes(out, 1, 2).reshape(Bn, Sn, H)
        out = jnp.einsum('bsh,eh->bse', out, w_proj) + b_proj
        return out

    def _L0_ffn_ref(hidden_states, gate_w, Wg, Wu, Wd, Sg, Su, Sd):
        import jax, jax.numpy as jnp
        import numpy as np
        E = 16
        F_C = 2.0
        D = 256
        I = 4 * D
        IS = 2 * D
        B, S = (4, 256)
        b, s, d = hidden_states.shape
        T = b * s
        C = int(T * F_C / E)
        flat_x = hidden_states.reshape(T, d)
        logits = flat_x @ gate_w.T
        scores = jax.nn.softmax(logits, axis=-1).T
        topk_weight, topk_idx = jax.lax.top_k(scores, C)
        xg = flat_x[topk_idx]
        g = jnp.einsum('ecd,eid->eci', xg, Wg)
        u = jnp.einsum('ecd,eid->eci', xg, Wu)
        h = jax.nn.gelu(g, approximate=False) * u
        eo = jnp.einsum('eci,edi->ecd', h, Wd)
        eo = eo * topk_weight[..., None]
        flat_out = jnp.zeros_like(flat_x).at[topk_idx.reshape(-1)].add(eo.reshape(-1, d))
        out = flat_out.reshape(b, s, d)
        sg = hidden_states @ Sg.T
        su = hidden_states @ Su.T
        shared = jax.nn.gelu(sg, approximate=False) * su @ Sd.T
        return out + shared
    x = L0_attn_x
    x = x + _layernorm(_L0_attn_ref(_layernorm(x, axis=-1), L0_attn_w_qkv, L0_attn_w_proj, L0_attn_b_proj), axis=-1)
    x = x + _layernorm(_L0_ffn_ref(_layernorm(x, axis=-1), L0_ffn_gate_w, L0_ffn_Wg, L0_ffn_Wu, L0_ffn_Wd, L0_ffn_Sg, L0_ffn_Su, L0_ffn_Sd), axis=-1)
    return x

_drawn_inputs = setup_inputs


def setup_inputs(seed=0):
    import zlib

    import numpy as np

    out = dict(_drawn_inputs(seed))
    spreads = {}
    factors = {}
    for name, (base, spread) in spreads.items():
        noise = np.random.default_rng([zlib.crc32(name.encode()), seed]).standard_normal(out[name].shape)
        drawn = base * np.exp(spread * noise) if base else spread * noise
        out[name] = jnp.asarray(drawn.astype(out[name].dtype))
    for name, factor in factors.items():
        out[name] = (out[name] * factor).astype(out[name].dtype)
    return out
```

```python
import numpy as np
from contextlib import ExitStack

import concourse.bass as bass
from concourse import mybir

F32 = mybir.dt.float32
F32R = mybir.dt.float32r
BF16 = mybir.dt.bfloat16
I32 = mybir.dt.int32
ALU = mybir.AluOpType
ACT = mybir.ActivationFunctionType
AX = mybir.AxisListType

NB, S, D = 8, 1024, 256
T = NB * S
P = 128
E = 16
CAP = 2 * T // E
I_EXP, I_SH = 4 * D, 2 * D
KD = D // P
NT = S // P
NU = T // 512
ROW = D + E
EPS = 1e-5
XS = 4
GROUPS, GE = 4, 4


def wait(eng, sem, value):
    if isinstance(value, int) and value <= 0:
        return
    eng.wait_ge(sem, value)


def mm3(pe, out, w_hi, w_lo, x_hi, x_lo, first, last):
    pe.matmul(out, w_hi, x_hi, start=first, stop=False)
    pe.matmul(out, w_hi, x_lo, start=False, stop=False)
    return pe.matmul(out, w_lo, x_hi, start=False, stop=last)


def layernorm_scale(v, part, mv, ve, y, shift, t, n):
    if part == 0:
        v.tensor_scalar(ve, mv[:, 0:n, 1], EPS, None, ALU.add)
        v.drain()
        v.tensor_scalar(y.bitcast(I32), ve.bitcast(I32), -0.5, 1597463007.0, ALU.mult, ALU.add)
        v.drain()
    for _ in range(1 + part):
        v.tensor_tensor(t, y, y, ALU.mult)
        v.drain()
        v.scalar_tensor_tensor(t, t, -0.5, ve, ALU.mult, ALU.mult)
        v.drain()
        last = v.scalar_tensor_tensor(y, t, 1.5, y, ALU.add, ALU.mult)
        v.drain()
    if part == 1:
        last = v.scalar_tensor_tensor(shift, mv[:, 0:n, 0], -1.0, y, ALU.mult, ALU.mult)
    return last


def rows_of(dram, b):
    return dram.rearrange("(b h p j) c -> b p h (j c)", b=NB, h=2, p=P)[b]


def setup(nc, io, c):
    with ExitStack() as ctx:
        sb = lambda n, s, d=F32: ctx.enter_context(nc.sbuf_tensor(n, s, d))
        raw = {n: sb("raw_" + n, [P, KD, D]) for n in ("wq", "wk", "wv", "wp")}
        mf = sb("mf", [P, KD, D])
        ps = ctx.enter_context(nc.psum_tensor("ps_m", [P, KD, 512], F32))
        sem = lambda n: ctx.enter_context(nc.semaphore(n))
        s_ld = {n: sem("s_ld_" + n) for n in raw}
        s_k, s_m, s_mf, s_c = sem("s_k"), sem("s_m"), sem("s_mf"), sem("s_c")
        blk = ctx.enter_context(nc.Block())

        @blk.sync
        def _(sp):
            for n in raw:
                sp.dma_start(raw[n][:, :, :], io[n]).then_inc(s_ld[n], 16)
            sp.dma_start(c.gw[:, :, :], io["gate"]).then_inc(s_c, 16)
            sp.dma_start(c.bias[:, :], io["bias"].partition_broadcast(P)).then_inc(s_c, 16)
            sp.wait_ge(s_c, 32)

        @blk.gpsimd
        def _(g):
            g.memset(c.ident[:, :], 0.0)
            g.drain()
            g.affine_select(out=c.ident[:, :], in_=c.ident[:, :], compare_op=ALU.not_equal, fill=1.0, base=0,
                            pattern=[[-1, P]], channel_multiplier=1)

        @blk.tensor
        def _(pe):
            pe.wait_ge(s_ld["wq"], 16)
            pe.wait_ge(s_ld["wk"], 16)
            for m in range(KD):
                for k in range(KD):
                    i = pe.matmul(ps[:, m, 0:D], raw["wq"][:, k, m * P:(m + 1) * P], raw["wk"][:, k, :],
                                  start=(k == 0), stop=(k == KD - 1))
            i.then_inc(s_m, 1)

        @blk.scalar
        def _(a):
            a.wait_ge(s_m, 1)
            a.activation(mf[:, :, :], ps[:, :, 0:D], ACT.Copy, scale=0.25).then_inc(s_mf, 1)

        @blk.vector
        def _(v):
            for n, dst in (("wv", c.wv), ("wp", c.wp), ("m", c.m)):
                if n == "m":
                    v.wait_ge(s_mf, 1)
                    src = mf
                else:
                    v.wait_ge(s_ld[n], 16)
                    src = raw[n]
                v.tensor_copy(dst[0][:, :, :], src[:, :, :])
                v.drain()
                v.tensor_tensor(dst[1][:, :, :], src[:, :, :], dst[0][:, :, :].bitcast(F32), ALU.subtract)


def attention(nc, io, c):
    with ExitStack() as ctx:
        sb = lambda n, s, d=F32: ctx.enter_context(nc.sbuf_tensor(n, s, d))
        pair = lambda n, s: (sb(n + "_hi", s, F32R), sb(n + "_lo", s, F32R))
        X = sb("X", [P, XS, NT, D])
        xn = sb("xn", [P, NT, D])
        xnT = pair("xnT", [P, KD, S])
        tT = pair("tT", [P, KD, S])
        V = pair("V", [P, NT, D])
        Pr = sb("Pr", [P, 2, S])
        PT = pair("PT", [P, 2, NT, P])
        O = pair("O", [P, NT, D])
        Y = sb("Y", [P, NT, D])
        XNB = sb("XNB", [P, NT, ROW])
        xn2T = sb("xn2T", [P, KD, S])
        LT = sb("LT", [E, S])
        negmax, rowsum, rinv = sb("negmax", [P, NT]), sb("rowsum", [P, NT]), sb("rinv", [P, NT])
        st = [sb(f"st{n}", [P, NT, 6]) for n in range(3)]
        mv = [sb(f"mv{n}", [P, NT, 2]) for n in range(3)]
        rs = [sb(f"rs{n}", [P, NT]) for n in range(3)]
        shift = [sb(f"shift{n}", [P, NT]) for n in range(3)]
        ve, tmp = sb("ve", [P, NT]), sb("tmp", [P, NT])
        gmax, gsum, SM = sb("gmax", [P, NT]), sb("gsum", [P, NT]), sb("SM", [P, NT, E])
        psS = ctx.enter_context(nc.psum_tensor("psS", [P, 4, 512], F32))
        psPT = ctx.enter_context(nc.psum_tensor("psPT", [P, S], F32))
        psO = ctx.enter_context(nc.psum_tensor("psO", [P, 512], F32))
        psL = ctx.enter_context(nc.psum_tensor("psL", [P, 512], F32))

        sem = lambda n: ctx.enter_context(nc.semaphore(n))
        s_x = sem("s_x")
        s_tr, s_xh, s_xl = sem("s_tr"), sem("s_xh"), sem("s_xl")
        s_tt, s_th, s_tl = sem("s_tt"), sem("s_th"), sem("s_tl")
        s_v, s_vh, s_vl = sem("s_v"), sem("s_vh"), sem("s_vl")
        s_y, s_yb = sem("s_y"), sem("s_yb")
        s_tr2, s_n2 = sem("s_tr2"), sem("s_n2")
        s_lt, s_lte, s_lg = sem("s_lt"), sem("s_lte"), sem("s_lg")
        s_s, s_max, s_exp, s_ri = sem("s_s"), sem("s_max"), sem("s_exp"), sem("s_ri")
        s_t, s_pth, s_ptl = sem("s_t"), sem("s_pth"), sem("s_ptl")
        s_pv, s_oh, s_ol = sem("s_pv"), sem("s_oh"), sem("s_ol")
        s_r1, s_xn, s_ry, s_yn, s_x1, s_r2, s_xn2 = (sem(n) for n in ("s_r1", "s_xn", "s_ry", "s_yn", "s_x1", "s_r2", "s_xn2"))
        s_sm, s_sme, s_sc = sem("s_sm"), sem("s_sme"), sem("s_sc")
        s_x1st, s_xnst, s_xtst = sem("s_x1st"), sem("s_xnst"), sem("s_xtst")
        blk = ctx.enter_context(nc.Block())

        class Round:
            def __init__(self, r, attn=True, post=True, gate=True, ln_next=True):
                self.r, self.attn, self.post, self.gate, self.ln_next = r, attn, post, gate, ln_next

        def rounds(eng, body):
            body(Round(0, post=False, gate=False))
            body(Round(1, gate=False))
            body(Round(2))
            with eng.Fori(3, NB - 1) as r:
                body(Round(r))
            body(Round(NB - 1, ln_next=False))
            body(Round(NB, attn=False, ln_next=False))
            body(Round(NB + 1, attn=False, post=False, ln_next=False))

        @blk.sync
        def _(sp):
            def slot(b):
                return X[:, b % XS, :, :].rearrange("p (h j) c -> p h (j c)", h=2)

            sp.dma_start(slot(0), rows_of(io["x"], 0)).then_inc(s_x, 16)

            def body(R):
                r = R.r
                if R.ln_next:
                    wait(sp, s_x, 16 * (r + 1))
                    wait(sp, s_x1st, 16 * (r + 2 - XS))
                    sp.dma_start(slot(r + 1), rows_of(io["x"], r + 1)).then_inc(s_x, 16)
                if R.gate:
                    wait(sp, s_n2, 4 * (r - 1))
                    sp.dma_start(io["XN2T"][r - 2], xn2T[:, :, :]).then_inc(s_xtst, 16)
                    wait(sp, s_sc, r - 1)
                    sp.dma_start(rows_of(io["XN"], r - 2),
                                 XNB[:, :, :].rearrange("p (h j) c -> p h (j c)", h=2)).then_inc(s_xnst, 16)
                if R.post:
                    wait(sp, s_x1, 2 * r)
                    sp.dma_start(rows_of(io["X1"], r - 1),
                                 slot(r - 1)).then_inc(s_x1st, 16)
            rounds(sp, body)
            sp.wait_ge(s_x1st, 16 * NB)
            sp.wait_ge(s_xnst, 16 * NB)
            sp.wait_ge(s_xtst, 16 * NB)

        @blk.tensor
        def _(pe):
            def body(R):
                r = R.r
                if R.attn:
                    wait(pe, s_xn, 2 * (r + 1))
                    for k in range(4):
                        dk, ht = k % 2, k // 2
                        if k == 0:
                            wait(pe, s_exp, 8 * r)
                        for j in range(4):
                            i = pe.transpose(psS[:, k, j * P:(j + 1) * P], xn[:, 4 * ht + j, dk * P:(dk + 1) * P], c.ident[:, :])
                        i.then_inc(s_tr, 1)
                if R.gate:
                    wait(pe, s_xn2, 2 * (r - 1))
                    for k in range(4):
                        dk, ht = k % 2, k // 2
                        if R.attn:
                            wait(pe, s_xl, 4 * r + k + 1)
                        for j in range(4):
                            i = pe.transpose(psS[:, k, j * P:(j + 1) * P], XNB[:, 4 * ht + j, dk * P:(dk + 1) * P], c.ident[:, :])
                        i.then_inc(s_tr2, 1)
                if R.post:
                    wait(pe, s_ol, 8 * r)
                    for k in range(4):
                        hm, jp = k // 2, k % 2
                        if R.gate:
                            wait(pe, s_n2, 4 * (r - 2) + k + 1)
                        elif R.attn:
                            wait(pe, s_xl, 4 * r + k + 1)
                        for jj in range(2):
                            for q in range(2):
                                ot = 2 * (2 * jp + jj) + q
                                i = mm3(pe, psS[:, k, jj * D:(jj + 1) * D],
                                        O[0][:, ot, hm * P:(hm + 1) * P], O[1][:, ot, hm * P:(hm + 1) * P],
                                        c.wp[0][:, q, :], c.wp[1][:, q, :], q == 0, q == 1)
                        i.then_inc(s_y, 1)
                if R.gate:
                    wait(pe, s_n2, 4 * (r - 1))
                    wait(pe, s_sm, r - 2)
                    wait(pe, s_ol, 8 * r if R.attn else 8 * NB)
                    for h, bank in enumerate((psL, psO)):
                        for k in range(KD):
                            i = pe.matmul(bank[0:E, :], c.gw[:, k, :], xn2T[:, k, h * 512:(h + 1) * 512],
                                          start=(k == 0), stop=(k == KD - 1))
                        i.then_inc(s_lt, 1)
                if R.attn:
                    wait(pe, s_xl, 4 * (r + 1))
                    if R.post:
                        wait(pe, s_yb, 4 * r)
                    for k in range(4):
                        m, h = k % 2, k // 2
                        for kk in range(KD):
                            w = [c.m[z][:, kk, m * P:(m + 1) * P] for z in (0, 1)]
                            x = [xnT[z][:, kk, h * 512:(h + 1) * 512] for z in (0, 1)]
                            i = mm3(pe, psS[:, k, :], w[0], w[1], x[0], x[1], kk == 0, kk == KD - 1)
                        i.then_inc(s_tt, 1)
                def gate_back():
                    for t in range(NT):
                        i = pe.transpose(psL[:, t * E:(t + 1) * E], LT[:, t * P:(t + 1) * P], c.ident[0:E, 0:E])
                    i.then_inc(s_lg, 1)

                if R.gate:
                    wait(pe, s_lte, 2 * (r - 1))
                    if not R.attn:
                        gate_back()
                if R.attn:
                    for k in range(4):
                        if k == 1 and R.gate:
                            gate_back()
                        wait(pe, s_tl, 4 * r + k + 1)
                        for t2 in range(2):
                            t = 2 * k + t2
                            for kk in range(KD):
                                w = [xnT[z][:, kk, t * P:(t + 1) * P] for z in (0, 1)]
                                i = mm3(pe, psS[:, k, t2 * D:(t2 + 1) * D], w[0], w[1],
                                        c.wv[0][:, kk, :], c.wv[1][:, kk, :], kk == 0, kk == KD - 1)
                        i.then_inc(s_v, 1)
                    for step in range(NT + 2):
                        i0, i1, i2 = step, step - 1, step - 2
                        if i0 < NT:
                            b = 2 * (i0 % 2)
                            if i0 < 2:
                                wait(pe, s_vl, 4 * r + 2 * i0 + 2)
                            else:
                                wait(pe, s_exp, 8 * r + i0 - 1)
                            for n in range(2):
                                for kk in range(KD):
                                    w = [tT[z][:, kk, i0 * P:(i0 + 1) * P] for z in (0, 1)]
                                    x = [xnT[z][:, kk, n * 512:(n + 1) * 512] for z in (0, 1)]
                                    i = mm3(pe, psS[:, b + n, :], w[0], w[1], x[0], x[1], kk == 0, kk == KD - 1)
                            i.then_inc(s_s, 1)
                        if 0 <= i1 < NT:
                            wait(pe, s_exp, 8 * r + i1 + 1)
                            wait(pe, s_ptl, 2 * (8 * r + i1))
                            for t in range(NT):
                                i = pe.transpose(psPT[:, t * P:(t + 1) * P], Pr[:, i1 % 2, t * P:(t + 1) * P], c.ident[:, :])
                                if t % 4 == 3:
                                    i.then_inc(s_t, 1)
                        if i2 >= 0:
                            wait(pe, s_ptl, 2 * (8 * r + i2 + 1))
                            wait(pe, s_ol, 8 * r + i2)
                            if i2 == 0:
                                wait(pe, s_vl, 4 * (r + 1))
                            for t in range(NT):
                                i = mm3(pe, psO[:, 0:D], PT[0][:, i2 % 2, t, :], PT[1][:, i2 % 2, t, :],
                                        V[0][:, t, :], V[1][:, t, :], t == 0, t == NT - 1)
                            i.then_inc(s_pv, 1)
            rounds(pe, body)

        @blk.scalar
        def _(a):
            def normalize(dst, src, n, h):
                for t in range(4 * h, 4 * h + 4):
                    i = a.activation(dst(t), src(t), ACT.Identity, bias=shift[n][:, t:t + 1], scale=rs[n][:, t:t + 1])
                return i

            def norm_x(b, h):
                wait(a, s_r1, b + 1)
                wait(a, s_tr, 4 * b)
                normalize(lambda t: xn[:, t, :], lambda t: X[:, b % XS, t, :], 0, h).then_inc(s_xn, 1)

            def norm_y(r, h):
                wait(a, s_ry, r)
                normalize(lambda t: Y[:, t, :], lambda t: Y[:, t, :], 1, h).then_inc(s_yn, 1)

            def norm_x1(r, h):
                wait(a, s_r2, r)
                wait(a, s_xnst, 16 * (r - 1))
                normalize(lambda t: XNB[:, t, 0:D], lambda t: X[:, (r - 1) % XS, t, :], 2, h).then_inc(s_xn2, 1)

            for h in range(2):
                norm_x(0, h)

            def body(R):
                r = R.r
                if R.attn:
                    for k in range(4):
                        dk, ht = k % 2, k // 2
                        wait(a, s_tr, 4 * r + k + 1)
                        a.activation(xnT[0][:, dk, ht * 512:(ht + 1) * 512].rearrange("d (p j) -> d j p", j=4),
                                     psS[:, k, :].rearrange("d (j p) -> d j p", j=4), ACT.Copy).then_inc(s_xh, 1)
                if R.gate:
                    wait(a, s_xtst, 16 * (r - 2))
                    wait(a, s_lt, 2 * (r - 2))
                    for k in range(4):
                        dk, ht = k % 2, k // 2
                        wait(a, s_tr2, 4 * (r - 2) + k + 1)
                        a.activation(xn2T[:, dk, ht * 512:(ht + 1) * 512], psS[:, k, :], ACT.Copy).then_inc(s_n2, 1)
                    wait(a, s_lg, r - 2)
                    for h, bank in enumerate((psL, psO)):
                        wait(a, s_lt, 2 * (r - 2) + h + 1)
                        a.activation(LT[:, h * 512:(h + 1) * 512], bank[0:E, :], ACT.Copy).then_inc(s_lte, 1)
                if R.attn:
                    for k in range(4):
                        m, h = k % 2, k // 2
                        wait(a, s_tt, 4 * r + k + 1)
                        a.activation(tT[0][:, m, h * 512:(h + 1) * 512], psS[:, k, :], ACT.Copy).then_inc(s_th, 1)
                    for k in range(4):
                        wait(a, s_v, 4 * r + k + 1)
                        a.activation(V[0][:, 2 * k:2 * k + 2, :], psS[:, k, :].rearrange("p (t c) -> p t c", t=2),
                                     ACT.Copy).then_inc(s_vh, 1)
                if R.gate:
                    wait(a, s_sm, r - 1)
                    a.activation(SM[:, :, :], SM[:, :, :], ACT.Exp).then_inc(s_sme, 1)
                if R.attn:
                    for step in range(NT + 2):
                        i0, i1, i2 = step, step - 1, step - 2
                        if i0 < NT:
                            wait(a, s_max, 8 * r + i0 + 1)
                            wait(a, s_t, 2 * (8 * r + i0 - 1))
                            b = 2 * (i0 % 2)
                            a.activation(Pr[:, i0 % 2, :], psS[:, b:b + 2, :].rearrange("p a c -> p (a c)"), ACT.Exp,
                                         bias=negmax[:, i0:i0 + 1], accum_out=rowsum[:, i0:i0 + 1]).then_inc(s_exp, 1)
                        if 0 <= i1 < NT:
                            wait(a, s_pv, 8 * r + i1 - 1)
                            for h in range(2):
                                wait(a, s_t, 2 * (8 * r + i1) + h + 1)
                                a.activation(PT[0][:, i1 % 2, 4 * h:4 * h + 4, :],
                                             psPT[:, h * 512:(h + 1) * 512].rearrange("p (t c) -> p t c", t=4),
                                             ACT.Copy).then_inc(s_pth, 1)
                        if i2 >= 0:
                            if i2 == 0:
                                wait(a, s_y, 4 * r)
                            wait(a, s_ri, 8 * r + i2 + 1)
                            wait(a, s_pv, 8 * r + i2 + 1)
                            a.activation(O[0][:, i2, :], psO[:, 0:D], ACT.Copy, scale=rinv[:, i2:i2 + 1]).then_inc(s_oh, 1)
                        if R.post and step in (3, 4):
                            norm_y(r, step - 3)
                        if R.ln_next and step in (6, 7):
                            norm_x(r + 1, step - 6)
                        if R.post and step in (8, 9):
                            norm_x1(r, step - 8)
                elif R.post:
                    for f in (norm_y, norm_x1):
                        for h in range(2):
                            f(r, h)
            rounds(a, body)

        def stats(v, src, n, part):
            if part < 2:
                for t in range(4 * part, 4 * part + 4):
                    i = v.bn_stats(st[n][:, t, :], src(t))
                return i
            if part == 2:
                v.drain()
                for t in range(NT):
                    v.bn_aggr(mv[n][:, t, :], st[n][:, t, :])
                v.drain()
            return layernorm_scale(v, part - 2, mv[n], ve[:, :], rs[n][:, :], shift[n][:, :], tmp[:, :], NT)

        @blk.vector
        def _(v):
            v.wait_ge(s_x, 16)
            for part in range(4):
                i = stats(v, lambda t: X[:, 0, t, :], 0, part)
            i.then_inc(s_r1, 1)

            def body(R):
                r = R.r
                if R.attn:
                    for k in range(4):
                        dk, ht = k % 2, k // 2
                        wait(v, s_xh, 4 * r + k + 1)
                        hi = xnT[0][:, dk, ht * 512:(ht + 1) * 512].rearrange("d (p j) -> d j p", j=4)
                        lo = xnT[1][:, dk, ht * 512:(ht + 1) * 512].rearrange("d (p j) -> d j p", j=4)
                        v.tensor_tensor(lo, psS[:, k, :].rearrange("d (j p) -> d j p", j=4), hi.bitcast(F32),
                                        ALU.subtract).then_inc(s_xl, 1)
                if R.post:
                    for k in range(4):
                        hm, jp = k // 2, k % 2
                        wait(v, s_y, 4 * (r - 1) + k + 1)
                        t = 4 * hm + 2 * jp
                        v.tensor_tensor(Y[:, t:t + 2, :], psS[:, k, :].rearrange("p (t c) -> p t c", t=2),
                                        c.bias[:, :].unsqueeze(1).to_broadcast([P, 2, D]), ALU.add).then_inc(s_yb, 1)
                if R.attn:
                    for k in range(4):
                        m, h = k % 2, k // 2
                        wait(v, s_th, 4 * r + k + 1)
                        v.tensor_tensor(tT[1][:, m, h * 512:(h + 1) * 512], psS[:, k, :],
                                        tT[0][:, m, h * 512:(h + 1) * 512].bitcast(F32), ALU.subtract).then_inc(s_tl, 1)
                    for k in range(4):
                        wait(v, s_vh, 4 * r + k + 1)
                        v.tensor_tensor(V[1][:, 2 * k:2 * k + 2, :], psS[:, k, :].rearrange("p (t c) -> p t c", t=2),
                                        V[0][:, 2 * k:2 * k + 2, :].bitcast(F32), ALU.subtract).then_inc(s_vl, 1)

                def gate_shift():
                    wait(v, s_lg, r - 1)
                    lg = psL[:, 0:NT * E].rearrange("p (t e) -> p t e", t=NT)
                    v.tensor_reduce(gmax[:, :], lg, AX.X, ALU.max)
                    v.drain()
                    v.tensor_tensor(SM[:, :, :], lg, gmax[:, :].unsqueeze(2).to_broadcast([P, NT, E]),
                                    ALU.subtract).then_inc(s_sm, 1)

                def gate_scores():
                    wait(v, s_sme, r - 1)
                    v.tensor_reduce(gsum[:, :], SM[:, :, :], AX.X, ALU.add)
                    v.drain()
                    v.reciprocal(gsum[:, :], gsum[:, :])
                    v.drain()
                    v.tensor_tensor(XNB[:, :, D:ROW], SM[:, :, :], gsum[:, :].unsqueeze(2).to_broadcast([P, NT, E]), ALU.mult)
                    v.drain()
                    v.tensor_copy(c.SC[:, :, bass.ds(2 * (r - 2), 2), :].rearrange("p j h e -> p h j e"),
                                  XNB[:, :, D:ROW].rearrange("p (h j) e -> p h j e", h=2)).then_inc(s_sc, 1)

                def ln_next(part):
                    if part == 0:
                        wait(v, s_x, 16 * (r + 2))
                    i = stats(v, lambda t: X[:, (r + 1) % XS, t, :], 0, part)
                    if part == 3:
                        i.then_inc(s_r1, 1)

                def ln_y(part):
                    if part == 0:
                        v.drain()
                    i = stats(v, lambda t: Y[:, t, :], 1, part)
                    if part == 3:
                        i.then_inc(s_ry, 1)

                def ln_x1(part):
                    if part < 2:
                        wait(v, s_x1, 2 * (r - 1) + part + 1)
                    i = stats(v, lambda t: X[:, (r - 1) % XS, t, :], 2, part)
                    if part == 3:
                        i.then_inc(s_r2, 1)

                tasks = {}
                if R.post:
                    tasks |= {(0, 1): (ln_y, 0), (1, 0): (ln_y, 1), (2, 0): (ln_y, 2), (2, 1): (ln_y, 3),
                              (6, 0): (ln_x1, 0), (6, 1): (ln_x1, 1), (7, 0): (ln_x1, 2), (7, 1): (ln_x1, 3)}
                if R.ln_next:
                    tasks |= {(3, 0): (ln_next, 0), (3, 1): (ln_next, 1), (4, 0): (ln_next, 2), (4, 1): (ln_next, 3)}

                def task(step, side):
                    if (step, side) in tasks:
                        f, part = tasks[step, side]
                        f(part)

                if R.gate:
                    gate_shift()
                for step in range(NT + 3 if R.attn else 0):
                    i0, i1, i3 = step, step - 1, step - 3
                    if i3 >= 0:
                        wait(v, s_oh, 8 * r + i3 + 1)
                        v.scalar_tensor_tensor(O[1][:, i3, :], psO[:, 0:D], rinv[:, i3:i3 + 1], O[0][:, i3, :].bitcast(F32),
                                               ALU.mult, ALU.subtract).then_inc(s_ol, 1)
                    if i0 < NT:
                        wait(v, s_s, 8 * r + i0 + 1)
                        b = 2 * (i0 % 2)
                        v.tensor_reduce(negmax[:, i0:i0 + 1], psS[:, b:b + 2, :].rearrange("p a c -> p (a c)"), AX.X, ALU.max,
                                        negate=True).then_inc(s_max, 1)
                    task(step, 0)
                    if 0 <= i1 < NT:
                        wait(v, s_exp, 8 * r + i1 + 1)
                        v.reciprocal(rinv[:, i1:i1 + 1], rowsum[:, i1:i1 + 1]).then_inc(s_ri, 1)
                        for h in range(2):
                            wait(v, s_pth, 2 * (8 * r + i1) + h + 1)
                            v.tensor_tensor(PT[1][:, i1 % 2, 4 * h:4 * h + 4, :],
                                            psPT[:, h * 512:(h + 1) * 512].rearrange("p (t c) -> p t c", t=4),
                                            PT[0][:, i1 % 2, 4 * h:4 * h + 4, :].bitcast(F32), ALU.subtract).then_inc(s_ptl, 1)
                    task(step, 1)
                    if step == 1 and R.gate:
                        gate_scores()
                if not R.attn:
                    if R.gate:
                        gate_scores()
                    if R.post:
                        for part in range(4):
                            ln_y(part)
                        for part in range(4):
                            ln_x1(part)
            rounds(v, body)

        @blk.gpsimd
        def _(g):
            def add_x(r):
                for h in range(2):
                    wait(g, s_yn, 2 * (r - 1) + h + 1)
                    x = X[:, (r - 1) % XS, 4 * h:4 * h + 4, :]
                    g.tensor_tensor(x, x, Y[:, 4 * h:4 * h + 4, :], ALU.add).then_inc(s_x1, 1)

            def body(R):
                r = R.r
                if R.post:
                    add_x(r)
            rounds(g, body)


def topk(nc, io, c):
    NG = NU * E
    C = 4 * NG
    SL = 32
    with ExitStack() as ctx:
        sb = lambda n, s, d=F32: ctx.enter_context(nc.sbuf_tensor(n, s, d))
        SCT = sb("SCT", [P, C])
        junk = sb("junk", [P, C], BF16)
        cnt, gsel = sb("cnt", [P, 1]), sb("gsel", [P, 1], I32)
        thr, bit, cand = sb("thr", [P, 1], I32), sb("bit", [P, 1], I32), sb("cand", [P, 1], I32)
        same = sb("same", [P, P])
        mcol, mrow = sb("mcol", [P, P], I32), sb("mrow", [P, 1], I32)
        mcolf, mrowf = sb("mcolf", [P, P]), sb("mrowf", [P, 1])
        ones, incl, strict, identb = (sb(n, [P, P], BF16) for n in ("ones", "incl", "strict", "identb"))
        MT = sb("MT", [P, 2, C], BF16)
        MK = sb("MK", [P, 4, 2, NG], BF16)
        tot = [sb(f"tot{n}", [P, 2, NU, E]) for n in range(2)]
        PRE = sb("PRE", [P, 2, NG])
        A = sb("A", [P, 4, NG])
        B = sb("B", [P, 4, NG])
        posi, part = sb("posi", [P, C], I32), sb("part", [P, C], I32)
        LO, HI = sb("LO", [P, GROUPS, C // GROUPS], BF16), sb("HI", [P, GROUPS, C // GROUPS], BF16)
        TV = sb("TV", [P, C // GROUPS], BF16)
        TVi = sb("TVi", [P, C // GROUPS], I32)
        pcol_i, pcol = sb("pcol_i", [P, 1], I32), sb("pcol", [P, 1])
        W = C // GROUPS
        VI = sb("VI", [P, SL, W], BF16)
        lo1, hi1 = sb("lo1", [P, SL, W], BF16), sb("hi1", [P, SL, W], BF16)
        val = sb("val", [P, 2, SL, W], BF16)
        vp, vt, vu, vj = (sb(n, [SL, GE * SL], I32) for n in ("vp", "vt", "vu", "vj"))
        LS = sb("LS", [SL, E, SL], I32)
        psT = ctx.enter_context(nc.psum_tensor("psT", [P, C], F32))
        psC = ctx.enter_context(nc.psum_tensor("psC", [P, 512], F32))
        psM = ctx.enter_context(nc.psum_tensor("psM", [P, 2, C], BF16))
        psR = ctx.enter_context(nc.psum_tensor("psR", [P, 2, 512], F32))
        psX = ctx.enter_context(nc.psum_tensor("psX", [P, GE, 2 * SL], F32))
        sem = lambda n: ctx.enter_context(nc.semaphore(n))
        s_const, s_sct, s_scv, s_cnt, s_sum = (sem(n) for n in ("s_const", "s_sct", "s_scv", "s_cnt", "s_sum"))
        s_mask, s_mt, s_mk, s_tot, s_rank, s_pos = (sem(n) for n in ("s_mask", "s_mt", "s_mk", "s_tot", "s_rank", "s_pos"))
        s_pl, s_lst, s_dec, s_out = (sem(n) for n in ("s_pl", "s_lst", "s_dec", "s_out"))
        blk = ctx.enter_context(nc.Block())
        BITS = 30

        @blk.gpsimd
        def _(g):
            g.iota(mcol[:, :], [[1, P]], base=0, channel_multiplier=0)
            g.iota(mrow[:, :], [[0, 1]], base=0, channel_multiplier=1)
            g.iota(pcol_i[:, :], [[0, 1]], base=0, channel_multiplier=1)
            g.iota(TVi[:, :], [[NU, 4], [1, NU], [0, GE]], base=0, channel_multiplier=0)
            g.memset(thr[:, :], 0)
            g.memset(bit[:, :], 1 << (BITS - 1))
            g.memset(ones[:, :], 1.0)
            for v in range(SL):
                g.memset(VI[:, v, :], float(v))
            g.drain().then_inc(s_const, 1)

        def decode(v, g):
            v.wait_ge(s_lst, g + 1)
            r3 = lambda t: t[:, :].rearrange("l (e h) -> l e h", e=GE)
            v.tensor_copy(r3(vp), psX[0:SL, :, 0:SL])
            v.tensor_copy(r3(vt), psX[0:SL, :, SL:2 * SL])
            v.drain().then_inc(s_dec, 1)
            v.tensor_scalar(vu[:, :], vt[:, :], NU - 1, None, ALU.bitwise_and)
            v.tensor_scalar(vj[:, :], vt[:, :], 4, None, ALU.logical_shift_right)
            v.drain()
            v.scalar_tensor_tensor(vj[:, :], vp[:, :], 4.0, vj[:, :], ALU.mult, ALU.add)
            v.drain()
            i = v.scalar_tensor_tensor(LS[:, GE * g:GE * (g + 1), :].rearrange("l e h -> l (e h)"), vu[:, :], 512.0, vj[:, :],
                                       ALU.mult, ALU.add)
            if g == GROUPS - 1:
                v.drain().then_inc(s_out, 1)

        @blk.vector
        def _(v):
            v.wait_ge(s_const, 1)
            v.tensor_copy(mcolf[:, :], mcol[:, :])
            v.tensor_copy(mrowf[:, :], mrow[:, :])
            v.tensor_copy(pcol[:, :], pcol_i[:, :])
            v.tensor_copy(TV[:, :], TVi[:, :])
            v.tensor_copy(identb[:, :], c.ident[:, :])
            v.tensor_copy(cand[:, :], bit[:, :])
            v.drain()
            v.tensor_scalar(incl[:, :], mcolf[:, :], mrowf[:, 0:1], None, ALU.is_ge)
            v.tensor_scalar(strict[:, :], mcolf[:, :], mrowf[:, 0:1], None, ALU.is_gt)
            v.tensor_scalar(mcol[:, :], mcol[:, :], E - 1, None, ALU.bitwise_and)
            v.tensor_scalar(mrow[:, :], mrow[:, :], E - 1, None, ALU.bitwise_and)
            v.drain()
            v.tensor_copy(mcolf[:, :], mcol[:, :])
            v.tensor_copy(mrowf[:, :], mrow[:, :])
            v.drain()
            v.tensor_scalar(same[:, :], mcolf[:, :], mrowf[:, 0:1], None, ALU.is_equal)
            v.wait_ge(s_sct, 1)
            v.tensor_copy(SCT[:, :], psT[:, :])
            v.drain()
            with v.Fori(0, BITS) as i:
                v.tensor_scalar(junk[:, :], SCT[:, :], cand[:, 0:1].bitcast(F32), 0.0, ALU.is_ge, ALU.add,
                                accum_out=cnt[:, 0:1]).then_inc(s_cnt, 1)
                v.wait_ge(s_sum, i + 1)
                v.tensor_scalar(gsel[:, :], psC[:, 0:1], float(CAP), None, ALU.is_ge)
                v.drain()
                v.tensor_tensor(gsel[:, :], gsel[:, :], bit[:, :], ALU.mult)
                v.drain()
                v.tensor_tensor(thr[:, :], thr[:, :], gsel[:, :], ALU.bitwise_or)
                v.tensor_scalar(bit[:, :], bit[:, :], 1, None, ALU.logical_shift_right)
                v.drain()
                v.tensor_tensor(cand[:, :], thr[:, :], bit[:, :], ALU.bitwise_or)
                v.drain()
            v.tensor_scalar(MT[:, 0, :], SCT[:, :], thr[:, 0:1].bitcast(F32), None, ALU.is_gt)
            v.tensor_scalar(MT[:, 1, :], SCT[:, :], thr[:, 0:1].bitcast(F32), None, ALU.is_equal).then_inc(s_mask, 1)
            v.wait_ge(s_mt, 1)
            for k in range(2):
                v.tensor_copy(MK[:, :, k, :].rearrange("p j (h q) -> p h j q", h=2),
                              psM[:, k, :].rearrange("p (h j q) -> p h j q", h=2, j=4))
            v.drain().then_inc(s_mk, 1)
            v.wait_ge(s_tot, 1)
            v.tensor_copy(tot[0][:, :, :, :].rearrange("p k u e -> p (k u e)"), psC[:, :])
            v.drain()
            cur, step = 0, 1
            while step < NU:
                a, b = tot[cur], tot[1 - cur]
                v.tensor_copy(b[:, :, 0:step, :], a[:, :, 0:step, :])
                v.tensor_tensor(b[:, :, step:NU, :], a[:, :, step:NU, :], a[:, :, 0:NU - step, :], ALU.add)
                v.drain()
                cur, step = 1 - cur, 2 * step
            inc = tot[cur]
            pre = PRE[:, :, :].rearrange("p k (u e) -> p k u e", e=E)
            v.memset(pre[:, :, 0:1, :], 0.0)
            v.tensor_copy(pre[:, :, 1:NU, :], inc[:, :, 0:NU - 1, :])
            v.drain()
            v.tensor_tensor(pre[:, 1, :, :], pre[:, 1, :, :], inc[:, 0, NU - 1:NU, :].to_broadcast([P, NU, E]), ALU.add)
            v.drain()
            for j in range(4):
                v.wait_ge(s_rank, j + 1)
                r = psR[:, j % 2, :].rearrange("p (k n) -> p k n", k=2)
                v.tensor_tensor(A[:, j, :], r[:, 0, :], PRE[:, 0, :], ALU.add)
                v.tensor_tensor(B[:, j, :], r[:, 1, :], PRE[:, 1, :], ALU.add)
                v.drain().then_inc(s_pos, 1)
            v.scalar_tensor_tensor(A[:, :, :], A[:, :, :], -4096.0, MK[:, :, 0, :], ALU.add, ALU.mult)
            v.scalar_tensor_tensor(B[:, :, :], B[:, :, :], -4096.0, MK[:, :, 1, :], ALU.add, ALU.mult)
            v.drain()
            v.tensor_tensor(A[:, :, :], A[:, :, :], B[:, :, :], ALU.add)
            v.drain()
            v.tensor_scalar(posi[:, :], A[:, :, :].rearrange("p j n -> p (j n)"), 4096.0, None, ALU.add)
            v.drain()
            for dst, op, n in ((HI, ALU.logical_shift_right, 5), (LO, ALU.bitwise_and, SL - 1)):
                v.tensor_scalar(part[:, :], posi[:, :], n, None, op)
                v.drain()
                v.tensor_copy(dst[:, :, :].rearrange("p g (t e) -> p g t e", e=GE),
                              part[:, :].rearrange("p (t g e) -> p g t e", g=GROUPS, e=GE))
                v.drain()
            for g in range(GROUPS):
                wide = lambda ap: ap.unsqueeze(1).to_broadcast([P, SL, W])
                if g:
                    v.wait_ge(s_lst, g)
                v.tensor_tensor(lo1[:, :, :], wide(LO[:, g, :]), VI[:, :, :], ALU.is_equal)
                v.tensor_tensor(hi1[:, :, :], wide(HI[:, g, :]), VI[:, :, :], ALU.is_equal)
                v.drain()
                v.tensor_scalar(val[:, 0, :, :], hi1[:, :, :], pcol[:, 0:1], None, ALU.mult)
                v.tensor_tensor(val[:, 1, :, :], hi1[:, :, :], wide(TV[:, :]), ALU.mult)
                v.drain().then_inc(s_pl, 1)
                if g:
                    decode(v, g - 1)
            decode(v, GROUPS - 1)

        @blk.tensor
        def _(pe):
            for h in range(2):
                for j in range(4):
                    i = pe.transpose(psT[:, (4 * h + j) * P:(4 * h + j + 1) * P],
                                     c.SC[:, j, 8 * h:8 * h + 8, :].rearrange("p u e -> p (u e)"), c.ident[:, :])
            i.then_inc(s_sct, 1)
            with pe.Fori(0, BITS) as i:
                pe.wait_ge(s_cnt, i + 1)
                pe.matmul(psC[:, 0:1], same[:, :], cnt[:, 0:1], start=True, stop=True).then_inc(s_sum, 1)
            pe.wait_ge(s_mask, 1)
            for k in range(2):
                for t in range(8):
                    i = pe.transpose(psM[:, k, t * P:(t + 1) * P], MT[:, k, t * P:(t + 1) * P], identb[:, :])
            i.then_inc(s_mt, 1)
            pe.wait_ge(s_mk, 1)
            mk = lambda j: MK[:, j, :, :].rearrange("p k n -> p (k n)")
            for j in range(4):
                i = pe.matmul(psC[:, :], ones[:, :], mk(j), start=(j == 0), stop=(j == 3))
            i.then_inc(s_tot, 1)
            for j in range(4):
                if j >= 2:
                    pe.wait_ge(s_pos, j - 1)
                for jj in range(4):
                    i = pe.matmul(psR[:, j % 2, :], (incl if jj < j else strict)[:, :], mk(jj), start=(jj == 0), stop=(jj == 3))
                i.then_inc(s_rank, 1)
            for g in range(GROUPS):
                pe.wait_ge(s_pl, g + 1)
                if g:
                    pe.wait_ge(s_dec, g)
                for e in range(GE):
                    for t in range(W // GE):
                        col = t * GE + e
                        i = pe.matmul(psX[0:SL, e, :], lo1[:, :, col], val[:, :, :, col].rearrange("p a v -> p (a v)"),
                                      start=(t == 0), stop=(t == W // GE - 1))
                i.then_inc(s_lst, 1)

        @blk.sync
        def _(sp):
            sp.wait_ge(s_out, 1)
            sp.dma_start(io["LIST"].rearrange("e (l h) -> l e h", l=SL), LS[:, :, :]).then_inc(s_out, 16)
            sp.wait_ge(s_out, 17)
            sp.dma_start(c.IDX[:, :, :], io["LIST"].rearrange("e (p c) -> p e c", p=P)).then_inc(s_out, 16)
            sp.wait_ge(s_out, 33)


def mlp(nc, io, c, shared):
    NI = (I_SH if shared else I_EXP) // P
    N = NB if shared else E
    W_N = 1 if shared else 2
    SLOTS = NI + 2
    with ExitStack() as ctx:
        tag = "sh_" if shared else "ex_"
        sb = lambda n, s, d=F32: ctx.enter_context(nc.sbuf_tensor(tag + n, s, d))
        pair = lambda n, s: (sb(n + "_hi", s, F32R), sb(n + "_lo", s, F32R))
        wg = [pair(f"wg{i}", [P, KD, NI * P]) for i in range(W_N)]
        wu = [pair(f"wu{i}", [P, KD, NI * P]) for i in range(W_N)]
        wd = pair("wd", [P, NI, D])
        raw = {n: sb("raw_" + n, [P, NI * D]) for n in "gud"}
        XT = [pair(f"XT{i}", [P, KD, 512]) for i in range(2)]
        GL, HF = sb("GL", [P, 2, 512]), sb("HF", [P, 2, 512])
        H = pair("H", [P, SLOTS, 512])
        OUT = sb("OUT", [P, 8, D])
        psG = ctx.enter_context(nc.psum_tensor(tag + "psG", [P, 2, 512], F32))
        psU = ctx.enter_context(nc.psum_tensor(tag + "psU", [P, 2, 512], F32))
        psX = ctx.enter_context(nc.psum_tensor(tag + "psXT", [P, 2, 512], F32))
        psD = ctx.enter_context(nc.psum_tensor(tag + "psD", [P, 2, 512], F32))
        sem = lambda n: ctx.enter_context(nc.semaphore(tag + n))
        s_up, s_gelu, s_mul, s_hhi, s_hlo = (sem(n) for n in ("s_up", "s_gelu", "s_mul", "s_hhi", "s_hlo"))
        s_dn, s_ev = sem("s_dn"), sem("s_ev")
        s_xt, s_xhi, s_xlo = sem("s_xt"), sem("s_xhi"), sem("s_xlo")
        s_raw = {n: sem("s_raw_" + n) for n in "gud"}
        s_whi = {n: sem("s_whi_" + n) for n in "gud"}
        s_wlo = {n: sem("s_wlo_" + n) for n in "gud"}
        EV0 = 2
        if shared:
            XR = sb("XR", [P, 2, KD, 512])
            s_xr = [sem("s_xr0"), sem("s_xr1")]
            s_st = [sem("s_st0"), sem("s_st1")]
        else:
            XG = [sb(f"XG{i}", [P, 8, ROW]) for i in range(2)]
            GI = [sb(f"GI{i}", [P, 8], I32) for i in range(2)]
            TW = [sb(f"TW{i}", [P, 8]) for i in range(2)]
            s_gi, s_tw = sem("s_gi"), sem("s_tw")
            s_ga = [sem("s_ga0"), sem("s_ga1")]
            s_sc = [sem("s_sc0"), sem("s_sc1")]
        blk = ctx.enter_context(nc.Block())

        def slot(tb, it):
            return it if tb == 0 or it >= 2 else NI + it

        def units(body):
            def run(eng):
                for q in range(2):
                    body(q, q, False)
                with eng.Fori(1, N // 2 - 1) as r:
                    for q in range(2):
                        body(2 * r + q, q, False)
                for q in range(2):
                    body(N - 2 + q, q, q == 1)
            return run

        def schedule(n, q, last, step, down):
            for tb in range(2):
                h = 2 * n + tb
                for it in range(2, NI):
                    step(n, h, q, tb, it)
                if not (last and tb):
                    n2, q2, tb2 = (n, q, 1) if tb == 0 else (n + 1, 1 - q, 0)
                    for it in range(2):
                        step(n2, h + 1, q2, tb2, it)
                down(n, h, q, tb)

        @blk.tensor
        def _(pe):
            def turn(n, h, q, tb, dk):
                if tb == 0 and dk == 0:
                    wait(pe, s_ga[q], 128 * (n // 2 + 1) if isinstance(n, int) else 64 * (n + 2 - q))
                wait(pe, s_xlo, 2 * h + dk - 1)
                for t in range(4):
                    i = pe.transpose(psX[:, dk, t * P:(t + 1) * P], XG[q][:, 4 * tb + t, dk * P:(dk + 1) * P], c.ident[:, :])
                i.then_inc(s_xt, 1)

            def step(n, h, q, tb, it):
                s = NI * h + it
                if tb == 0 and (not shared or isinstance(n, int)):
                    if it % 2 == 0:
                        u = 0 if shared else n
                        quarter = it * 4 // NI if shared else it // 2
                        for w in "gu":
                            wait(pe, s_wlo[w], 4 * u + quarter + 1)
                    elif shared:
                        for w in "gu":
                            wait(pe, s_wlo[w], it + 1)
                if it == 0:
                    wait(pe, s_xlo, 2 * (h + 1))
                wait(pe, s_mul, s - 1)
                cols = slice(it * P, (it + 1) * P)
                for ps, w in ((psG, wg), (psU, wu)):
                    w_hi, w_lo = w[q % W_N]
                    for k in range(KD):
                        i = mm3(pe, ps[:, it % 2, :], w_hi[:, k, cols], w_lo[:, k, cols],
                                XT[tb][0][:, k, :], XT[tb][1][:, k, :], k == 0, k == KD - 1)
                i.then_inc(s_up, 1)
                if not shared and it in (3, 4):
                    n2, q2, tb2 = (n, q, 1) if tb == 0 else (n + 1, 1 - q, 0)
                    if not (isinstance(n2, int) and n2 >= N):
                        turn(n2, h + 1, q2, tb2, it - 3)

            def down(n, h, q, tb):
                wait(pe, s_hlo, NI * (h + 1))
                if tb == 0 and (not shared or isinstance(n, int)):
                    wait(pe, s_wlo["d"], 4 if shared else 4 * (n + 1))
                for t in range(4):
                    wait(pe, s_ev, EV0 + 4 * h + t - 1)
                    for it in range(NI):
                        z = slot(tb, it)
                        i = mm3(pe, psD[:, t % 2, 0:D], H[0][:, z, t * P:(t + 1) * P], H[1][:, z, t * P:(t + 1) * P],
                                wd[0][:, it, :], wd[1][:, it, :], it == 0, it == NI - 1)
                    i.then_inc(s_dn, 1)

            if not shared:
                for dk in range(KD):
                    turn(0, 0, 0, 0, dk)
            if shared:
                for w in "gud":
                    wait(pe, s_wlo[w], 4)
            for it in range(2):
                step(0, 0, 0, 0, it)
            units(lambda n, q, last: schedule(n, q, last, step, down))(pe)

        def weight_part(w, q, quarter):
            if w == "d":
                a = NI // 4
                cut = lambda t: t[:, quarter * a:(quarter + 1) * a, :]
                return cut(raw[w][:, :].rearrange("p (i n) -> p i n", n=D)), cut(wd[0]), cut(wd[1])
            a = NI * P // 4
            cut = lambda t: t[:, :, quarter * a:(quarter + 1) * a]
            hi, lo = (wg if w == "g" else wu)[q % W_N]
            return cut(raw[w][:, :].rearrange("p (k n) -> p k n", k=KD)), cut(hi), cut(lo)

        def w_hi(a, w, n, q, quarter):
            src, hi, _ = weight_part(w, q, quarter)
            if quarter == 0:
                wait(a, s_raw[w], 16 * (n + 1))
                if w == "d":
                    wait(a, s_dn, 8 * n)
                else:
                    wait(a, s_up, 2 * NI * (n - 1) if isinstance(n, int) else NI * 2 * (n - 1))
            a.activation(hi, src, ACT.Copy).then_inc(s_whi[w], 1)

        def w_lo(v, w, n, q, quarter):
            src, hi, lo = weight_part(w, q, quarter)
            wait(v, s_whi[w], 4 * n + quarter + 1)
            v.tensor_tensor(lo, src, hi.bitcast(F32), ALU.subtract).then_inc(s_wlo[w], 1)

        def weight_task(n, tb, it, last):
            if shared:
                return None
            if tb == 0:
                return ("d", 0, it - 2) if 2 <= it < 6 else None
            if last:
                return None
            return ("g", 1, it) if it < 4 else ("u", 1, it - 4)

        def x_part(h, tb, dk):
            src = XR[:, tb, dk, :] if shared else psX[:, dk, :]
            return src, XT[tb][0][:, dk, :], XT[tb][1][:, dk, :]

        def x_hi(a, n, h, tb, dk):
            src, hi, _ = x_part(h, tb, dk)
            if dk == 0:
                wait(a, s_up, NI * (h - 1))
                if shared:
                    wait(a, s_xr[tb], 16 * (n + 1))
            if not shared:
                wait(a, s_xt, 2 * h + dk + 1)
            a.activation(hi, src, ACT.Copy).then_inc(s_xhi, 1)

        def x_lo(v, n, h, tb, dk):
            src, hi, lo = x_part(h, tb, dk)
            wait(v, s_xhi, 2 * h + dk + 1)
            v.tensor_tensor(lo, src, hi.bitcast(F32), ALU.subtract).then_inc(s_xlo, 1)

        XAT = (1, 2) if shared else (3, 4)

        def next_x(f, eng, n, h, tb, it):
            if it in XAT:
                n2, tb2 = (n, 1) if tb == 0 else (n + 1, 0)
                if not (isinstance(n2, int) and n2 >= N):
                    f(eng, n2, h + 1, tb2, it - XAT[0])
                    return n2, tb2

        @blk.scalar
        def _(a):
            a.sem_inc(s_ev, EV0)

            def part_hi(h, tb, it):
                wait(a, s_mul, NI * h + it + 1)
                if it == 2:
                    wait(a, s_dn, 4 * h)
                a.activation(H[0][:, slot(tb, it), :], HF[:, it % 2, :], ACT.Copy).then_inc(s_hhi, 1)

            def step(n, h, q, tb, it, last=False):
                s = NI * h + it
                wait(a, s_up, s + 1)
                wait(a, s_mul, s - 1)
                a.activation(GL[:, it % 2, :], psG[:, it % 2, :], ACT.Gelu).then_inc(s_gelu, 1)
                if it:
                    part_hi(h, tb, it - 1)
                elif not (isinstance(s, int) and s == 0):
                    part_hi(h - 1, 1 - tb, NI - 1)
                task = weight_task(n, tb, it, isinstance(n, int) and n == N - 1)
                if task:
                    w_hi(a, task[0], n + task[1], (q + task[1]) % 2, task[2])
                next_x(x_hi, a, n, h, tb, it)

            def down(n, h, q, tb):
                if isinstance(h, int) and h == 2 * N - 1:
                    part_hi(h, tb, NI - 1)
                for t in range(4):
                    z = 4 * tb + t
                    wait(a, s_dn, 4 * h + t + 1)
                    if t == 0:
                        if shared:
                            wait(a, s_st[tb], 16 * n)
                        elif tb == 0:
                            wait(a, s_tw, n + 1)
                            wait(a, s_sc[1 - q], 64 * (n - q) + 128 * q)
                    scale = 1.0 if shared else TW[q][:, z:z + 1]
                    a.activation(OUT[:, z, :], psD[:, t % 2, 0:D], ACT.Copy, scale=scale).then_inc(s_ev, 1)

            for w in "gud" if shared else "gu":
                for quarter in range(4):
                    w_hi(a, w, 0, 0, quarter)
            for dk in range(KD):
                x_hi(a, 0, 0, 0, dk)
            for it in range(2):
                step(0, 0, 0, 0, it)
            units(lambda n, q, last: schedule(n, q, last, step, down))(a)

        @blk.vector
        def _(v):
            def part_lo(h, tb, it):
                wait(v, s_hhi, NI * h + it + 1)
                v.tensor_tensor(H[1][:, slot(tb, it), :], HF[:, it % 2, :],
                                H[0][:, slot(tb, it), :].bitcast(F32), ALU.subtract).then_inc(s_hlo, 1)

            def scores_of(n, q):
                wait(v, s_ga[q], 128 * (n // 2 + 1) if isinstance(n, int) else 64 * (n + 2 - q))
                wait(v, s_ev, EV0 + 8 * (n - 1) if not (isinstance(n, int) and n < 2) else 0)
                v.tensor_copy(TW[q][:, :], XG[q][:, :, bass.ds(D + n, 1)].rearrange("p t o -> p (t o)")).then_inc(s_tw, 1)

            def step(n, h, q, tb, it):
                s = NI * h + it
                wait(v, s_gelu, s + 1)
                if not (isinstance(s, int) and s < 2):
                    wait(v, s_hlo, s - 1)
                v.tensor_tensor(HF[:, it % 2, :], psU[:, it % 2, :], GL[:, it % 2, :], ALU.mult).then_inc(s_mul, 1)
                if it:
                    part_lo(h, tb, it - 1)
                elif not (isinstance(s, int) and s == 0):
                    part_lo(h - 1, 1 - tb, NI - 1)
                task = weight_task(n, tb, it, isinstance(n, int) and n == N - 1)
                if task:
                    w_lo(v, task[0], n + task[1], (q + task[1]) % 2, task[2])
                got = next_x(x_lo, v, n, h, tb, it)
                if got and not shared and it == XAT[1] and got[1] == 0:
                    scores_of(got[0], 1 - q)

            def down(n, h, q, tb):
                if isinstance(h, int) and h == 2 * N - 1:
                    part_lo(h, tb, NI - 1)

            for w in "gud" if shared else "gu":
                for quarter in range(4):
                    w_lo(v, w, 0, 0, quarter)
            for dk in range(KD):
                x_lo(v, 0, 0, 0, dk)
            if not shared:
                scores_of(0, 0)
            for it in range(2):
                step(0, 0, 0, 0, it)
            units(lambda n, q, last: schedule(n, q, last, step, down))(v)

        if shared:
            @blk.sync
            def _(sp):
                for w, name in (("g", "sg"), ("u", "su"), ("d", "sd")):
                    sp.dma_start(raw[w][:, :], io[name].rearrange("p a n -> p (a n)")).then_inc(s_raw[w], 16)

                def load(n, tb):
                    wait(sp, s_xlo, 2 * (2 * n + tb - 1))
                    sp.dma_start(XR[:, tb, :, :], io["XN2T"][n][:, :, tb * 512:(tb + 1) * 512]).then_inc(s_xr[tb], 16)

                def store(n, tb):
                    wait(sp, s_ev, EV0 + 4 * (2 * n + tb + 1))
                    sp.dma_start(io["ACC"].rearrange("(n h p j) d -> n h p (j d)", n=NB, h=2, p=P)[n][tb],
                                 OUT[:, 4 * tb:4 * tb + 4, :].rearrange("p j d -> p (j d)")).then_inc(s_st[tb], 16)

                for tb in range(2):
                    load(0, tb)

                def body(n, q, last):
                    for tb in range(2):
                        if not last:
                            load(n + 1, tb)
                        store(n, tb)
                units(body)(sp)
                for tb in range(2):
                    sp.wait_ge(s_st[tb], 16 * N)
        else:
            @blk.sync
            def _(sp):
                def load(w, name, n):
                    wait(sp, s_wlo[w], 4 * n)
                    wait(sp, s_whi[w], 4 * n)
                    sp.dma_start(raw[w][:, :], io[name].rearrange("e p a n -> e p (a n)")[n]).then_inc(s_raw[w], 16)
                load("g", "wg", 0)
                load("u", "wu", 0)
                load("d", "wd", 0)

                def body(n, q, last):
                    if not last:
                        load("g", "wg", n + 1)
                        load("u", "wu", n + 1)
                        load("d", "wd", n + 1)
                units(body)(sp)

            s_pass = sem("s_pass")

            @blk.gpsimd
            def _(g):
                def pass_wait(s, value):
                    wait(g, s, value)
                    g.sem_inc(s_pass, 1)

                def gather(n, q):
                    wait(g, s_xt, 4 * (n - 1))
                    wait(g, s_tw, n - 1)
                    if not (isinstance(n, int) and n < 2):
                        wait(g, s_sc[q], 64 * (n - q))
                    g.tensor_copy(GI[q][:, :], c.IDX[:, bass.ds(n, 1), :].rearrange("p o c -> p (o c)")).then_inc(s_gi, 1)
                    pass_wait(s_gi, n + 1)
                    for t in range(8):
                        g.indirect_dma_start(out=XG[q][:, t, :], out_offset=None, in_=io["XN"],
                                             in_offset=bass.IndirectOffsetOnAxis(ap=GI[q][:, t:t + 1], axis=0)).then_inc(s_ga[q], 16)

                def scatter(n, q, tb):
                    for t in range(4 * tb, 4 * tb + 4):
                        if t == 0:
                            wait(g, s_sc[1 - q], 64 * (n - q) + 128 * q)
                        pass_wait(s_ev, EV0 + 8 * n + t + 1)
                        g.indirect_dma_start(out=io["ACC"], out_offset=bass.IndirectOffsetOnAxis(ap=GI[q][:, t:t + 1], axis=0),
                                             in_=OUT[:, t, :], in_offset=None, compute_op=ALU.add).then_inc(s_sc[q], 16)

                gather(0, 0)

                def body(n, q, last):
                    if not last:
                        gather(n + 1, 1 - q)
                    for tb in range(2):
                        scatter(n, q, tb)
                units(body)(g)
                for q in range(2):
                    g.wait_ge(s_sc[q], 64 * N)


def output(nc, io, c):
    with ExitStack() as ctx:
        sb = lambda n, s, d=F32: ctx.enter_context(nc.sbuf_tensor(n, s, d))
        NBUF = 4
        F = [sb(f"F{i}", [P, NT, D]) for i in range(NBUF)]
        X1 = [sb(f"X1_{i}", [P, NT, D]) for i in range(NBUF)]
        st, mv = [sb(f"fst{i}", [P, NT, 6]) for i in range(2)], [sb(f"fmv{i}", [P, NT, 2]) for i in range(2)]
        ve, tmp = sb("fve", [P, NT]), sb("ftmp", [P, NT])
        rs, shift = [sb(f"frs{i}", [P, NT]) for i in range(2)], [sb(f"fsh{i}", [P, NT]) for i in range(2)]
        sem = lambda n: ctx.enter_context(nc.semaphore(n))
        s_ld = [sem(f"s_ld{i}") for i in range(NBUF)]
        s_st = [sem(f"s_st{i}") for i in range(NBUF)]
        s_r, s_n, s_a = sem("s_r"), sem("s_n"), sem("s_a")
        blk = ctx.enter_context(nc.Block())
        flat = lambda t: t[:, :, :].rearrange("p (h j) d -> p h (j d)", h=2)

        @blk.sync
        def _(sp):
            def load(b):
                i = b % NBUF
                wait(sp, s_st[i], 16 * (b // NBUF))
                sp.dma_start(flat(F[i]), rows_of(io["ACC"], b)).then_inc(s_ld[i], 16)
                sp.dma_start(flat(X1[i]), rows_of(io["X1"], b)).then_inc(s_ld[i], 16)
            for b in range(NBUF):
                load(b)
            for b in range(NB):
                wait(sp, s_a, 2 * (b + 1))
                sp.dma_start(rows_of(io["out"], b), flat(F[b % NBUF])).then_inc(s_st[b % NBUF], 16)
                if b + NBUF < NB:
                    load(b + NBUF)
            for i in range(NBUF):
                sp.wait_ge(s_st[i], 16 * (NB // NBUF))

        def add(v, b):
            i = b % NBUF
            for h in range(2):
                wait(v, s_n, 2 * b + h + 1)
                f = F[i][:, 4 * h:4 * h + 4, :]
                v.tensor_tensor(f, f, X1[i][:, 4 * h:4 * h + 4, :], ALU.add).then_inc(s_a, 1)

        @blk.vector
        def _(v):
            for b in range(NB):
                i = b % NBUF
                v.wait_ge(s_ld[i], 32 * (b // NBUF + 1))
                wait(v, s_n, 2 * (b - 1))
                for t in range(NT):
                    v.bn_stats(st[b % 2][:, t, :], F[i][:, t, :])
                v.drain()
                for t in range(NT):
                    v.bn_aggr(mv[b % 2][:, t, :], st[b % 2][:, t, :])
                v.drain()
                for part in range(2):
                    last = layernorm_scale(v, part, mv[b % 2], ve[:, :], rs[b % 2][:, :], shift[b % 2][:, :], tmp[:, :], NT)
                last.then_inc(s_r, 1)
                if b:
                    add(v, b - 1)
            add(v, NB - 1)

        @blk.scalar
        def _(a):
            for b in range(NB):
                i = b % NBUF
                wait(a, s_r, b + 1)
                for h in range(2):
                    for t in range(4 * h, 4 * h + 4):
                        j = a.activation(F[i][:, t, :], F[i][:, t, :], ACT.Identity, bias=shift[b % 2][:, t:t + 1],
                                         scale=rs[b % 2][:, t:t + 1])
                    j.then_inc(s_n, 1)


class Consts:
    pass


def build(nc, io, phases="abcde", taps=None):
    with ExitStack() as ctx:
        c = Consts()
        sb = lambda n, s, d=F32: ctx.enter_context(nc.sbuf_tensor(n, s, d))
        c.ident = sb("ident", [P, P])
        c.SC = sb("SC", [P, 4, NU, E])
        c.IDX = sb("IDX", [P, E, CAP // P], I32)
        with ExitStack() as inner:
            sa = lambda n, s, d=F32: inner.enter_context(nc.sbuf_tensor(n, s, d))
            c.gw = sa("gw", [P, KD, E])
            c.bias = sa("bias", [P, D])
            c.wv, c.wp, c.m = ([sa(f"{n}{z}", [P, KD, D], F32R) for z in (0, 1)] for n in ("wv_", "wp_", "m_"))
            setup(nc, io, c)
            attention(nc, io, c)
        if "b" in phases:
            topk(nc, io, c)
        if "c" in phases:
            mlp(nc, io, c, shared=True)
        if "d" in phases:
            mlp(nc, io, c, shared=False)
        if "e" in phases:
            output(nc, io, c)


def layouts(i):
    a = {k: np.asarray(v) for k, v in i.items()}
    wqkv = a["L0_attn_w_qkv"]
    tiles = lambda w: np.ascontiguousarray(w.reshape(-1, P, w.shape[-1]).transpose(1, 0, 2))
    etiles = lambda w: np.ascontiguousarray(w.transpose(0, 2, 1).reshape(E, -1, P, w.shape[1]).transpose(0, 2, 1, 3))
    return {
        "x": np.ascontiguousarray(a["L0_attn_x"].reshape(T, D)),
        "wq": tiles(wqkv[0:D]), "wk": tiles(wqkv[D:2 * D]), "wv": tiles(wqkv[2 * D:].T), "wp": tiles(a["L0_attn_w_proj"].T),
        "bias": np.ascontiguousarray(a["L0_attn_b_proj"]),
        "gate": tiles(a["L0_ffn_gate_w"].T),
        "wg": etiles(a["L0_ffn_Wg"]), "wu": etiles(a["L0_ffn_Wu"]), "wd": etiles(a["L0_ffn_Wd"]),
        "sg": tiles(a["L0_ffn_Sg"].T), "su": tiles(a["L0_ffn_Su"].T), "sd": tiles(a["L0_ffn_Sd"].T),
    }


def kernel(**inputs):
    import concourse.bacc as bacc
    from concourse.bass_utils import run_bass_kernel_spmd as run

    arrays = {f"{n}_in": v for n, v in layouts(inputs).items()}
    nc = bacc.Bacc("TRN2", target_bir_lowering=False, num_devices=1)
    io = {n[:-3]: nc.dram_tensor(n, v.shape, mybir.dt.from_np(v.dtype), kind="ExternalInput").ap() for n, v in arrays.items()}
    io["out"] = nc.dram_tensor("out_dram", (T, D), F32, kind="ExternalOutput").ap()
    for n, shape, dt in (("XN", (T, ROW), F32), ("X1", (T, D), F32), ("XN2T", (NB, P, KD, S), F32), ("ACC", (T, D), F32),
                         ("LIST", (E, CAP), I32)):
        io[n] = nc.dram_tensor(n, shape, dt).ap()
    build(nc, io)
    r = run(nc, [arrays], core_ids=[0])
    return r.results[0]["out_dram"].reshape(NB, S, D)
```

```python
import numpy as np
from contextlib import ExitStack

import concourse.bass as bass
from concourse import mybir

F32 = mybir.dt.float32
F32R = mybir.dt.float32r
BF16 = mybir.dt.bfloat16
I32 = mybir.dt.int32
ALU = mybir.AluOpType
ACT = mybir.ActivationFunctionType
AX = mybir.AxisListType

NB, S, D = 8, 1024, 256
T = NB * S
P = 128
E = 16
CAP = 2 * T // E
I_EXP, I_SH = 4 * D, 2 * D
KD = D // P
NT = S // P
NU = T // 512
ROW = D + E
EPS = 1e-5
XS = 4
GROUPS, GE = 4, 4


def wait(eng, sem, value):
    if isinstance(value, int) and value <= 0:
        return
    eng.wait_ge(sem, value)


def mm3(pe, out, w_hi, w_lo, x_hi, x_lo, first, last):
    pe.matmul(out, w_hi, x_hi, start=first, stop=False)
    pe.matmul(out, w_hi, x_lo, start=False, stop=False)
    return pe.matmul(out, w_lo, x_hi, start=False, stop=last)


def layernorm_scale(v, part, mv, ve, y, shift, t, n):
    if part == 0:
        v.tensor_scalar(ve, mv[:, 0:n, 1], EPS, None, ALU.add)
        v.drain()
        v.tensor_scalar(y.bitcast(I32), ve.bitcast(I32), -0.5, 1597463007.0, ALU.mult, ALU.add)
        v.drain()
    for _ in range(1 + part):
        v.tensor_tensor(t, y, y, ALU.mult)
        v.drain()
        v.scalar_tensor_tensor(t, t, -0.5, ve, ALU.mult, ALU.mult)
        v.drain()
        last = v.scalar_tensor_tensor(y, t, 1.5, y, ALU.add, ALU.mult)
        v.drain()
    if part == 1:
        last = v.scalar_tensor_tensor(shift, mv[:, 0:n, 0], -1.0, y, ALU.mult, ALU.mult)
    return last


def rows_of(dram, b):
    return dram.rearrange("(b h p j) c -> b p h (j c)", b=NB, h=2, p=P)[b]


def setup(nc, io, c):
    with ExitStack() as ctx:
        sb = lambda n, s, d=F32: ctx.enter_context(nc.sbuf_tensor(n, s, d))
        raw = {n: sb("raw_" + n, [P, KD, D]) for n in ("wq", "wk", "wv", "wp")}
        mf = sb("mf", [P, KD, D])
        ps = ctx.enter_context(nc.psum_tensor("ps_m", [P, KD, 512], F32))
        sem = lambda n: ctx.enter_context(nc.semaphore(n))
        s_ld = {n: sem("s_ld_" + n) for n in raw}
        s_k, s_m, s_mf, s_c = sem("s_k"), sem("s_m"), sem("s_mf"), sem("s_c")
        blk = ctx.enter_context(nc.Block())

        @blk.sync
        def _(sp):
            for n in raw:
                sp.dma_start(raw[n][:, :, :], io[n]).then_inc(s_ld[n], 16)
            sp.dma_start(c.gw[:, :, :], io["gate"]).then_inc(s_c, 16)
            sp.dma_start(c.bias[:, :], io["bias"].partition_broadcast(P)).then_inc(s_c, 16)
            sp.wait_ge(s_c, 32)

        @blk.gpsimd
        def _(g):
            g.memset(c.ident[:, :], 0.0)
            g.drain()
            g.affine_select(out=c.ident[:, :], in_=c.ident[:, :], compare_op=ALU.not_equal, fill=1.0, base=0,
                            pattern=[[-1, P]], channel_multiplier=1)

        @blk.tensor
        def _(pe):
            pe.wait_ge(s_ld["wq"], 16)
            pe.wait_ge(s_ld["wk"], 16)
            for m in range(KD):
                for k in range(KD):
                    i = pe.matmul(ps[:, m, 0:D], raw["wq"][:, k, m * P:(m + 1) * P], raw["wk"][:, k, :],
                                  start=(k == 0), stop=(k == KD - 1))
            i.then_inc(s_m, 1)

        @blk.scalar
        def _(a):
            a.wait_ge(s_m, 1)
            a.activation(mf[:, :, :], ps[:, :, 0:D], ACT.Copy, scale=0.25).then_inc(s_mf, 1)

        @blk.vector
        def _(v):
            for n, dst in (("wv", c.wv), ("wp", c.wp), ("m", c.m)):
                if n == "m":
                    v.wait_ge(s_mf, 1)
                    src = mf
                else:
                    v.wait_ge(s_ld[n], 16)
                    src = raw[n]
                v.tensor_copy(dst[0][:, :, :], src[:, :, :])
                v.drain()
                v.tensor_tensor(dst[1][:, :, :], src[:, :, :], dst[0][:, :, :].bitcast(F32), ALU.subtract)


def attention(nc, io, c):
    with ExitStack() as ctx:
        sb = lambda n, s, d=F32: ctx.enter_context(nc.sbuf_tensor(n, s, d))
        pair = lambda n, s: (sb(n + "_hi", s, F32R), sb(n + "_lo", s, F32R))
        X = sb("X", [P, XS, NT, D])
        xn = sb("xn", [P, NT, D])
        xnT = pair("xnT", [P, KD, S])
        tT = pair("tT", [P, KD, S])
        V = pair("V", [P, NT, D])
        Pr = sb("Pr", [P, 2, S])
        PT = pair("PT", [P, 2, NT, P])
        O = pair("O", [P, NT, D])
        Y = sb("Y", [P, NT, D])
        XNB = sb("XNB", [P, NT, ROW])
        xn2T = sb("xn2T", [P, KD, S])
        LT = sb("LT", [E, S])
        negmax, rowsum, rinv = sb("negmax", [P, NT]), sb("rowsum", [P, NT]), sb("rinv", [P, NT])
        st = [sb(f"st{n}", [P, NT, 6]) for n in range(3)]
        mv = [sb(f"mv{n}", [P, NT, 2]) for n in range(3)]
        rs = [sb(f"rs{n}", [P, NT]) for n in range(3)]
        shift = [sb(f"shift{n}", [P, NT]) for n in range(3)]
        ve, tmp = sb("ve", [P, NT]), sb("tmp", [P, NT])
        gmax, gsum, SM = sb("gmax", [P, NT]), sb("gsum", [P, NT]), sb("SM", [P, NT, E])
        psS = ctx.enter_context(nc.psum_tensor("psS", [P, 4, 512], F32))
        psPT = ctx.enter_context(nc.psum_tensor("psPT", [P, S], F32))
        psO = ctx.enter_context(nc.psum_tensor("psO", [P, 512], F32))
        psL = ctx.enter_context(nc.psum_tensor("psL", [P, 512], F32))

        sem = lambda n: ctx.enter_context(nc.semaphore(n))
        s_x = sem("s_x")
        s_tr, s_xh, s_xl = sem("s_tr"), sem("s_xh"), sem("s_xl")
        s_tt, s_th, s_tl = sem("s_tt"), sem("s_th"), sem("s_tl")
        s_v, s_vh, s_vl = sem("s_v"), sem("s_vh"), sem("s_vl")
        s_y, s_yb = sem("s_y"), sem("s_yb")
        s_tr2, s_n2 = sem("s_tr2"), sem("s_n2")
        s_lt, s_lte, s_lg = sem("s_lt"), sem("s_lte"), sem("s_lg")
        s_s, s_max, s_exp, s_ri = sem("s_s"), sem("s_max"), sem("s_exp"), sem("s_ri")
        s_t, s_pth, s_ptl = sem("s_t"), sem("s_pth"), sem("s_ptl")
        s_pv, s_oh, s_ol = sem("s_pv"), sem("s_oh"), sem("s_ol")
        s_r1, s_xn, s_ry, s_yn, s_x1, s_r2, s_xn2 = (sem(n) for n in ("s_r1", "s_xn", "s_ry", "s_yn", "s_x1", "s_r2", "s_xn2"))
        s_sm, s_sme, s_sc = sem("s_sm"), sem("s_sme"), sem("s_sc")
        s_x1st, s_xnst, s_xtst = sem("s_x1st"), sem("s_xnst"), sem("s_xtst")
        blk = ctx.enter_context(nc.Block())

        def output_bank(i):
            return (psO, psL)[i % 2][:, 0:D]

        class Round:
            def __init__(self, r, attn=True, post=True, gate=True, ln_next=True):
                self.r, self.attn, self.post, self.gate, self.ln_next = r, attn, post, gate, ln_next

        def rounds(eng, body):
            body(Round(0, post=False, gate=False))
            body(Round(1, gate=False))
            body(Round(2))
            with eng.Fori(3, NB - 1) as r:
                body(Round(r))
            body(Round(NB - 1, ln_next=False))
            body(Round(NB, attn=False, ln_next=False))
            body(Round(NB + 1, attn=False, post=False, ln_next=False))

        @blk.sync
        def _(sp):
            def slot(b):
                return X[:, b % XS, :, :].rearrange("p (h j) c -> p h (j c)", h=2)

            sp.dma_start(slot(0), rows_of(io["x"], 0)).then_inc(s_x, 16)

            def body(R):
                r = R.r
                if R.ln_next:
                    wait(sp, s_x, 16 * (r + 1))
                    wait(sp, s_x1st, 16 * (r + 2 - XS))
                    sp.dma_start(slot(r + 1), rows_of(io["x"], r + 1)).then_inc(s_x, 16)
                if R.gate:
                    wait(sp, s_n2, 4 * (r - 1))
                    sp.dma_start(io["XN2T"][r - 2], xn2T[:, :, :]).then_inc(s_xtst, 16)
                    wait(sp, s_sc, r - 1)
                    sp.dma_start(rows_of(io["XN"], r - 2),
                                 XNB[:, :, :].rearrange("p (h j) c -> p h (j c)", h=2)).then_inc(s_xnst, 16)
                if R.post:
                    wait(sp, s_x1, 2 * r)
                    sp.dma_start(rows_of(io["X1"], r - 1),
                                 slot(r - 1)).then_inc(s_x1st, 16)
            rounds(sp, body)
            sp.wait_ge(s_x1st, 16 * NB)
            sp.wait_ge(s_xnst, 16 * NB)
            sp.wait_ge(s_xtst, 16 * NB)

        @blk.tensor
        def _(pe):
            def turn_x(b, ks):
                wait(pe, s_xn, 2 * (b + 1))
                for k in ks:
                    dk, ht = k % 2, k // 2
                    for j in range(4):
                        i = pe.transpose(psS[:, k, j * P:(j + 1) * P], xn[:, 4 * ht + j, dk * P:(dk + 1) * P], c.ident[:, :])
                    i.then_inc(s_tr, 1)

            turn_x(0, range(4))

            def body(R):
                r = R.r
                if R.gate:
                    wait(pe, s_xn2, 2 * (r - 1))
                    for k in range(4):
                        dk, ht = k % 2, k // 2
                        if R.attn:
                            wait(pe, s_xl, 4 * r + k + 1)
                        for j in range(4):
                            i = pe.transpose(psS[:, k, j * P:(j + 1) * P], XNB[:, 4 * ht + j, dk * P:(dk + 1) * P], c.ident[:, :])
                        i.then_inc(s_tr2, 1)
                if R.post:
                    wait(pe, s_ol, 8 * r)
                    for k in range(4):
                        hm, jp = k // 2, k % 2
                        if R.gate:
                            wait(pe, s_n2, 4 * (r - 2) + k + 1)
                        elif R.attn:
                            wait(pe, s_xl, 4 * r + k + 1)
                        for jj in range(2):
                            for q in range(2):
                                ot = 2 * (2 * jp + jj) + q
                                i = mm3(pe, psS[:, k, jj * D:(jj + 1) * D],
                                        O[0][:, ot, hm * P:(hm + 1) * P], O[1][:, ot, hm * P:(hm + 1) * P],
                                        c.wp[0][:, q, :], c.wp[1][:, q, :], q == 0, q == 1)
                        i.then_inc(s_y, 1)
                if R.gate:
                    wait(pe, s_n2, 4 * (r - 1))
                    wait(pe, s_sm, r - 2)
                    wait(pe, s_ol, 8 * r if R.attn else 8 * NB)
                    for h, bank in enumerate((psL, psO)):
                        for k in range(KD):
                            i = pe.matmul(bank[0:E, :], c.gw[:, k, :], xn2T[:, k, h * 512:(h + 1) * 512],
                                          start=(k == 0), stop=(k == KD - 1))
                        i.then_inc(s_lt, 1)
                if R.attn:
                    wait(pe, s_xl, 4 * (r + 1))
                    if R.post:
                        wait(pe, s_yb, 4 * r)
                    for k in range(4):
                        m, h = k % 2, k // 2
                        for kk in range(KD):
                            w = [c.m[z][:, kk, m * P:(m + 1) * P] for z in (0, 1)]
                            x = [xnT[z][:, kk, h * 512:(h + 1) * 512] for z in (0, 1)]
                            i = mm3(pe, psS[:, k, :], w[0], w[1], x[0], x[1], kk == 0, kk == KD - 1)
                        i.then_inc(s_tt, 1)
                def gate_back():
                    for t in range(NT):
                        i = pe.transpose(psL[:, t * E:(t + 1) * E], LT[:, t * P:(t + 1) * P], c.ident[0:E, 0:E])
                    i.then_inc(s_lg, 1)

                if R.gate:
                    wait(pe, s_lte, 2 * (r - 1))
                    if not R.attn:
                        gate_back()
                if R.attn:
                    for k in range(4):
                        if k == 1 and R.gate:
                            gate_back()
                        wait(pe, s_tl, 4 * r + k + 1)
                        for t2 in range(2):
                            t = 2 * k + t2
                            for kk in range(KD):
                                w = [xnT[z][:, kk, t * P:(t + 1) * P] for z in (0, 1)]
                                i = mm3(pe, psS[:, k, t2 * D:(t2 + 1) * D], w[0], w[1],
                                        c.wv[0][:, kk, :], c.wv[1][:, kk, :], kk == 0, kk == KD - 1)
                        i.then_inc(s_v, 1)
                    for step in range(NT + 2):
                        i0, i1, i2 = step, step - 1, step - 2
                        if i0 < NT:
                            b = 2 * (i0 % 2)
                            if i0 < 2:
                                wait(pe, s_vl, 4 * r + 2 * i0 + 2)
                            else:
                                wait(pe, s_exp, 8 * r + i0 - 1)
                            for n in range(2):
                                for kk in range(KD):
                                    w = [tT[z][:, kk, i0 * P:(i0 + 1) * P] for z in (0, 1)]
                                    x = [xnT[z][:, kk, n * 512:(n + 1) * 512] for z in (0, 1)]
                                    i = mm3(pe, psS[:, b + n, :], w[0], w[1], x[0], x[1], kk == 0, kk == KD - 1)
                            i.then_inc(s_s, 1)
                        if R.ln_next and i0 >= NT:
                            if i0 == NT:
                                wait(pe, s_exp, 8 * r + 7)
                                turn_x(r + 1, (0, 1))
                            else:
                                wait(pe, s_exp, 8 * r + 8)
                                turn_x(r + 1, (2, 3))
                        def turn_p():
                            wait(pe, s_exp, 8 * r + i1 + 1)
                            wait(pe, s_ptl, 2 * (8 * r + i1))
                            for t in range(NT):
                                i = pe.transpose(psPT[:, t * P:(t + 1) * P], Pr[:, i1 % 2, t * P:(t + 1) * P], c.ident[:, :])
                                if t % 4 == 3:
                                    i.then_inc(s_t, 1)

                        def output(ts):
                            if ts[0] == 0:
                                wait(pe, s_ptl, 2 * (8 * r + i2 + 1))
                                wait(pe, s_ol, 8 * r + i2 - 1)
                                if i2 == 1 and R.gate:
                                    wait(pe, s_sm, r - 1)
                                if i2 == 0:
                                    wait(pe, s_vl, 4 * (r + 1))
                            for t in ts:
                                i = mm3(pe, output_bank(i2), PT[0][:, i2 % 2, t, :], PT[1][:, i2 % 2, t, :],
                                        V[0][:, t, :], V[1][:, t, :], t == 0, t == NT - 1)
                            if ts[-1] == NT - 1:
                                i.then_inc(s_pv, 1)

                        if i0 == NT:
                            output(range(NT // 2))
                            turn_p()
                            output(range(NT // 2, NT))
                        else:
                            if 0 <= i1 < NT:
                                turn_p()
                            if i2 >= 0:
                                output(range(NT))
            rounds(pe, body)

        @blk.scalar
        def _(a):
            def normalize(dst, src, n, h):
                for t in range(4 * h, 4 * h + 4):
                    i = a.activation(dst(t), src(t), ACT.Identity, bias=shift[n][:, t:t + 1], scale=rs[n][:, t:t + 1])
                return i

            def norm_x(b, h):
                wait(a, s_r1, b + 1)
                wait(a, s_tr, 4 * b)
                normalize(lambda t: xn[:, t, :], lambda t: X[:, b % XS, t, :], 0, h).then_inc(s_xn, 1)

            def norm_y(r, h):
                wait(a, s_ry, r)
                normalize(lambda t: Y[:, t, :], lambda t: Y[:, t, :], 1, h).then_inc(s_yn, 1)

            def norm_x1(r, h):
                wait(a, s_r2, r)
                wait(a, s_xnst, 16 * (r - 1))
                normalize(lambda t: XNB[:, t, 0:D], lambda t: X[:, (r - 1) % XS, t, :], 2, h).then_inc(s_xn2, 1)

            def turned_hi(b, ks):
                for k in ks:
                    dk, ht = k % 2, k // 2
                    wait(a, s_tr, 4 * b + k + 1)
                    a.activation(xnT[0][:, dk, ht * 512:(ht + 1) * 512].rearrange("d (p j) -> d j p", j=4),
                                 psS[:, k, :].rearrange("d (j p) -> d j p", j=4), ACT.Copy).then_inc(s_xh, 1)

            for h in range(2):
                norm_x(0, h)
            turned_hi(0, range(4))

            def body(R):
                r = R.r
                if R.gate:
                    wait(a, s_xtst, 16 * (r - 2))
                    wait(a, s_lt, 2 * (r - 2))
                    for k in range(4):
                        dk, ht = k % 2, k // 2
                        wait(a, s_tr2, 4 * (r - 2) + k + 1)
                        a.activation(xn2T[:, dk, ht * 512:(ht + 1) * 512], psS[:, k, :], ACT.Copy).then_inc(s_n2, 1)
                    wait(a, s_lg, r - 2)
                    for h, bank in enumerate((psL, psO)):
                        wait(a, s_lt, 2 * (r - 2) + h + 1)
                        a.activation(LT[:, h * 512:(h + 1) * 512], bank[0:E, :], ACT.Copy).then_inc(s_lte, 1)
                if R.attn:
                    for k in range(4):
                        m, h = k % 2, k // 2
                        wait(a, s_tt, 4 * r + k + 1)
                        a.activation(tT[0][:, m, h * 512:(h + 1) * 512], psS[:, k, :], ACT.Copy).then_inc(s_th, 1)
                    for k in range(4):
                        wait(a, s_v, 4 * r + k + 1)
                        a.activation(V[0][:, 2 * k:2 * k + 2, :], psS[:, k, :].rearrange("p (t c) -> p t c", t=2),
                                     ACT.Copy).then_inc(s_vh, 1)
                if R.gate:
                    wait(a, s_sm, r - 1)
                    a.activation(SM[:, :, :], SM[:, :, :], ACT.Exp).then_inc(s_sme, 1)
                if R.attn:
                    for step in range(NT + 2):
                        i0, i1, i2 = step, step - 1, step - 2
                        if R.ln_next and step >= NT:
                            turned_hi(r + 1, (0, 1) if step == NT else (2, 3))
                        if 0 <= i1 < NT:
                            wait(a, s_pv, 8 * r + i1 - 1)
                            for h in range(2):
                                wait(a, s_t, 2 * (8 * r + i1) + h + 1)
                                a.activation(PT[0][:, i1 % 2, 4 * h:4 * h + 4, :],
                                             psPT[:, h * 512:(h + 1) * 512].rearrange("p (t c) -> p t c", t=4),
                                             ACT.Copy).then_inc(s_pth, 1)
                        if i0 < NT:
                            wait(a, s_max, 8 * r + i0 + 1)
                            wait(a, s_t, 2 * (8 * r + i0 - 1))
                            b = 2 * (i0 % 2)
                            a.activation(Pr[:, i0 % 2, :], psS[:, b:b + 2, :].rearrange("p a c -> p (a c)"), ACT.Exp,
                                         bias=negmax[:, i0:i0 + 1], accum_out=rowsum[:, i0:i0 + 1]).then_inc(s_exp, 1)
                        if i2 >= 0:
                            if i2 == 0:
                                wait(a, s_y, 4 * r)
                            wait(a, s_ri, 8 * r + i2 + 1)
                            wait(a, s_pv, 8 * r + i2 + 1)
                            a.activation(O[0][:, i2, :], output_bank(i2), ACT.Copy, scale=rinv[:, i2:i2 + 1]).then_inc(s_oh, 1)
                        if R.post and step in (3, 4):
                            norm_y(r, step - 3)
                        if R.ln_next and step in (5, 6):
                            norm_x(r + 1, step - 5)
                        if R.post and step in (7, 8):
                            norm_x1(r, step - 7)
                elif R.post:
                    for f in (norm_y, norm_x1):
                        for h in range(2):
                            f(r, h)
            rounds(a, body)

        def stats(v, src, n, part):
            if part < 2:
                for t in range(4 * part, 4 * part + 4):
                    i = v.bn_stats(st[n][:, t, :], src(t))
                return i
            if part == 2:
                v.drain()
                for t in range(NT):
                    v.bn_aggr(mv[n][:, t, :], st[n][:, t, :])
                v.drain()
            return layernorm_scale(v, part - 2, mv[n], ve[:, :], rs[n][:, :], shift[n][:, :], tmp[:, :], NT)

        @blk.vector
        def _(v):
            v.wait_ge(s_x, 16)
            for part in range(4):
                i = stats(v, lambda t: X[:, 0, t, :], 0, part)
            i.then_inc(s_r1, 1)

            def turned_lo(b, ks):
                for k in ks:
                    dk, ht = k % 2, k // 2
                    wait(v, s_xh, 4 * b + k + 1)
                    hi = xnT[0][:, dk, ht * 512:(ht + 1) * 512].rearrange("d (p j) -> d j p", j=4)
                    lo = xnT[1][:, dk, ht * 512:(ht + 1) * 512].rearrange("d (p j) -> d j p", j=4)
                    v.tensor_tensor(lo, psS[:, k, :].rearrange("d (j p) -> d j p", j=4), hi.bitcast(F32),
                                    ALU.subtract).then_inc(s_xl, 1)

            turned_lo(0, range(4))

            def body(R):
                r = R.r
                if R.post:
                    for k in range(4):
                        hm, jp = k // 2, k % 2
                        wait(v, s_y, 4 * (r - 1) + k + 1)
                        t = 4 * hm + 2 * jp
                        v.tensor_tensor(Y[:, t:t + 2, :], psS[:, k, :].rearrange("p (t c) -> p t c", t=2),
                                        c.bias[:, :].unsqueeze(1).to_broadcast([P, 2, D]), ALU.add).then_inc(s_yb, 1)
                if R.attn:
                    for k in range(4):
                        m, h = k % 2, k // 2
                        wait(v, s_th, 4 * r + k + 1)
                        v.tensor_tensor(tT[1][:, m, h * 512:(h + 1) * 512], psS[:, k, :],
                                        tT[0][:, m, h * 512:(h + 1) * 512].bitcast(F32), ALU.subtract).then_inc(s_tl, 1)
                    for k in range(4):
                        wait(v, s_vh, 4 * r + k + 1)
                        v.tensor_tensor(V[1][:, 2 * k:2 * k + 2, :], psS[:, k, :].rearrange("p (t c) -> p t c", t=2),
                                        V[0][:, 2 * k:2 * k + 2, :].bitcast(F32), ALU.subtract).then_inc(s_vl, 1)

                def gate_shift():
                    wait(v, s_lg, r - 1)
                    lg = psL[:, 0:NT * E].rearrange("p (t e) -> p t e", t=NT)
                    v.tensor_reduce(gmax[:, :], lg, AX.X, ALU.max)
                    v.drain()
                    v.tensor_tensor(SM[:, :, :], lg, gmax[:, :].unsqueeze(2).to_broadcast([P, NT, E]),
                                    ALU.subtract).then_inc(s_sm, 1)

                def gate_scores():
                    wait(v, s_sme, r - 1)
                    v.tensor_reduce(gsum[:, :], SM[:, :, :], AX.X, ALU.add)
                    v.drain()
                    v.reciprocal(gsum[:, :], gsum[:, :])
                    v.drain()
                    v.tensor_tensor(XNB[:, :, D:ROW], SM[:, :, :], gsum[:, :].unsqueeze(2).to_broadcast([P, NT, E]), ALU.mult)
                    v.drain()
                    v.tensor_copy(c.SC[:, :, bass.ds(2 * (r - 2), 2), :].rearrange("p j h e -> p h j e"),
                                  XNB[:, :, D:ROW].rearrange("p (h j) e -> p h j e", h=2)).then_inc(s_sc, 1)

                def ln_next(part):
                    if part == 0:
                        wait(v, s_x, 16 * (r + 2))
                    i = stats(v, lambda t: X[:, (r + 1) % XS, t, :], 0, part)
                    if part == 3:
                        i.then_inc(s_r1, 1)

                def ln_y(part):
                    if part == 0:
                        v.drain()
                    i = stats(v, lambda t: Y[:, t, :], 1, part)
                    if part == 3:
                        i.then_inc(s_ry, 1)

                def ln_x1(part):
                    if part < 2:
                        wait(v, s_x1, 2 * (r - 1) + part + 1)
                    i = stats(v, lambda t: X[:, (r - 1) % XS, t, :], 2, part)
                    if part == 3:
                        i.then_inc(s_r2, 1)

                tasks = {}
                if R.post:
                    tasks |= {(0, 1): (ln_y, 0), (1, 0): (ln_y, 1), (2, 0): (ln_y, 2), (2, 1): (ln_y, 3),
                              (5, 0): (ln_x1, 0), (5, 1): (ln_x1, 1), (6, 0): (ln_x1, 2), (6, 1): (ln_x1, 3)}
                if R.ln_next:
                    tasks |= {(3, 0): (ln_next, 0), (3, 1): (ln_next, 1), (4, 0): (ln_next, 2), (4, 1): (ln_next, 3)}

                def task(step, side):
                    if (step, side) in tasks:
                        f, part = tasks[step, side]
                        f(part)

                if R.gate:
                    gate_shift()
                for step in range(NT + 3 if R.attn else 0):
                    i0, i1, i3 = step, step - 1, step - 3
                    if i0 < NT:
                        wait(v, s_s, 8 * r + i0 + 1)
                        b = 2 * (i0 % 2)
                        v.tensor_reduce(negmax[:, i0:i0 + 1], psS[:, b:b + 2, :].rearrange("p a c -> p (a c)"), AX.X, ALU.max,
                                        negate=True).then_inc(s_max, 1)
                    if i3 >= 0:
                        wait(v, s_oh, 8 * r + i3 + 1)
                        v.scalar_tensor_tensor(O[1][:, i3, :], output_bank(i3), rinv[:, i3:i3 + 1], O[0][:, i3, :].bitcast(F32),
                                               ALU.mult, ALU.subtract).then_inc(s_ol, 1)
                    if R.ln_next and NT <= step < NT + 2:
                        turned_lo(r + 1, (0, 1) if step == NT else (2, 3))
                    if 0 <= i1 < NT:
                        wait(v, s_exp, 8 * r + i1 + 1)
                        v.reciprocal(rinv[:, i1:i1 + 1], rowsum[:, i1:i1 + 1]).then_inc(s_ri, 1)
                        for h in range(2):
                            wait(v, s_pth, 2 * (8 * r + i1) + h + 1)
                            v.tensor_tensor(PT[1][:, i1 % 2, 4 * h:4 * h + 4, :],
                                            psPT[:, h * 512:(h + 1) * 512].rearrange("p (t c) -> p t c", t=4),
                                            PT[0][:, i1 % 2, 4 * h:4 * h + 4, :].bitcast(F32), ALU.subtract).then_inc(s_ptl, 1)
                    task(step, 0)
                    task(step, 1)
                    if step == 1 and R.gate:
                        gate_scores()
                if not R.attn:
                    if R.gate:
                        gate_scores()
                    if R.post:
                        for part in range(4):
                            ln_y(part)
                        for part in range(4):
                            ln_x1(part)
            rounds(v, body)

        @blk.gpsimd
        def _(g):
            def add_x(r):
                for h in range(2):
                    wait(g, s_yn, 2 * (r - 1) + h + 1)
                    x = X[:, (r - 1) % XS, 4 * h:4 * h + 4, :]
                    g.tensor_tensor(x, x, Y[:, 4 * h:4 * h + 4, :], ALU.add).then_inc(s_x1, 1)

            def body(R):
                r = R.r
                if R.post:
                    add_x(r)
            rounds(g, body)


SL = 32
NG = NU * E
SC_N = 4 * NG
CW = SC_N // GROUPS // 2
NBIT = 30


class TopK:
    FIRST_COUNT = 3
    MASKS = FIRST_COUNT + 31
    CHUNKS = MASKS + 8

    def __init__(self, nc, io, c, sb, sem, ps):
        self.io, self.c, self.ps = io, c, ps
        self.SCT = sb("SCT", [P, SC_N])
        self.junk = sb("junk", [P, SC_N], BF16)
        self.cnt = sb("cnt", [P, 1])
        self.off, self.cand, self.BT = sb("off", [P, 1], I32), sb("cand", [P, 1], I32), sb("BT", [P, NBIT + 4], I32)
        self.same = sb("same", [P, P])
        self.mcol, self.mrow = sb("mcol", [P, P], I32), sb("mrow", [P, 1], I32)
        self.mcolf, self.mrowf = sb("mcolf", [P, P]), sb("mrowf", [P, 1])
        self.ones, self.incl, self.strict, self.identb = (sb(n, [P, P], BF16) for n in ("ones", "incl", "strict", "identb"))
        self.MT = sb("MT", [P, 2, SC_N], BF16)
        self.MK = sb("MK", [P, 4, 2, NG], BF16)
        self.RK = sb("RK", [P, 4, 2, NG])
        self.tot = [sb(f"tot{n}", [P, 2, NU, E]) for n in range(2)]
        self.PRE = sb("PRE", [P, 2, NG])
        self.digit = sb("digit", [P, SC_N], I32)
        self.LO, self.HI = (sb(n, [P, GROUPS, SC_N // GROUPS], BF16) for n in ("LO", "HI"))
        self.TV, self.TVi = sb("TV", [P, SC_N // GROUPS], BF16), sb("TVi", [P, SC_N // GROUPS], I32)
        self.pcol_i, self.pcol = sb("pcol_i", [P, 1], I32), sb("pcol", [P, 1])
        self.VI = sb("VI", [P, SL, CW], BF16)
        self.lo1 = sb("lo1", [P, 2, CW // GE, SL, GE], BF16)
        self.hi1 = sb("hi1", [P, SL, CW], BF16)
        self.val = sb("val", [P, 2, 2, SL, CW], BF16)
        self.vi, self.vu, self.vj = (sb(n, [P, 2, GE * SL], I32) for n in ("vi", "vu", "vj"))
        self.LS = sb("LS", [P, GROUPS, GE, SL], I32)
        self.s_const, self.s_sct, self.s_scv = sem("s_const"), sem("s_sct"), sem("s_scv")
        self.s_cnt, self.s_sum = sem("s_cnt"), sem("s_sum")
        self.s_mask, self.s_mt, self.s_mk = sem("s_mask"), sem("s_mt"), sem("s_mk")
        self.s_tot, self.s_totc, self.s_rank, self.s_rkc = sem("s_tot"), sem("s_totc"), sem("s_rank"), sem("s_rkc")
        self.s_dig, self.s_digc = sem("s_dig"), sem("s_digc")
        self.s_lo1, self.s_hi1 = sem("s_lo1"), sem("s_hi1")
        self.s_val, self.s_val_pool = sem("s_val"), sem("s_val_pool")
        self.s_mul, self.s_dec, self.s_ls = sem("s_lmul"), sem("s_dec"), sem("s_ls")
        self.s_lst = sem("s_lst")
        H = SL // 2
        M = self.MASKS
        self.vec = {2: [self.v_const], M: [self.v_masks], M + 2: [self.v_prefix], M + 3: [self.v_ahead],
                    M + 4: [self.v_rank], M + 5: [self.v_slot], M + 6: [self.v_slot2], M + 7: [self.v_digits]}
        self.act = {1: [self.a_sct], M + 1: [self.a_mk], M + 2: [self.a_tot, lambda a: self.a_rank(a, (0,))],
                    M + 3: [lambda a: self.a_rank(a, (1, 2))], M + 3.5: [lambda a: self.a_rank(a, (3,))],
                    M + 7.5: [self.a_digits]}
        self.pe = {1: [self.p_sct], M + 1: [self.p_masks], M + 2: [self.p_tot, lambda e: self.p_rank(e, (0,))],
                   M + 3: [lambda e: self.p_rank(e, (1, 2))], M + 3.5: [lambda e: self.p_rank(e, (3,))]}
        put = lambda table, step, f: table.setdefault(step, []).append(f)
        places = [x for s in range(self.CHUNKS, 4 * self.CHUNKS) for x in [s] * (2 if s % 4 == 3 else 1) + [s + 0.5] * (4 if s % 4 == 1 else 0)]
        later = lambda place, n: sorted(set(x for x in places if x > place))[n - 1]
        for k in range(2 * GROUPS):
            at = lambda piece: places[5 * k + piece]
            for h in range(2):
                put(self.vec, at(h), lambda v, k=k, h=h: self.v_lo1(v, k, h))
                put(self.vec, at(2 + h), lambda v, k=k, h=h: self.v_hi1(v, k, h))
                put(self.pe, min(later(at(4), 2 + h), places[5 * (k + 2)]), lambda e, k=k, h=h: self.p_lists(e, k, h))
            put(self.vec, at(4), lambda v, k=k: self.v_val(v, k))
            if k % 2:
                put(self.act, later(at(4), 4), lambda a, k=k: self.a_dec(a, k // 2))
                put(self.vec, later(at(4), 4), lambda v, k=k: self.v_dec(v, k // 2))

    def run(self, table, eng, step, rest=False):
        for s in sorted(table):
            if (s > step) if rest else (s == step):
                for f in table[s]:
                    f(eng)

    def pool(self, g):
        g.iota(self.mcol[:, :], [[1, P]], base=0, channel_multiplier=0)
        g.iota(self.mrow[:, :], [[0, 1]], base=0, channel_multiplier=1)
        g.iota(self.pcol_i[:, :], [[0, 1]], base=0, channel_multiplier=1)
        g.iota(self.TVi[:, :], [[NU, 4], [1, NU], [0, GE]], base=0, channel_multiplier=0)
        g.memset(self.ones[:, :], 1.0)
        for i in range(NBIT + 4):
            g.memset(self.BT[:, i:i + 1], 1 << (NBIT - 1 - i) if i < NBIT else 0)
        for v in range(SL):
            g.memset(self.VI[:, v, :], float(v))
        g.drain().then_inc(self.s_const, 1)
        for k in range(2 * GROUPS):
            if k >= 2:
                g.wait_ge(self.s_mul, 2 * (k - 1))
            g.wait_ge(self.s_hi1, 2 * k + 2)
            g.tensor_tensor(self.val[:, k % 2, 1, SL // 2:SL, :], self.hi1[:, SL // 2:SL, :], self.tile_numbers(k, SL // 2),
                            ALU.mult).then_inc(self.s_val_pool, 1)

    def cols(self, k):
        return k // 2, slice(k % 2 * CW, (k % 2 + 1) * CW)

    def tile_numbers(self, k, n):
        return self.TV[:, self.cols(k)[1]].unsqueeze(1).to_broadcast([P, n, CW])

    def count(self, v, i):
        v.tensor_scalar(self.junk[:, :], self.SCT[:, :], self.cand[:, 0:1].bitcast(F32), 0.0, ALU.is_ge, ALU.add,
                        accum_out=self.cnt[:, 0:1]).then_inc(self.s_cnt, 1)

    def sum(self, pe, i):
        wait(pe, self.s_cnt, i + 1)
        pe.matmul(self.ps[:, 0, 0:1], self.same[:, :], self.cnt[:, 0:1], start=True, stop=True).then_inc(self.s_sum, 1)

    def update(self, v, i):
        wait(v, self.s_sum, i + 1)
        v.scalar_tensor_tensor(self.off[:, :], self.ps[:, 0, 0:1], float(CAP), self.BT[:, bass.ds(i, 1)], ALU.is_lt, ALU.mult)
        v.drain()
        v.scalar_tensor_tensor(self.cand[:, :], self.cand[:, :], self.BT[:, bass.ds(i + 1, 1)], self.off[:, :],
                               ALU.bitwise_or, ALU.bitwise_xor)
        v.drain()

    def vec_step(self, v, s):
        first, n = self.FIRST_COUNT, self.MASKS
        if not isinstance(s, int):
            self.update(v, s - first - 1)
            self.count(v, s - first)
            return
        if first < s < n:
            self.update(v, s - first - 1)
        if first <= s < n:
            self.count(v, s - first)
        self.run(self.vec, v, s)

    def pe_middle(self, pe, s):
        if not isinstance(s, int) or self.FIRST_COUNT < s - 1 < self.MASKS:
            self.sum(pe, s - self.FIRST_COUNT - 2)

    def pe_step(self, pe, s):
        if isinstance(s, int):
            self.run(self.pe, pe, s)

    def act_step(self, a, s):
        if isinstance(s, int):
            self.run(self.act, a, s)

    def p_sct(self, pe):
        for h in range(2):
            for j in range(4):
                i = pe.transpose(self.ps[:, h, j * P:(j + 1) * P], self.c.SC[:, j, 8 * h:8 * h + 8, :].rearrange("p u e -> p (u e)"),
                                 self.c.ident[:, :])
        i.then_inc(self.s_sct, 1)

    def a_sct(self, a):
        a.wait_ge(self.s_sct, 1)
        a.activation(self.SCT[:, :], self.ps[:, :, :].rearrange("p h c -> p (h c)"), ACT.Copy).then_inc(self.s_scv, 1)

    def v_const(self, v):
        v.wait_ge(self.s_const, 1)
        v.tensor_copy(self.mcolf[:, :], self.mcol[:, :])
        v.tensor_copy(self.mrowf[:, :], self.mrow[:, :])
        v.tensor_copy(self.pcol[:, :], self.pcol_i[:, :])
        v.tensor_copy(self.TV[:, :], self.TVi[:, :])
        v.tensor_copy(self.identb[:, :], self.c.ident[:, :])
        v.tensor_copy(self.cand[:, :], self.BT[:, 0:1])
        v.drain()
        v.tensor_scalar(self.incl[:, :], self.mcolf[:, :], self.mrowf[:, 0:1], None, ALU.is_ge)
        v.tensor_scalar(self.strict[:, :], self.mcolf[:, :], self.mrowf[:, 0:1], None, ALU.is_gt)
        v.tensor_scalar(self.mcol[:, :], self.mcol[:, :], E - 1, None, ALU.bitwise_and)
        v.tensor_scalar(self.mrow[:, :], self.mrow[:, :], E - 1, None, ALU.bitwise_and)
        v.drain()
        v.tensor_copy(self.mcolf[:, :], self.mcol[:, :])
        v.tensor_copy(self.mrowf[:, :], self.mrow[:, :])
        v.drain()
        v.tensor_scalar(self.same[:, :], self.mcolf[:, :], self.mrowf[:, 0:1], None, ALU.is_equal)
        v.wait_ge(self.s_scv, 1)
        v.drain()

    def v_masks(self, v):
        thr = self.cand[:, 0:1].bitcast(F32)
        v.tensor_scalar(self.MT[:, 0, :], self.SCT[:, :], thr, None, ALU.is_gt)
        v.tensor_scalar(self.MT[:, 1, :], self.SCT[:, :], thr, None, ALU.is_equal).then_inc(self.s_mask, 1)

    def p_masks(self, pe):
        pe.wait_ge(self.s_mask, 1)
        for k in range(2):
            out = self.ps[:, k, :].bitcast(BF16)
            for t in range(8):
                i = pe.transpose(out[:, t * P:(t + 1) * P], self.MT[:, k, t * P:(t + 1) * P], self.identb[:, :])
        i.then_inc(self.s_mt, 1)

    def a_mk(self, a):
        a.wait_ge(self.s_mt, 1)
        for k in range(2):
            for h in range(2):
                i = a.activation(self.MK[:, :, k, h * P:(h + 1) * P],
                                 self.ps[:, k, :].bitcast(BF16)[:, h * 512:(h + 1) * 512].rearrange("p (j q) -> p j q", j=4), ACT.Copy)
        i.then_inc(self.s_mk, 1)

    def mk(self, j):
        return self.MK[:, j, :, :].rearrange("p k n -> p (k n)")

    def p_tot(self, pe):
        pe.wait_ge(self.s_mk, 1)
        for j in range(4):
            i = pe.matmul(self.ps[:, 0, :], self.ones[:, :], self.mk(j), start=(j == 0), stop=(j == 3))
        i.then_inc(self.s_tot, 1)

    def a_tot(self, a):
        a.wait_ge(self.s_tot, 1)
        a.activation(self.tot[0][:, :, :, :].rearrange("p k u e -> p (k u e)"), self.ps[:, 0, :], ACT.Copy).then_inc(self.s_totc, 1)

    def p_rank(self, pe, js):
        for j in js:
            pe.wait_ge(self.s_totc, 1)
            if j >= 1:
                wait(pe, self.s_rkc, j - 1)
            for jj in range(4):
                i = pe.matmul(self.ps[:, (j + 1) % 2, :], (self.incl if jj < j else self.strict)[:, :], self.mk(jj),
                              start=(jj == 0), stop=(jj == 3))
            i.then_inc(self.s_rank, 1)

    def a_rank(self, a, js):
        for j in js:
            a.wait_ge(self.s_rank, j + 1)
            a.activation(self.RK[:, j, :, :].rearrange("p k n -> p (k n)"), self.ps[:, (j + 1) % 2, :], ACT.Copy).then_inc(self.s_rkc, 1)

    def v_prefix(self, v):
        v.wait_ge(self.s_totc, 1)
        cur, step = 0, 1
        while step < NU:
            a, b = self.tot[cur], self.tot[1 - cur]
            v.tensor_copy(b[:, :, 0:step, :], a[:, :, 0:step, :])
            v.tensor_tensor(b[:, :, step:NU, :], a[:, :, step:NU, :], a[:, :, 0:NU - step, :], ALU.add)
            v.drain()
            cur, step = 1 - cur, 2 * step
        self.inc = self.tot[cur]

    def v_ahead(self, v):
        pre, inc = self.PRE[:, :, :].rearrange("p k (u e) -> p k u e", e=E), self.inc
        v.memset(pre[:, :, 0:1, :], 0.0)
        v.tensor_copy(pre[:, :, 1:NU, :], inc[:, :, 0:NU - 1, :])
        v.drain()
        v.tensor_tensor(pre[:, 1, :, :], pre[:, 1, :, :], inc[:, 0, NU - 1:NU, :].to_broadcast([P, NU, E]), ALU.add)
        v.drain()

    def v_rank(self, v):
        v.wait_ge(self.s_rkc, 4)
        v.tensor_tensor(self.RK[:, :, :, :].rearrange("p j k n -> p j (k n)"), self.RK[:, :, :, :].rearrange("p j k n -> p j (k n)"),
                        self.PRE[:, :, :].rearrange("p k n -> p (k n)").unsqueeze(1).to_broadcast([P, 4, 2 * NG]), ALU.add)
        v.drain()

    def v_slot(self, v):
        for k in range(2):
            v.scalar_tensor_tensor(self.RK[:, :, k, :], self.RK[:, :, k, :], -4096.0, self.MK[:, :, k, :], ALU.add, ALU.mult)
        v.drain()

    def v_slot2(self, v):
        v.tensor_tensor(self.RK[:, :, 0, :], self.RK[:, :, 0, :], self.RK[:, :, 1, :], ALU.add)
        v.drain()
        v.tensor_scalar(self.SCT[:, :].bitcast(I32).rearrange("p (j n) -> p j n", j=4), self.RK[:, :, 0, :], 4096.0, None, ALU.add)
        v.drain()

    def v_digits(self, v):
        slot = self.SCT[:, :].bitcast(I32)
        v.tensor_scalar(self.digit[:, :], slot, 5, None, ALU.logical_shift_right)
        v.drain()
        v.tensor_scalar(slot, slot, SL - 1, None, ALU.bitwise_and).then_inc(self.s_dig, 1)

    def a_digits(self, a):
        a.wait_ge(self.s_dig, 1)
        for dst, src in ((self.LO, self.SCT[:, :].bitcast(I32)), (self.HI, self.digit[:, :])):
            i = a.activation(dst[:, :, :].rearrange("p g (t e) -> p g t e", e=GE),
                             src.rearrange("p (t g e) -> p g t e", g=GROUPS, e=GE), ACT.Copy).then_inc(self.s_digc, 1)

    def one_hot(self, v, out, digits, k, h):
        g, cols = self.cols(k)
        a, n = h * SL // 2, SL // 2
        return v.tensor_tensor(out[:, a:a + n, :], digits[:, g, cols].unsqueeze(1).to_broadcast([P, n, CW]),
                               self.VI[:, a:a + n, :], ALU.is_equal)

    def v_lo1(self, v, k, h):
        if h == 0:
            v.wait_ge(self.s_digc, 2)
            wait(v, self.s_mul, 2 * (k - 1))
        g, cols = self.cols(k)
        a, n = h * SL // 2, SL // 2
        split = lambda x: x.rearrange("p v (t e) -> p v t e", e=GE)
        v.tensor_tensor(self.lo1[:, k % 2, :, a:a + n, :].rearrange("p t v e -> p v t e"),
                        split(self.LO[:, g, cols].unsqueeze(1).to_broadcast([P, n, CW])),
                        split(self.VI[:, a:a + n, :]), ALU.is_equal).then_inc(self.s_lo1, 1)

    def v_hi1(self, v, k, h):
        if h == 0 and k:
            v.wait_ge(self.s_val, k)
            v.wait_ge(self.s_val_pool, k)
        self.one_hot(v, self.hi1, self.HI, k, h).then_inc(self.s_hi1, 1)

    def v_val(self, v, k):
        v.wait_ge(self.s_hi1, 2 * k + 2)
        wait(v, self.s_mul, 2 * (k - 1))
        v.tensor_scalar(self.val[:, k % 2, 0, :, :], self.hi1[:, :, :], self.pcol[:, 0:1], None, ALU.mult)
        v.tensor_tensor(self.val[:, k % 2, 1, 0:SL // 2, :], self.hi1[:, 0:SL // 2, :], self.tile_numbers(k, SL // 2),
                        ALU.mult).then_inc(self.s_val, 1)

    def p_lists(self, pe, k, h):
        g = k // 2
        if h == 0:
            pe.wait_ge(self.s_lo1, 2 * k + 2)
            pe.wait_ge(self.s_val, k + 1)
            pe.wait_ge(self.s_val_pool, k + 1)
            if k % 2 == 0:
                wait(pe, self.s_dec, g - 1)
        tiles = CW // GE
        for t in range(h * tiles // 2, (h + 1) * tiles // 2):
            cols = slice(t * GE, (t + 1) * GE)
            i = pe.matmul(self.ps[:, g % 2, 0:2 * SL * GE], self.lo1[:, k % 2, t, :, :].rearrange("p v e -> p (v e)"), self.val[:, k % 2, :, :, cols],
                          start=(k % 2 == 0 and t == 0), stop=(k % 2 == 1 and t == tiles - 1))
        i.then_inc(self.s_mul, 1)

    def a_dec(self, a, g):
        a.wait_ge(self.s_mul, 4 * (g + 1))
        wait(a, self.s_ls, g)
        a.activation(self.vi[:, :, :].rearrange("m a (e h) -> m a h e", e=GE),
                     self.ps[:, g % 2, 0:2 * SL * GE].rearrange("m (a h e) -> m a h e", a=2, e=GE), ACT.Copy).then_inc(self.s_dec, 1)

    def v_dec(self, v, g):
        v.wait_ge(self.s_dec, g + 1)
        u, j = self.vu[:, 0, :], self.vj[:, 0, :]
        v.tensor_scalar(u, self.vi[:, 1, :], NU - 1, None, ALU.bitwise_and)
        v.tensor_scalar(j, self.vi[:, 1, :], 4, None, ALU.logical_shift_right)
        v.drain()
        v.scalar_tensor_tensor(j, self.vi[:, 0, :], 4.0, j, ALU.mult, ALU.add)
        v.drain()
        v.scalar_tensor_tensor(self.LS[:, g, :, :].rearrange("m e h -> m (e h)"), u, 512.0, j, ALU.mult, ALU.add)
        v.drain().then_inc(self.s_ls, 1)

    def store(self, sp):
        sp.wait_ge(self.s_ls, GROUPS)
        for e in range(GE):
            sp.dma_start(self.io["LIST"].rearrange("(g e) (l h) -> e l g h", e=GE, l=SL)[e],
                         self.LS[e:e + GE * (SL - 1) + 1:GE, :, e, :]).then_inc(self.s_lst, 16)
        sp.wait_ge(self.s_lst, 16 * GE)
        sp.dma_start(self.c.IDX[:, :, :], self.io["LIST"].rearrange("e (p c) -> p e c", p=P)).then_inc(self.s_lst, 16)
        sp.wait_ge(self.s_lst, 16 * (GE + 1))


def mlp(nc, io, c, shared):
    NI = (I_SH if shared else I_EXP) // P
    N = NB if shared else E
    W_N = 1 if shared else 2
    SLOTS = NI + 2
    with ExitStack() as ctx:
        tag = "sh_" if shared else "ex_"
        sb = lambda n, s, d=F32: ctx.enter_context(nc.sbuf_tensor(tag + n, s, d))
        pair = lambda n, s: (sb(n + "_hi", s, F32R), sb(n + "_lo", s, F32R))
        wg = [pair(f"wg{i}", [P, KD, NI * P]) for i in range(W_N)]
        wu = [pair(f"wu{i}", [P, KD, NI * P]) for i in range(W_N)]
        wd = pair("wd", [P, NI, D])
        XT = [pair(f"XT{i}", [P, KD, 512]) for i in range(2)]
        GL, HF = sb("GL", [P, 2, 512]), sb("HF", [P, 2, 512])
        H = pair("H", [P, SLOTS, 512])
        OUT = sb("OUT", [P, 8, D])
        lists = None
        psG = ctx.enter_context(nc.psum_tensor(tag + "psG", [P, 2, 512], F32))
        psU = ctx.enter_context(nc.psum_tensor(tag + "psU", [P, 2, 512], F32))
        psX = ctx.enter_context(nc.psum_tensor(tag + "psXT", [P, 2, 512], F32))
        psD = ctx.enter_context(nc.psum_tensor(tag + "psD", [P, 2, 512], F32))
        sem = lambda n: ctx.enter_context(nc.semaphore(tag + n))
        s_up, s_gelu, s_mul, s_hhi, s_hlo = (sem(n) for n in ("s_up", "s_gelu", "s_mul", "s_hhi", "s_hlo"))
        s_dn, s_ev = sem("s_dn"), sem("s_ev")
        s_xt, s_xhi, s_xlo = sem("s_xt"), sem("s_xhi"), sem("s_xlo")
        s_raw = {n: sem("s_raw_" + n) for n in "gud"}
        s_whi = {n: sem("s_whi_" + n) for n in "gud"}
        s_wlo = {n: sem("s_wlo_" + n) for n in "gud"}
        EV0 = 2
        if shared:
            XR = sb("XR", [P, 2, KD, 512])
            s_xr = [sem("s_xr0"), sem("s_xr1")]
            s_st = [sem("s_st0"), sem("s_st1")]
            lists = TopK(nc, io, c, sb, sem, psX)
            spare = lists.lo1[:, :, :, :, :].rearrange("p b t v e -> p (b t v e)").bitcast(F32)
            raw = {w: spare[:, i * NI * D:(i + 1) * NI * D] for i, w in enumerate("gud")}
        else:
            raw = {w: sb("raw_" + w, [P, NI * D])[:, :] for w in "gud"}
            XG = [sb(f"XG{i}", [P, 8, ROW]) for i in range(2)]
            GI = [sb(f"GI{i}", [P, 8], I32) for i in range(2)]
            TW = [sb(f"TW{i}", [P, 8]) for i in range(2)]
            s_gi, s_tw = sem("s_gi"), sem("s_tw")
            s_ga = [sem("s_ga0"), sem("s_ga1")]
            s_sc = [sem("s_sc0"), sem("s_sc1")]
        blk = ctx.enter_context(nc.Block())

        def slot(tb, it):
            return it if tb == 0 or it >= 2 else NI + it

        def units(body):
            def run(eng):
                if shared:
                    body(0, 0, False)
                    with eng.Fori(1, 4) as n:
                        body(n, 0, False)
                    for n in range(4, N):
                        body(n, 0, n == N - 1)
                    return
                for q in range(2):
                    body(q, q, False)
                with eng.Fori(1, N // 2 - 1) as r:
                    for q in range(2):
                        body(2 * r + q, q, False)
                for q in range(2):
                    body(N - 2 + q, q, q == 1)
            return run

        def schedule(n, q, last, step, down):
            for tb in range(2):
                h = 2 * n + tb
                for it in range(2, NI):
                    step(n, h, q, tb, it)
                if not (last and tb):
                    n2, q2, tb2 = (n, q, 1) if tb == 0 else (n + 1, 1 - q, 0)
                    for it in range(2):
                        step(n2, h + 1, q2, tb2, it)
                down(n, h, q, tb)

        @blk.tensor
        def _(pe):
            def turn(n, h, q, tb, dk):
                if tb == 0 and dk == 0:
                    wait(pe, s_ga[q], 128 * (n // 2 + 1) if isinstance(n, int) else 64 * (n + 2 - q))
                wait(pe, s_xlo, 2 * h + dk - 1)
                for t in range(4):
                    i = pe.transpose(psX[:, dk, t * P:(t + 1) * P], XG[q][:, 4 * tb + t, dk * P:(dk + 1) * P], c.ident[:, :])
                i.then_inc(s_xt, 1)

            def step(n, h, q, tb, it):
                s = NI * h + it
                if tb == 0 and (not shared or isinstance(n, int)):
                    if it % 2 == 0:
                        u = 0 if shared else n
                        quarter = it * 4 // NI if shared else it // 2
                        for w in "gu":
                            wait(pe, s_wlo[w], 4 * u + quarter + 1)
                    elif shared:
                        for w in "gu":
                            wait(pe, s_wlo[w], it + 1)
                if it == 0:
                    wait(pe, s_xlo, 2 * (h + 1))
                wait(pe, s_mul, s - 1)
                cols = slice(it * P, (it + 1) * P)
                for ps, w in ((psG, wg), (psU, wu)):
                    w_hi, w_lo = w[q % W_N]
                    for k in range(KD):
                        i = mm3(pe, ps[:, it % 2, :], w_hi[:, k, cols], w_lo[:, k, cols],
                                XT[tb][0][:, k, :], XT[tb][1][:, k, :], k == 0, k == KD - 1)
                    if lists and w is wg:
                        lists.pe_middle(pe, s)
                i.then_inc(s_up, 1)
                if not shared and it in (3, 4):
                    n2, q2, tb2 = (n, q, 1) if tb == 0 else (n + 1, 1 - q, 0)
                    if not (isinstance(n2, int) and n2 >= N):
                        turn(n2, h + 1, q2, tb2, it - 3)
                if lists:
                    lists.pe_step(pe, s)

            def down(n, h, q, tb):
                wait(pe, s_hlo, NI * (h + 1))
                if tb == 0 and (not shared or isinstance(n, int)):
                    wait(pe, s_wlo["d"], 4 if shared else 4 * (n + 1))
                for t in range(4):
                    wait(pe, s_ev, EV0 + 4 * h + t - 1)
                    for it in range(NI):
                        z = slot(tb, it)
                        i = mm3(pe, psD[:, t % 2, 0:D], H[0][:, z, t * P:(t + 1) * P], H[1][:, z, t * P:(t + 1) * P],
                                wd[0][:, it, :], wd[1][:, it, :], it == 0, it == NI - 1)
                    i.then_inc(s_dn, 1)
                if lists and isinstance(h, int) and h < 2 * N - 1:
                    lists.run(lists.pe, pe, NI * (h + 1) + 1.5)

            if not shared:
                for dk in range(KD):
                    turn(0, 0, 0, 0, dk)
            if shared:
                for w in "gud":
                    wait(pe, s_wlo[w], 4)
            for it in range(2):
                step(0, 0, 0, 0, it)
            units(lambda n, q, last: schedule(n, q, last, step, down))(pe)
            if lists:
                lists.run(lists.pe, pe, 2 * NI * N - 1, True)

        def weight_part(w, q, quarter):
            if w == "d":
                a = NI // 4
                cut = lambda t: t[:, quarter * a:(quarter + 1) * a, :]
                return cut(raw[w].rearrange("p (i n) -> p i n", n=D)), cut(wd[0]), cut(wd[1])
            a = NI * P // 4
            cut = lambda t: t[:, :, quarter * a:(quarter + 1) * a]
            hi, lo = (wg if w == "g" else wu)[q % W_N]
            return cut(raw[w].rearrange("p (k n) -> p k n", k=KD)), cut(hi), cut(lo)

        def w_hi(a, w, n, q, quarter):
            src, hi, _ = weight_part(w, q, quarter)
            if quarter == 0:
                wait(a, s_raw[w], 16 * (n + 1))
                if w == "d":
                    wait(a, s_dn, 8 * n)
                else:
                    wait(a, s_up, 2 * NI * (n - 1) if isinstance(n, int) else NI * 2 * (n - 1))
            a.activation(hi, src, ACT.Copy).then_inc(s_whi[w], 1)

        def w_lo(v, w, n, q, quarter):
            src, hi, lo = weight_part(w, q, quarter)
            wait(v, s_whi[w], 4 * n + quarter + 1)
            v.tensor_tensor(lo, src, hi.bitcast(F32), ALU.subtract).then_inc(s_wlo[w], 1)

        def weight_task(n, tb, it, last):
            if shared:
                return None
            if tb == 0:
                return ("d", 0, it - 2) if 2 <= it < 6 else None
            if last:
                return None
            return ("g", 1, it) if it < 4 else ("u", 1, it - 4)

        def x_part(h, tb, dk):
            src = XR[:, tb, dk, :] if shared else psX[:, dk, :]
            return src, XT[tb][0][:, dk, :], XT[tb][1][:, dk, :]

        def x_hi(a, n, h, tb, dk):
            src, hi, _ = x_part(h, tb, dk)
            if dk == 0:
                wait(a, s_up, NI * (h - 1))
                if shared:
                    wait(a, s_xr[tb], 16 * (n + 1))
            if not shared:
                wait(a, s_xt, 2 * h + dk + 1)
            a.activation(hi, src, ACT.Copy).then_inc(s_xhi, 1)

        def x_lo(v, n, h, tb, dk):
            src, hi, lo = x_part(h, tb, dk)
            wait(v, s_xhi, 2 * h + dk + 1)
            v.tensor_tensor(lo, src, hi.bitcast(F32), ALU.subtract).then_inc(s_xlo, 1)

        XAT = (1, 2) if shared else (3, 4)

        def next_x(f, eng, n, h, tb, it):
            if it in XAT:
                n2, tb2 = (n, 1) if tb == 0 else (n + 1, 0)
                if not (isinstance(n2, int) and n2 >= N):
                    f(eng, n2, h + 1, tb2, it - XAT[0])
                    return n2, tb2

        @blk.scalar
        def _(a):
            a.sem_inc(s_ev, EV0)

            def part_hi(h, tb, it):
                wait(a, s_mul, NI * h + it + 1)
                if it == 2:
                    wait(a, s_dn, 4 * h)
                a.activation(H[0][:, slot(tb, it), :], HF[:, it % 2, :], ACT.Copy).then_inc(s_hhi, 1)

            def step(n, h, q, tb, it, last=False):
                s = NI * h + it
                wait(a, s_up, s + 1)
                wait(a, s_mul, s - 1)
                a.activation(GL[:, it % 2, :], psG[:, it % 2, :], ACT.Gelu).then_inc(s_gelu, 1)
                if it:
                    part_hi(h, tb, it - 1)
                elif not (isinstance(s, int) and s == 0):
                    part_hi(h - 1, 1 - tb, NI - 1)
                task = weight_task(n, tb, it, isinstance(n, int) and n == N - 1)
                if task:
                    w_hi(a, task[0], n + task[1], (q + task[1]) % 2, task[2])
                next_x(x_hi, a, n, h, tb, it)
                if lists:
                    lists.act_step(a, s)

            def down(n, h, q, tb):
                if isinstance(h, int) and h == 2 * N - 1:
                    part_hi(h, tb, NI - 1)
                for t in range(4):
                    z = 4 * tb + t
                    wait(a, s_dn, 4 * h + t + 1)
                    if t == 0:
                        if shared:
                            wait(a, s_st[tb], 16 * n)
                        elif tb == 0:
                            wait(a, s_tw, n + 1)
                            wait(a, s_sc[1 - q], 64 * (n - q) + 128 * q)
                    scale = 1.0 if shared else TW[q][:, z:z + 1]
                    a.activation(OUT[:, z, :], psD[:, t % 2, 0:D], ACT.Copy, scale=scale).then_inc(s_ev, 1)
                if lists and isinstance(h, int) and h < 2 * N - 1:
                    lists.run(lists.act, a, NI * (h + 1) + 1.5)

            for w in "gud" if shared else "gu":
                for quarter in range(4):
                    w_hi(a, w, 0, 0, quarter)
            for dk in range(KD):
                x_hi(a, 0, 0, 0, dk)
            for it in range(2):
                step(0, 0, 0, 0, it)
            units(lambda n, q, last: schedule(n, q, last, step, down))(a)
            if lists:
                lists.run(lists.act, a, 2 * NI * N - 1, True)

        @blk.vector
        def _(v):
            def part_lo(h, tb, it):
                wait(v, s_hhi, NI * h + it + 1)
                v.tensor_tensor(H[1][:, slot(tb, it), :], HF[:, it % 2, :],
                                H[0][:, slot(tb, it), :].bitcast(F32), ALU.subtract).then_inc(s_hlo, 1)

            def scores_of(n, q):
                wait(v, s_ga[q], 128 * (n // 2 + 1) if isinstance(n, int) else 64 * (n + 2 - q))
                wait(v, s_ev, EV0 + 8 * (n - 1) if not (isinstance(n, int) and n < 2) else 0)
                v.tensor_copy(TW[q][:, :], XG[q][:, :, bass.ds(D + n, 1)].rearrange("p t o -> p (t o)")).then_inc(s_tw, 1)

            def step(n, h, q, tb, it):
                s = NI * h + it
                wait(v, s_gelu, s + 1)
                if not (isinstance(s, int) and s < 2):
                    wait(v, s_hlo, s - 1)
                v.tensor_tensor(HF[:, it % 2, :], psU[:, it % 2, :], GL[:, it % 2, :], ALU.mult).then_inc(s_mul, 1)
                if it:
                    part_lo(h, tb, it - 1)
                elif not (isinstance(s, int) and s == 0):
                    part_lo(h - 1, 1 - tb, NI - 1)
                task = weight_task(n, tb, it, isinstance(n, int) and n == N - 1)
                if task:
                    w_lo(v, task[0], n + task[1], (q + task[1]) % 2, task[2])
                got = next_x(x_lo, v, n, h, tb, it)
                if lists:
                    lists.vec_step(v, s)
                if got and not shared and it == XAT[1] and got[1] == 0:
                    scores_of(got[0], 1 - q)

            def down(n, h, q, tb):
                if isinstance(h, int) and h == 2 * N - 1:
                    part_lo(h, tb, NI - 1)
                if lists and isinstance(h, int) and h < 2 * N - 1:
                    lists.run(lists.vec, v, NI * (h + 1) + 1.5)

            for w in "gud" if shared else "gu":
                for quarter in range(4):
                    w_lo(v, w, 0, 0, quarter)
            for dk in range(KD):
                x_lo(v, 0, 0, 0, dk)
            if not shared:
                scores_of(0, 0)
            for it in range(2):
                step(0, 0, 0, 0, it)
            units(lambda n, q, last: schedule(n, q, last, step, down))(v)
            if lists:
                lists.run(lists.vec, v, 2 * NI * N - 1, True)

        if shared:
            @blk.sync
            def _(sp):
                for w, name in (("g", "sg"), ("u", "su"), ("d", "sd")):
                    sp.dma_start(raw[w], io[name].rearrange("p a n -> p (a n)")).then_inc(s_raw[w], 16)

                def load(n, tb):
                    wait(sp, s_xlo, 2 * (2 * n + tb - 1))
                    sp.dma_start(XR[:, tb, :, :], io["XN2T"][n][:, :, tb * 512:(tb + 1) * 512]).then_inc(s_xr[tb], 16)

                def store(n, tb):
                    wait(sp, s_ev, EV0 + 4 * (2 * n + tb + 1))
                    sp.dma_start(io["ACC"].rearrange("(n h p j) d -> n h p (j d)", n=NB, h=2, p=P)[n][tb],
                                 OUT[:, 4 * tb:4 * tb + 4, :].rearrange("p j d -> p (j d)")).then_inc(s_st[tb], 16)

                for tb in range(2):
                    load(0, tb)

                def body(n, q, last):
                    for tb in range(2):
                        if not last:
                            load(n + 1, tb)
                        store(n, tb)
                units(body)(sp)
                for tb in range(2):
                    sp.wait_ge(s_st[tb], 16 * N)

            @blk.gpsimd
            def _(g):
                lists.pool(g)
                lists.store(g)
        else:
            @blk.sync
            def _(sp):
                def load(w, name, n):
                    wait(sp, s_wlo[w], 4 * n)
                    wait(sp, s_whi[w], 4 * n)
                    sp.dma_start(raw[w], io[name].rearrange("e p a n -> e p (a n)")[n]).then_inc(s_raw[w], 16)
                load("g", "wg", 0)
                load("u", "wu", 0)
                load("d", "wd", 0)

                def body(n, q, last):
                    if not last:
                        load("g", "wg", n + 1)
                        load("u", "wu", n + 1)
                        load("d", "wd", n + 1)
                units(body)(sp)

            s_pass = sem("s_pass")

            @blk.gpsimd
            def _(g):
                def pass_wait(s, value):
                    wait(g, s, value)
                    g.sem_inc(s_pass, 1)

                def gather(n, q):
                    wait(g, s_xt, 4 * (n - 1))
                    wait(g, s_tw, n - 1)
                    if not (isinstance(n, int) and n < 2):
                        wait(g, s_sc[q], 64 * (n - q))
                    g.tensor_copy(GI[q][:, :], c.IDX[:, bass.ds(n, 1), :].rearrange("p o c -> p (o c)")).then_inc(s_gi, 1)
                    pass_wait(s_gi, n + 1)
                    for t in range(8):
                        g.indirect_dma_start(out=XG[q][:, t, :], out_offset=None, in_=io["XN"],
                                             in_offset=bass.IndirectOffsetOnAxis(ap=GI[q][:, t:t + 1], axis=0)).then_inc(s_ga[q], 16)

                def scatter(n, q, tb):
                    for t in range(4 * tb, 4 * tb + 4):
                        if t == 0:
                            wait(g, s_sc[1 - q], 64 * (n - q) + 128 * q)
                        pass_wait(s_ev, EV0 + 8 * n + t + 1)
                        g.indirect_dma_start(out=io["ACC"], out_offset=bass.IndirectOffsetOnAxis(ap=GI[q][:, t:t + 1], axis=0),
                                             in_=OUT[:, t, :], in_offset=None, compute_op=ALU.add).then_inc(s_sc[q], 16)

                gather(0, 0)

                def body(n, q, last):
                    if not last:
                        gather(n + 1, 1 - q)
                    for tb in range(2):
                        scatter(n, q, tb)
                units(body)(g)
                for q in range(2):
                    g.wait_ge(s_sc[q], 64 * N)


def output(nc, io, c):
    with ExitStack() as ctx:
        sb = lambda n, s, d=F32: ctx.enter_context(nc.sbuf_tensor(n, s, d))
        NBUF = 4
        F = [sb(f"F{i}", [P, NT, D]) for i in range(NBUF)]
        X1 = [sb(f"X1_{i}", [P, NT, D]) for i in range(NBUF)]
        st, mv = [sb(f"fst{i}", [P, NT, 6]) for i in range(2)], [sb(f"fmv{i}", [P, NT, 2]) for i in range(2)]
        ve, tmp = sb("fve", [P, NT]), sb("ftmp", [P, NT])
        rs, shift = [sb(f"frs{i}", [P, NT]) for i in range(2)], [sb(f"fsh{i}", [P, NT]) for i in range(2)]
        sem = lambda n: ctx.enter_context(nc.semaphore(n))
        s_ld = [sem(f"s_ld{i}") for i in range(NBUF)]
        s_st = [sem(f"s_st{i}") for i in range(NBUF)]
        s_r, s_n, s_a = sem("s_r"), sem("s_n"), sem("s_a")
        blk = ctx.enter_context(nc.Block())
        flat = lambda t: t[:, :, :].rearrange("p (h j) d -> p h (j d)", h=2)

        @blk.sync
        def _(sp):
            def load(b):
                i = b % NBUF
                wait(sp, s_st[i], 16 * (b // NBUF))
                sp.dma_start(flat(F[i]), rows_of(io["ACC"], b)).then_inc(s_ld[i], 16)
                sp.dma_start(flat(X1[i]), rows_of(io["X1"], b)).then_inc(s_ld[i], 16)
            for b in range(NBUF):
                load(b)
            for b in range(NB):
                wait(sp, s_a, 2 * (b + 1))
                sp.dma_start(rows_of(io["out"], b), flat(F[b % NBUF])).then_inc(s_st[b % NBUF], 16)
                if b + NBUF < NB:
                    load(b + NBUF)
            for i in range(NBUF):
                sp.wait_ge(s_st[i], 16 * (NB // NBUF))

        def add(v, b):
            i = b % NBUF
            for h in range(2):
                wait(v, s_n, 2 * b + h + 1)
                f = F[i][:, 4 * h:4 * h + 4, :]
                v.tensor_tensor(f, f, X1[i][:, 4 * h:4 * h + 4, :], ALU.add).then_inc(s_a, 1)

        @blk.vector
        def _(v):
            for b in range(NB):
                i = b % NBUF
                v.wait_ge(s_ld[i], 32 * (b // NBUF + 1))
                wait(v, s_n, 2 * (b - 1))
                for t in range(NT):
                    v.bn_stats(st[b % 2][:, t, :], F[i][:, t, :])
                v.drain()
                for t in range(NT):
                    v.bn_aggr(mv[b % 2][:, t, :], st[b % 2][:, t, :])
                v.drain()
                for part in range(2):
                    last = layernorm_scale(v, part, mv[b % 2], ve[:, :], rs[b % 2][:, :], shift[b % 2][:, :], tmp[:, :], NT)
                last.then_inc(s_r, 1)
                if b:
                    add(v, b - 1)
            add(v, NB - 1)

        @blk.scalar
        def _(a):
            for b in range(NB):
                i = b % NBUF
                wait(a, s_r, b + 1)
                for h in range(2):
                    for t in range(4 * h, 4 * h + 4):
                        j = a.activation(F[i][:, t, :], F[i][:, t, :], ACT.Identity, bias=shift[b % 2][:, t:t + 1],
                                         scale=rs[b % 2][:, t:t + 1])
                    j.then_inc(s_n, 1)


class Consts:
    pass


def build(nc, io, phases="abcde", taps=None):
    with ExitStack() as ctx:
        c = Consts()
        sb = lambda n, s, d=F32: ctx.enter_context(nc.sbuf_tensor(n, s, d))
        c.ident = sb("ident", [P, P])
        c.SC = sb("SC", [P, 4, NU, E])
        c.IDX = sb("IDX", [P, E, CAP // P], I32)
        with ExitStack() as inner:
            sa = lambda n, s, d=F32: inner.enter_context(nc.sbuf_tensor(n, s, d))
            c.gw = sa("gw", [P, KD, E])
            c.bias = sa("bias", [P, D])
            c.wv, c.wp, c.m = ([sa(f"{n}{z}", [P, KD, D], F32R) for z in (0, 1)] for n in ("wv_", "wp_", "m_"))
            setup(nc, io, c)
            attention(nc, io, c)
        if "c" in phases:
            mlp(nc, io, c, shared=True)
        if "d" in phases:
            mlp(nc, io, c, shared=False)
        if "e" in phases:
            output(nc, io, c)


def layouts(i):
    a = {k: np.asarray(v) for k, v in i.items()}
    wqkv = a["L0_attn_w_qkv"]
    tiles = lambda w: np.ascontiguousarray(w.reshape(-1, P, w.shape[-1]).transpose(1, 0, 2))
    etiles = lambda w: np.ascontiguousarray(w.transpose(0, 2, 1).reshape(E, -1, P, w.shape[1]).transpose(0, 2, 1, 3))
    return {
        "x": np.ascontiguousarray(a["L0_attn_x"].reshape(T, D)),
        "wq": tiles(wqkv[0:D]), "wk": tiles(wqkv[D:2 * D]), "wv": tiles(wqkv[2 * D:].T), "wp": tiles(a["L0_attn_w_proj"].T),
        "bias": np.ascontiguousarray(a["L0_attn_b_proj"]),
        "gate": tiles(a["L0_ffn_gate_w"].T),
        "wg": etiles(a["L0_ffn_Wg"]), "wu": etiles(a["L0_ffn_Wu"]), "wd": etiles(a["L0_ffn_Wd"]),
        "sg": tiles(a["L0_ffn_Sg"].T), "su": tiles(a["L0_ffn_Su"].T), "sd": tiles(a["L0_ffn_Sd"].T),
    }


def kernel(**inputs):
    import concourse.bacc as bacc
    from concourse.bass_utils import run_bass_kernel_spmd as run

    arrays = {f"{n}_in": v for n, v in layouts(inputs).items()}
    nc = bacc.Bacc("TRN2", target_bir_lowering=False, num_devices=1)
    io = {n[:-3]: nc.dram_tensor(n, v.shape, mybir.dt.from_np(v.dtype), kind="ExternalInput").ap() for n, v in arrays.items()}
    io["out"] = nc.dram_tensor("out_dram", (T, D), F32, kind="ExternalOutput").ap()
    for n, shape, dt in (("XN", (T, ROW), F32), ("X1", (T, D), F32), ("XN2T", (NB, P, KD, S), F32), ("ACC", (T, D), F32),
                         ("LIST", (E, CAP), I32)):
        io[n] = nc.dram_tensor(n, shape, dt).ap()
    build(nc, io)
    r = run(nc, [arrays], core_ids=[0])
    return r.results[0]["out_dram"].reshape(NB, S, D)
```

```python
import numpy as np
from contextlib import ExitStack

import concourse.bass as bass
from concourse import mybir

F32 = mybir.dt.float32
F32R = mybir.dt.float32r
BF16 = mybir.dt.bfloat16
I32 = mybir.dt.int32
ALU = mybir.AluOpType
ACT = mybir.ActivationFunctionType
AX = mybir.AxisListType

NB, S, D = 8, 1024, 256
T = NB * S
P = 128
E = 16
CAP = 2 * T // E
I_EXP, I_SH = 4 * D, 2 * D
KD = D // P
NT = S // P
NU = T // 512
ROW = D + E
EPS = 1e-5
XS = 4
GROUPS, GE = 4, 4


def wait(eng, sem, value):
    if isinstance(value, int) and value <= 0:
        return
    eng.wait_ge(sem, value)


def mm3(pe, out, w_hi, w_lo, x_hi, x_lo, first, last):
    pe.matmul(out, w_hi, x_hi, start=first, stop=False)
    pe.matmul(out, w_hi, x_lo, start=False, stop=False)
    return pe.matmul(out, w_lo, x_hi, start=False, stop=last)


def layernorm_scale(v, part, mv, ve, y, shift, t, n):
    if part == 0:
        v.tensor_scalar(ve, mv[:, 0:n, 1], EPS, None, ALU.add)
        v.drain()
        v.tensor_scalar(y.bitcast(I32), ve.bitcast(I32), -0.5, 1597463007.0, ALU.mult, ALU.add)
        v.drain()
    for _ in range(1 + part):
        v.tensor_tensor(t, y, y, ALU.mult)
        v.drain()
        v.scalar_tensor_tensor(t, t, -0.5, ve, ALU.mult, ALU.mult)
        v.drain()
        last = v.scalar_tensor_tensor(y, t, 1.5, y, ALU.add, ALU.mult)
        v.drain()
    if part == 1:
        last = v.scalar_tensor_tensor(shift, mv[:, 0:n, 0], -1.0, y, ALU.mult, ALU.mult)
    return last


def rows_of(dram, b):
    return dram.rearrange("(b h p j) c -> b p h (j c)", b=NB, h=2, p=P)[b]


class Setup:

    def __init__(self, io, c, sem, Y, XNB, xn2T, ps):
        self.io, self.c, self.ps = io, c, ps
        part = lambda t, i: t.rearrange("p a b -> p (a b)")[:, i * KD * D:(i + 1) * KD * D].rearrange("p (k d) -> p k d", k=KD)
        self.raw = {n: part(Y[:, :, :], i) for i, n in enumerate(("wq", "wk", "wv", "wp"))}
        self.mf = part(xn2T[:, :, :], 2)
        n = KD * I_SH
        rows = XNB[:, :, :].rearrange("p a b -> p (a b)")
        self.raw_sh = {"g": rows[:, 0:n], "u": rows[:, n:2 * n], "d": xn2T[:, :, :].rearrange("p a b -> p (a b)")[:, 0:n]}
        self.s_ld = {n: sem("s_ld_" + n) for n in self.raw}
        self.s_sh = {n: sem("s_sh_" + n) for n in self.raw_sh}
        self.s_c, self.s_id = sem("s_c"), sem("s_id")
        self.s_m, self.s_mf = sem("s_m"), sem("s_mf")
        self.s_w, self.s_whi = sem("s_w"), sem("s_whi")

    def sync(self, sp):
        for n in self.raw:
            sp.dma_start(self.raw[n], self.io[n]).then_inc(self.s_ld[n], 16)
        sp.dma_start(self.c.gw[:, :, :], self.io["gate"]).then_inc(self.s_c, 16)
        sp.dma_start(self.c.bias[:, :], self.io["bias"].partition_broadcast(P)).then_inc(self.s_c, 16)
        for w in "gud":
            sp.dma_start(self.raw_sh[w], self.io["s" + w].rearrange("p a n -> p (a n)")).then_inc(self.s_sh[w], 16)

    def pool(self, g):
        ident = self.c.ident[:, :]
        g.memset(ident, 0.0)
        g.drain()
        g.affine_select(out=ident, in_=ident, compare_op=ALU.not_equal, fill=1.0, base=0, pattern=[[-1, P]],
                        channel_multiplier=1).then_inc(self.s_id, 1)

    def tensor(self, pe):
        pe.wait_ge(self.s_ld["wq"], 16)
        pe.wait_ge(self.s_ld["wk"], 16)
        for m in range(KD):
            for k in range(KD):
                i = pe.matmul(self.ps[:, m, 0:D], self.raw["wq"][:, k, m * P:(m + 1) * P], self.raw["wk"][:, k, :],
                              start=(k == 0), stop=(k == KD - 1))
        i.then_inc(self.s_m, 1)
        pe.wait_ge(self.s_id, 1)
        pe.wait_ge(self.s_mf, 1)

    def scalar(self, a):
        a.wait_ge(self.s_m, 1)
        a.activation(self.mf, self.ps[:, 0:KD, 0:D], ACT.Copy, scale=0.25).then_inc(self.s_mf, 1)

    def vector(self, v):
        for n, dst in (("m", self.c.m), ("wv", self.c.wv), ("wp", self.c.wp)):
            if n == "m":
                v.wait_ge(self.s_mf, 1)
                src = self.mf
            else:
                v.wait_ge(self.s_ld[n], 16)
                src = self.raw[n]
            v.tensor_copy(dst[0][:, :, :], src)
            v.drain()
            v.tensor_tensor(dst[1][:, :, :], src, dst[0][:, :, :].bitcast(F32), ALU.subtract).then_inc(self.s_w, 1)

    def shared_hi(self, a, i):
        w = "gud"[i]
        a.wait_ge(self.s_sh[w], 16)
        a.activation(self.c.sw[w][0].rearrange("p a n -> p (a n)"), self.raw_sh[w], ACT.Copy).then_inc(self.s_whi, 1)

    def shared_lo(self, v, i):
        hi, lo = (t.rearrange("p a n -> p (a n)") for t in self.c.sw["gud"[i]])
        v.wait_ge(self.s_whi, i + 1)
        v.tensor_tensor(lo, self.raw_sh["gud"[i]], hi.bitcast(F32), ALU.subtract)


def attention(nc, io, c):
    with ExitStack() as ctx:
        sb = lambda n, s, d=F32: ctx.enter_context(nc.sbuf_tensor(n, s, d))
        pair = lambda n, s: (sb(n + "_hi", s, F32R), sb(n + "_lo", s, F32R))
        X = sb("X", [P, XS, NT, D])
        xn, Y = (c.X1a[:, z, :].rearrange("p (t d) -> p t d", t=NT) for z in range(2))
        xnT = pair("xnT", [P, KD, S])
        tT = pair("tT", [P, KD, S])
        V = pair("V", [P, NT, D])
        Pr = sb("Pr", [P, 2, S])
        PT = pair("PT", [P, 2, NT, P])
        O = pair("O", [P, NT, D])
        XNB = sb("XNB", [P, NT, ROW])
        xn2T = sb("xn2T", [P, KD, S])
        LT = sb("LT", [E, S])
        negmax, rowsum, rinv = sb("negmax", [P, NT]), sb("rowsum", [P, NT]), sb("rinv", [P, NT])
        st = [sb(f"st{n}", [P, NT, 6]) for n in range(3)]
        mv = [sb(f"mv{n}", [P, NT, 2]) for n in range(3)]
        rs = [sb(f"rs{n}", [P, NT]) for n in range(3)]
        shift = [sb(f"shift{n}", [P, NT]) for n in range(3)]
        ve, tmp = sb("ve", [P, NT]), sb("tmp", [P, NT])
        gmax, gsum, SM = sb("gmax", [P, NT]), sb("gsum", [P, NT]), sb("SM", [P, NT, E])
        psS = ctx.enter_context(nc.psum_tensor("psS", [P, 4, 512], F32))
        psPT = ctx.enter_context(nc.psum_tensor("psPT", [P, S], F32))
        psO = ctx.enter_context(nc.psum_tensor("psO", [P, 512], F32))
        psL = ctx.enter_context(nc.psum_tensor("psL", [P, 512], F32))

        sem = lambda n: ctx.enter_context(nc.semaphore(n))
        s_x = sem("s_x")
        s_tr, s_xh, s_xl = sem("s_tr"), sem("s_xh"), sem("s_xl")
        s_tt, s_th, s_tl = sem("s_tt"), sem("s_th"), sem("s_tl")
        s_v, s_vh, s_vl = sem("s_v"), sem("s_vh"), sem("s_vl")
        s_y, s_yb = sem("s_y"), sem("s_yb")
        s_tr2, s_n2 = sem("s_tr2"), sem("s_n2")
        s_lt, s_lte, s_lg = sem("s_lt"), sem("s_lte"), sem("s_lg")
        s_s, s_max, s_exp, s_ri = sem("s_s"), sem("s_max"), sem("s_exp"), sem("s_ri")
        s_t, s_pth, s_ptl = sem("s_t"), sem("s_pth"), sem("s_ptl")
        s_pv, s_oh, s_ol = sem("s_pv"), sem("s_oh"), sem("s_ol")
        s_r1, s_xn, s_ry, s_yn, s_x1, s_r2, s_xn2 = (sem(n) for n in ("s_r1", "s_xn", "s_ry", "s_yn", "s_x1", "s_r2", "s_xn2"))
        s_sm, s_sme, s_sc = sem("s_sm"), sem("s_sme"), sem("s_sc")
        s_x1st, s_xnst, s_xtst = sem("s_x1st"), sem("s_xnst"), sem("s_xtst")
        setup = Setup(io, c, sem, Y, XNB, xn2T, psS)
        blk = ctx.enter_context(nc.Block())

        SHARED_AT = (1, 2, 7)

        def output_bank(i):
            return (psO, psL)[i % 2][:, 0:D]

        class Round:
            def __init__(self, r, attn=True, post=True, gate=True, ln_next=True):
                self.r, self.attn, self.post, self.gate, self.ln_next = r, attn, post, gate, ln_next

        def rounds(eng, body):
            body(Round(0, post=False, gate=False))
            body(Round(1, gate=False))
            body(Round(2))
            with eng.Fori(3, NB - 1) as r:
                body(Round(r))
            body(Round(NB - 1, ln_next=False))
            body(Round(NB, attn=False, ln_next=False))
            body(Round(NB + 1, attn=False, post=False, ln_next=False))

        @blk.sync
        def _(sp):
            def slot(b):
                return X[:, b % XS, :, :].rearrange("p (h j) c -> p h (j c)", h=2)

            sp.dma_start(slot(0), rows_of(io["x"], 0)).then_inc(s_x, 16)
            setup.sync(sp)

            def body(R):
                r = R.r
                if R.ln_next:
                    wait(sp, s_x, 16 * (r + 1))
                    wait(sp, s_x1st, 16 * (r + 2 - XS))
                    sp.dma_start(slot(r + 1), rows_of(io["x"], r + 1)).then_inc(s_x, 16)
                if R.gate:
                    wait(sp, s_n2, 4 * (r - 1))
                    sp.dma_start(io["XN2T"][r - 2], xn2T[:, :, :]).then_inc(s_xtst, 16)
                    wait(sp, s_sc, r - 1)
                    sp.dma_start(rows_of(io["XN"], r - 2),
                                 XNB[:, :, :].rearrange("p (h j) c -> p h (j c)", h=2)).then_inc(s_xnst, 16)
                if R.post:
                    wait(sp, s_x1, 2 * r)
                    sp.dma_start(rows_of(io["X1"], r - 1),
                                 slot(r - 1)).then_inc(s_x1st, 16)
            rounds(sp, body)
            sp.wait_ge(s_x1st, 16 * NB)
            sp.wait_ge(s_xtst, 16 * NB)
            sp.dma_start(c.XR0[:, :, :], io["XN2T"][0][:, :, 0:512]).then_inc(c.s_xr0, 16)
            sp.wait_ge(s_xnst, 16 * NB)
            sp.wait_ge(c.s_xr0, 16)

        @blk.tensor
        def _(pe):
            def turn_x(b, ks):
                for k in ks:
                    dk, ht = k % 2, k // 2
                    if dk == 0:
                        wait(pe, s_xn, 2 * b + ht + 1)
                    for j in range(4):
                        i = pe.transpose(psS[:, k, j * P:(j + 1) * P], xn[:, 4 * ht + j, dk * P:(dk + 1) * P], c.ident[:, :])
                    i.then_inc(s_tr, 1)

            setup.tensor(pe)
            turn_x(0, range(4))
            pe.wait_ge(setup.s_w, 3)
            pe.wait_ge(setup.s_c, 32)

            def body(R):
                r = R.r
                if R.gate:
                    wait(pe, s_xn2, 2 * (r - 1))
                    for k in range(4):
                        dk, ht = k % 2, k // 2
                        if R.attn:
                            wait(pe, s_xl, 4 * r + k + 1)
                        for j in range(4):
                            i = pe.transpose(psS[:, k, j * P:(j + 1) * P], XNB[:, 4 * ht + j, dk * P:(dk + 1) * P], c.ident[:, :])
                        i.then_inc(s_tr2, 1)
                if R.post:
                    wait(pe, s_ol, 8 * r)
                    for k in range(4):
                        hm, jp = k // 2, k % 2
                        if R.gate:
                            wait(pe, s_n2, 4 * (r - 2) + k + 1)
                        elif R.attn:
                            wait(pe, s_xl, 4 * r + k + 1)
                        for jj in range(2):
                            for q in range(2):
                                ot = 2 * (2 * jp + jj) + q
                                i = mm3(pe, psS[:, k, jj * D:(jj + 1) * D],
                                        O[0][:, ot, hm * P:(hm + 1) * P], O[1][:, ot, hm * P:(hm + 1) * P],
                                        c.wp[0][:, q, :], c.wp[1][:, q, :], q == 0, q == 1)
                        i.then_inc(s_y, 1)
                if R.gate:
                    wait(pe, s_n2, 4 * (r - 1))
                    wait(pe, s_sm, r - 2)
                    wait(pe, s_ol, 8 * r if R.attn else 8 * NB)
                    for h, bank in enumerate((psL, psO)):
                        for k in range(KD):
                            i = pe.matmul(bank[0:E, :], c.gw[:, k, :], xn2T[:, k, h * 512:(h + 1) * 512],
                                          start=(k == 0), stop=(k == KD - 1))
                        i.then_inc(s_lt, 1)
                if R.attn:
                    wait(pe, s_xl, 4 * (r + 1))
                    if R.post:
                        wait(pe, s_yb, 4 * r)
                    for k in range(4):
                        m, h = k % 2, k // 2
                        for kk in range(KD):
                            w = [c.m[z][:, kk, m * P:(m + 1) * P] for z in (0, 1)]
                            x = [xnT[z][:, kk, h * 512:(h + 1) * 512] for z in (0, 1)]
                            i = mm3(pe, psS[:, k, :], w[0], w[1], x[0], x[1], kk == 0, kk == KD - 1)
                        i.then_inc(s_tt, 1)
                def gate_back():
                    for t in range(NT):
                        i = pe.transpose(psL[:, t * E:(t + 1) * E], LT[:, t * P:(t + 1) * P], c.ident[0:E, 0:E])
                    i.then_inc(s_lg, 1)

                if R.gate:
                    wait(pe, s_lte, 2 * (r - 1))
                    if not R.attn:
                        gate_back()
                if R.attn:
                    for k in range(4):
                        if k == 1 and R.gate:
                            gate_back()
                        wait(pe, s_tl, 4 * r + k + 1)
                        for t2 in range(2):
                            t = 2 * k + t2
                            for kk in range(KD):
                                w = [xnT[z][:, kk, t * P:(t + 1) * P] for z in (0, 1)]
                                i = mm3(pe, psS[:, k, t2 * D:(t2 + 1) * D], w[0], w[1],
                                        c.wv[0][:, kk, :], c.wv[1][:, kk, :], kk == 0, kk == KD - 1)
                        i.then_inc(s_v, 1)
                    for step in range(NT + 2):
                        i0, i1, i2 = step, step - 1, step - 2
                        if i0 < NT:
                            b = 2 * (i0 % 2)
                            if i0 < 2:
                                wait(pe, s_vl, 4 * r + 2 * i0 + 2)
                            else:
                                wait(pe, s_exp, 8 * r + i0 - 1)
                            for n in range(2):
                                for kk in range(KD):
                                    w = [tT[z][:, kk, i0 * P:(i0 + 1) * P] for z in (0, 1)]
                                    x = [xnT[z][:, kk, n * 512:(n + 1) * 512] for z in (0, 1)]
                                    i = mm3(pe, psS[:, b + n, :], w[0], w[1], x[0], x[1], kk == 0, kk == KD - 1)
                            i.then_inc(s_s, 1)
                        if R.ln_next and i0 >= NT:
                            if i0 == NT:
                                wait(pe, s_exp, 8 * r + 7)
                                turn_x(r + 1, (0, 1))
                            else:
                                wait(pe, s_exp, 8 * r + 8)
                                turn_x(r + 1, (2, 3))
                        def turn_p():
                            wait(pe, s_exp, 8 * r + i1 + 1)
                            wait(pe, s_ptl, 2 * (8 * r + i1))
                            for t in range(NT):
                                i = pe.transpose(psPT[:, t * P:(t + 1) * P], Pr[:, i1 % 2, t * P:(t + 1) * P], c.ident[:, :])
                                if t % 4 == 3:
                                    i.then_inc(s_t, 1)

                        def output(ts):
                            if ts[0] == 0:
                                wait(pe, s_ptl, 2 * (8 * r + i2 + 1))
                                wait(pe, s_ol, 8 * r + i2 - 1)
                                if i2 == 1 and R.gate:
                                    wait(pe, s_sm, r - 1)
                                if i2 == 0:
                                    wait(pe, s_vl, 4 * (r + 1))
                            for t in ts:
                                i = mm3(pe, output_bank(i2), PT[0][:, i2 % 2, t, :], PT[1][:, i2 % 2, t, :],
                                        V[0][:, t, :], V[1][:, t, :], t == 0, t == NT - 1)
                            if ts[-1] == NT - 1:
                                i.then_inc(s_pv, 1)

                        if i0 == NT:
                            output(range(NT // 2))
                            turn_p()
                            output(range(NT // 2, NT))
                        else:
                            if 0 <= i1 < NT:
                                turn_p()
                            if i2 >= 0:
                                output(range(NT))
            rounds(pe, body)

        @blk.scalar
        def _(a):
            def normalize(dst, src, n, h):
                for t in range(4 * h, 4 * h + 4):
                    i = a.activation(dst(t), src(t), ACT.Identity, bias=shift[n][:, t:t + 1], scale=rs[n][:, t:t + 1])
                return i

            def norm_x(b, h):
                wait(a, s_r1, b + 1)
                wait(a, s_tr, 4 * b)
                normalize(lambda t: xn[:, t, :], lambda t: X[:, b % XS, t, :], 0, h).then_inc(s_xn, 1)

            def norm_y(r, h):
                wait(a, s_ry, r)
                normalize(lambda t: Y[:, t, :], lambda t: Y[:, t, :], 1, h).then_inc(s_yn, 1)

            def norm_x1(r, h):
                wait(a, s_r2, r)
                wait(a, s_xnst, 16 * (r - 1))
                normalize(lambda t: XNB[:, t, 0:D], lambda t: X[:, (r - 1) % XS, t, :], 2, h).then_inc(s_xn2, 1)

            def turned_hi(b, ks):
                for k in ks:
                    dk, ht = k % 2, k // 2
                    wait(a, s_tr, 4 * b + k + 1)
                    a.activation(xnT[0][:, dk, ht * 512:(ht + 1) * 512].rearrange("d (p j) -> d j p", j=4),
                                 psS[:, k, :].rearrange("d (j p) -> d j p", j=4), ACT.Copy).then_inc(s_xh, 1)

            setup.scalar(a)
            for h in range(2):
                norm_x(0, h)
            turned_hi(0, range(4))

            def body(R):
                r = R.r
                if R.gate:
                    wait(a, s_xtst, 16 * (r - 2))
                    wait(a, s_lt, 2 * (r - 2))
                    for k in range(4):
                        dk, ht = k % 2, k // 2
                        wait(a, s_tr2, 4 * (r - 2) + k + 1)
                        a.activation(xn2T[:, dk, ht * 512:(ht + 1) * 512], psS[:, k, :], ACT.Copy).then_inc(s_n2, 1)
                    wait(a, s_lg, r - 2)
                    for h, bank in enumerate((psL, psO)):
                        wait(a, s_lt, 2 * (r - 2) + h + 1)
                        a.activation(LT[:, h * 512:(h + 1) * 512], bank[0:E, :], ACT.Copy).then_inc(s_lte, 1)
                if R.attn:
                    for k in range(4):
                        m, h = k % 2, k // 2
                        wait(a, s_tt, 4 * r + k + 1)
                        a.activation(tT[0][:, m, h * 512:(h + 1) * 512], psS[:, k, :], ACT.Copy).then_inc(s_th, 1)
                    for k in range(4):
                        wait(a, s_v, 4 * r + k + 1)
                        a.activation(V[0][:, 2 * k:2 * k + 2, :], psS[:, k, :].rearrange("p (t c) -> p t c", t=2),
                                     ACT.Copy).then_inc(s_vh, 1)
                if R.gate:
                    wait(a, s_sm, r - 1)
                    a.activation(SM[:, :, :], SM[:, :, :], ACT.Exp).then_inc(s_sme, 1)
                if R.attn:
                    for step in range(NT + 2):
                        i0, i1, i2 = step, step - 1, step - 2
                        if R.ln_next and step >= NT:
                            turned_hi(r + 1, (0, 1) if step == NT else (2, 3))
                        if 0 <= i1 < NT:
                            wait(a, s_pv, 8 * r + i1 - 1)
                            for h in range(2):
                                wait(a, s_t, 2 * (8 * r + i1) + h + 1)
                                a.activation(PT[0][:, i1 % 2, 4 * h:4 * h + 4, :],
                                             psPT[:, h * 512:(h + 1) * 512].rearrange("p (t c) -> p t c", t=4),
                                             ACT.Copy).then_inc(s_pth, 1)
                        if i0 < NT:
                            wait(a, s_max, 8 * r + i0 + 1)
                            wait(a, s_t, 2 * (8 * r + i0 - 1))
                            b = 2 * (i0 % 2)
                            a.activation(Pr[:, i0 % 2, :], psS[:, b:b + 2, :].rearrange("p a c -> p (a c)"), ACT.Exp,
                                         bias=negmax[:, i0:i0 + 1], accum_out=rowsum[:, i0:i0 + 1]).then_inc(s_exp, 1)
                        if i2 >= 0:
                            if i2 == 0:
                                wait(a, s_y, 4 * r)
                            wait(a, s_ri, 8 * r + i2 + 1)
                            wait(a, s_pv, 8 * r + i2 + 1)
                            a.activation(O[0][:, i2, :], output_bank(i2), ACT.Copy, scale=rinv[:, i2:i2 + 1]).then_inc(s_oh, 1)
                        if R.post and step in (3, 4):
                            norm_y(r, step - 3)
                        if isinstance(r, int) and r == 0 and step in SHARED_AT:
                            setup.shared_hi(a, SHARED_AT.index(step))
                        if R.ln_next and step in (5, 6):
                            norm_x(r + 1, step - 5)
                        if R.post and step in (7, 8):
                            norm_x1(r, step - 7)
                elif R.post:
                    norm_y(r, 0)
                    norm_x1(r, 0)
            rounds(a, body)

        def stats(v, src, n, part):
            if part < 2:
                for t in range(4 * part, 4 * part + 4):
                    i = v.bn_stats(st[n][:, t, :], src(t))
                return i
            if part == 2:
                v.drain()
                for t in range(NT):
                    v.bn_aggr(mv[n][:, t, :], st[n][:, t, :])
                v.drain()
            return layernorm_scale(v, part - 2, mv[n], ve[:, :], rs[n][:, :], shift[n][:, :], tmp[:, :], NT)

        @blk.vector
        def _(v):
            v.wait_ge(s_x, 16)
            for part in range(4):
                i = stats(v, lambda t: X[:, 0, t, :], 0, part)
            i.then_inc(s_r1, 1)

            def turned_lo(b, ks):
                for k in ks:
                    dk, ht = k % 2, k // 2
                    wait(v, s_xh, 4 * b + k + 1)
                    hi = xnT[0][:, dk, ht * 512:(ht + 1) * 512].rearrange("d (p j) -> d j p", j=4)
                    lo = xnT[1][:, dk, ht * 512:(ht + 1) * 512].rearrange("d (p j) -> d j p", j=4)
                    v.tensor_tensor(lo, psS[:, k, :].rearrange("d (j p) -> d j p", j=4), hi.bitcast(F32),
                                    ALU.subtract).then_inc(s_xl, 1)

            setup.vector(v)
            turned_lo(0, range(4))
            v.wait_ge(setup.s_c, 32)

            def body(R):
                r = R.r
                if R.post:
                    for k in range(4):
                        hm, jp = k // 2, k % 2
                        wait(v, s_y, 4 * (r - 1) + k + 1)
                        t = 4 * hm + 2 * jp
                        v.tensor_tensor(Y[:, t:t + 2, :], psS[:, k, :].rearrange("p (t c) -> p t c", t=2),
                                        c.bias[:, :].unsqueeze(1).to_broadcast([P, 2, D]), ALU.add).then_inc(s_yb, 1)
                if R.attn:
                    for k in range(4):
                        m, h = k % 2, k // 2
                        wait(v, s_th, 4 * r + k + 1)
                        v.tensor_tensor(tT[1][:, m, h * 512:(h + 1) * 512], psS[:, k, :],
                                        tT[0][:, m, h * 512:(h + 1) * 512].bitcast(F32), ALU.subtract).then_inc(s_tl, 1)
                    for k in range(4):
                        wait(v, s_vh, 4 * r + k + 1)
                        v.tensor_tensor(V[1][:, 2 * k:2 * k + 2, :], psS[:, k, :].rearrange("p (t c) -> p t c", t=2),
                                        V[0][:, 2 * k:2 * k + 2, :].bitcast(F32), ALU.subtract).then_inc(s_vl, 1)

                def gate_shift():
                    wait(v, s_lg, r - 1)
                    lg = psL[:, 0:NT * E].rearrange("p (t e) -> p t e", t=NT)
                    v.tensor_reduce(gmax[:, :], lg, AX.X, ALU.max)
                    v.drain()
                    v.tensor_tensor(SM[:, :, :], lg, gmax[:, :].unsqueeze(2).to_broadcast([P, NT, E]),
                                    ALU.subtract).then_inc(s_sm, 1)

                def gate_scores():
                    wait(v, s_sme, r - 1)
                    v.tensor_reduce(gsum[:, :], SM[:, :, :], AX.X, ALU.add)
                    v.drain()
                    v.reciprocal(gsum[:, :], gsum[:, :])
                    v.drain()
                    v.tensor_tensor(XNB[:, :, D:ROW], SM[:, :, :], gsum[:, :].unsqueeze(2).to_broadcast([P, NT, E]), ALU.mult)
                    v.drain()
                    v.tensor_copy(c.SC[:, :, bass.ds(2 * (r - 2), 2), :].rearrange("p j h e -> p h j e"),
                                  XNB[:, :, D:ROW].rearrange("p (h j) e -> p h j e", h=2)).then_inc(s_sc, 1)

                def ln_next(part):
                    if part == 0:
                        wait(v, s_x, 16 * (r + 2))
                    i = stats(v, lambda t: X[:, (r + 1) % XS, t, :], 0, part)
                    if part == 3:
                        i.then_inc(s_r1, 1)

                def ln_y(part):
                    if part == 0:
                        v.drain()
                    i = stats(v, lambda t: Y[:, t, :], 1, part)
                    if part == 3:
                        i.then_inc(s_ry, 1)

                def ln_x1(part):
                    if part < 2:
                        wait(v, s_x1, 2 * (r - 1) + part + 1)
                    i = stats(v, lambda t: X[:, (r - 1) % XS, t, :], 2, part)
                    if part == 3:
                        i.then_inc(s_r2, 1)

                tasks = {}
                if R.post:
                    tasks |= {(0, 1): (ln_y, 0), (1, 0): (ln_y, 1), (2, 0): (ln_y, 2), (2, 1): (ln_y, 3),
                              (5, 0): (ln_x1, 0), (5, 1): (ln_x1, 1), (6, 0): (ln_x1, 2), (6, 1): (ln_x1, 3)}
                if R.ln_next:
                    tasks |= {(3, 0): (ln_next, 0), (3, 1): (ln_next, 1), (4, 0): (ln_next, 2), (4, 1): (ln_next, 3)}

                def task(step, side):
                    if (step, side) in tasks:
                        f, part = tasks[step, side]
                        f(part)

                if R.gate and (R.attn or not R.post):
                    gate_shift()
                for step in range(NT + 3 if R.attn else 0):
                    i0, i1, i3 = step, step - 1, step - 3
                    if i0 < NT:
                        wait(v, s_s, 8 * r + i0 + 1)
                        b = 2 * (i0 % 2)
                        v.tensor_reduce(negmax[:, i0:i0 + 1], psS[:, b:b + 2, :].rearrange("p a c -> p (a c)"), AX.X, ALU.max,
                                        negate=True).then_inc(s_max, 1)
                    if i3 >= 0:
                        wait(v, s_oh, 8 * r + i3 + 1)
                        v.scalar_tensor_tensor(O[1][:, i3, :], output_bank(i3), rinv[:, i3:i3 + 1], O[0][:, i3, :].bitcast(F32),
                                               ALU.mult, ALU.subtract).then_inc(s_ol, 1)
                    if R.ln_next and NT <= step < NT + 2:
                        turned_lo(r + 1, (0, 1) if step == NT else (2, 3))
                    if 0 <= i1 < NT:
                        wait(v, s_exp, 8 * r + i1 + 1)
                        v.reciprocal(rinv[:, i1:i1 + 1], rowsum[:, i1:i1 + 1]).then_inc(s_ri, 1)
                        for h in range(2):
                            wait(v, s_pth, 2 * (8 * r + i1) + h + 1)
                            v.tensor_tensor(PT[1][:, i1 % 2, 4 * h:4 * h + 4, :],
                                            psPT[:, h * 512:(h + 1) * 512].rearrange("p (t c) -> p t c", t=4),
                                            PT[0][:, i1 % 2, 4 * h:4 * h + 4, :].bitcast(F32), ALU.subtract).then_inc(s_ptl, 1)
                    if isinstance(r, int) and r == 0 and step in SHARED_AT:
                        setup.shared_lo(v, SHARED_AT.index(step))
                    task(step, 0)
                    task(step, 1)
                    if step == 1 and R.gate:
                        gate_scores()
                if not R.attn and not R.post:
                    gate_scores()
                if not R.attn and R.post:
                    def normalize(dst, src, n):
                        v.drain()
                        for t in range(NT // 2, NT):
                            i = v.tensor_scalar(dst(t), src(t), rs[n][:, t:t + 1], shift[n][:, t:t + 1], ALU.mult, ALU.add)
                        return i

                    x = X[:, (r - 1) % XS, :, :]
                    ln_y(0)
                    ln_y(1)
                    gate_shift()
                    ln_y(2)
                    gate_scores()
                    ln_y(3)
                    normalize(lambda t: Y[:, t, :], lambda t: Y[:, t, :], 1)
                    v.drain()
                    v.tensor_tensor(x[:, 4:8, :], x[:, 4:8, :], Y[:, 4:8, :], ALU.add).then_inc(s_x1, 1)
                    v.drain()
                    stats(v, lambda t: x[:, t, :], 2, 1)
                    wait(v, s_x1, 2 * r)
                    stats(v, lambda t: x[:, t, :], 2, 0)
                    ln_x1(2)
                    ln_x1(3)
                    wait(v, s_xnst, 16 * (r - 1))
                    normalize(lambda t: XNB[:, t, 0:D], lambda t: x[:, t, :], 2).then_inc(s_xn2, 1)
            rounds(v, body)

        @blk.gpsimd
        def _(g):
            setup.pool(g)

            def add_x(r, halves):
                for h in range(halves):
                    wait(g, s_yn, 2 * (r - 1) + h + 1)
                    x = X[:, (r - 1) % XS, 4 * h:4 * h + 4, :]
                    g.tensor_tensor(x, x, Y[:, 4 * h:4 * h + 4, :], ALU.add).then_inc(s_x1, 1)

            def body(R):
                r = R.r
                if R.post:
                    add_x(r, 2 if R.attn else 1)
            rounds(g, body)


SL = 32
NG = NU * E
SC_N = 4 * NG
CW = SC_N // GROUPS // 2
NBIT = 30


class TopK:
    FIRST_COUNT = 3
    MASKS = FIRST_COUNT + 31
    CHUNKS = MASKS + 8

    def __init__(self, nc, io, c, sb, sem, ps):
        self.io, self.c, self.ps = io, c, ps
        self.SCT = sb("SCT", [P, SC_N])
        self.junk = sb("junk", [P, SC_N], BF16)
        self.cnt = sb("cnt", [P, 1])
        self.off, self.cand, self.BT = sb("off", [P, 1], I32), sb("cand", [P, 1], I32), sb("BT", [P, NBIT + 4], I32)
        self.same = sb("same", [P, P])
        self.mcol, self.mrow = sb("mcol", [P, P], I32), sb("mrow", [P, 1], I32)
        self.mcolf, self.mrowf = sb("mcolf", [P, P]), sb("mrowf", [P, 1])
        self.ones, self.incl, self.strict, self.identb = (sb(n, [P, P], BF16) for n in ("ones", "incl", "strict", "identb"))
        self.val = sb("val", [P, 2, 2, SL, CW], BF16)
        early = self.val[:, :, :, :, :].rearrange("p b a v c -> p (b a v c)")
        cut = lambda a, n: early[:, a:a + n]
        self.MT = cut(0, 2 * SC_N).rearrange("p (k n) -> p k n", k=2)
        self.MK = cut(2 * SC_N, 2 * SC_N).rearrange("p (j k n) -> p j k n", j=4, k=2)
        self.RK = cut(4 * SC_N, 4 * SC_N).bitcast(F32).rearrange("p (j k n) -> p j k n", j=4, k=2)
        self.tot = [sb(f"tot{n}", [P, 2, NU, E]) for n in range(2)]
        self.PRE = sb("PRE", [P, 2, NG])
        self.digit = sb("digit", [P, SC_N], I32)
        self.LO, self.HI = (sb(n, [P, GROUPS, SC_N // GROUPS], BF16) for n in ("LO", "HI"))
        self.TV, self.TVi = sb("TV", [P, SC_N // GROUPS], BF16), sb("TVi", [P, SC_N // GROUPS], I32)
        self.pcol_i, self.pcol = sb("pcol_i", [P, 1], I32), sb("pcol", [P, 1])
        self.VI = sb("VI", [P, SL, CW], BF16)
        self.lo1 = sb("lo1", [P, 2, CW // GE, SL, GE], BF16)
        self.hi1 = sb("hi1", [P, SL, CW], BF16)
        self.vi, self.vu, self.vj = (sb(n, [P, 2, GE * SL], I32) for n in ("vi", "vu", "vj"))
        self.LS = sb("LS", [P, GROUPS, GE, SL], I32)
        self.s_const, self.s_sct, self.s_scv = sem("s_const"), sem("s_sct"), sem("s_scv")
        self.s_cnt, self.s_sum = sem("s_cnt"), sem("s_sum")
        self.s_mask, self.s_mt, self.s_mk = sem("s_mask"), sem("s_mt"), sem("s_mk")
        self.s_tot, self.s_totc, self.s_rank, self.s_rkc = sem("s_tot"), sem("s_totc"), sem("s_rank"), sem("s_rkc")
        self.s_dig, self.s_digc = sem("s_dig"), sem("s_digc")
        self.s_lo1, self.s_hi1 = sem("s_lo1"), sem("s_hi1")
        self.s_val, self.s_val_pool = sem("s_val"), sem("s_val_pool")
        self.s_mul, self.s_dec, self.s_ls = sem("s_lmul"), sem("s_dec"), sem("s_ls")
        self.s_lst = sem("s_lst")
        M = self.MASKS
        self.vec = {2: [self.v_const], M: [self.v_masks], M + 2: [self.v_prefix], M + 3: [self.v_ahead],
                    M + 4: [self.v_rank], M + 5: [self.v_slot], M + 6: [self.v_slot2], M + 7: [self.v_digits]}
        self.act = {1: [self.a_sct], M + 1: [self.a_mk], M + 2: [self.a_tot, lambda a: self.a_rank(a, (0,))],
                    M + 3: [lambda a: self.a_rank(a, (1, 2))], M + 3.5: [lambda a: self.a_rank(a, (3,))],
                    M + 7.5: [self.a_digits]}
        self.pe = {1: [self.p_sct], M + 1: [self.p_masks], M + 2: [self.p_tot, lambda e: self.p_rank(e, (0,))],
                   M + 3: [lambda e: self.p_rank(e, (1, 2))], M + 3.5: [lambda e: self.p_rank(e, (3,))]}
        put = lambda table, step, f: table.setdefault(step, []).append(f)
        places = [x for s in range(self.CHUNKS, 4 * self.CHUNKS)
                  for x in [s] * (2 if s % 4 == 3 else 1) + [s + 0.5] * (4 if s % 4 == 1 else 0)]
        later = lambda place, n: sorted(set(x for x in places if x > place))[n - 1]
        for k in range(2 * GROUPS):
            at = lambda piece: places[5 * k + piece]
            for h in range(2):
                put(self.vec, at(h), lambda v, k=k, h=h: self.v_lo1(v, k, h))
                put(self.vec, at(2 + h), lambda v, k=k, h=h: self.v_hi1(v, k, h))
                put(self.pe, min(later(at(4), 2 + h), places[5 * (k + 2)]), lambda e, k=k, h=h: self.p_lists(e, k, h))
            put(self.vec, at(4), lambda v, k=k: self.v_val(v, k))
            if k % 2:
                put(self.act, later(at(4), 4), lambda a, k=k: self.a_dec(a, k // 2))
                put(self.vec, later(at(4), 4), lambda v, k=k: self.v_dec(v, k // 2))

    def run(self, table, eng, step, rest=False):
        for s in sorted(table):
            if (s > step) if rest else (s == step):
                for f in table[s]:
                    f(eng)

    def pool(self, g):
        g.iota(self.mcol[:, :], [[1, P]], base=0, channel_multiplier=0)
        g.iota(self.mrow[:, :], [[0, 1]], base=0, channel_multiplier=1)
        g.iota(self.pcol_i[:, :], [[0, 1]], base=0, channel_multiplier=1)
        g.iota(self.TVi[:, :], [[NU, 4], [1, NU], [0, GE]], base=0, channel_multiplier=0)
        g.memset(self.ones[:, :], 1.0)
        for i in range(NBIT + 4):
            g.memset(self.BT[:, i:i + 1], 1 << (NBIT - 1 - i) if i < NBIT else 0)
        for v in range(SL):
            g.memset(self.VI[:, v, :], float(v))
        g.drain().then_inc(self.s_const, 1)
        for k in range(2 * GROUPS):
            if k >= 2:
                g.wait_ge(self.s_mul, 2 * (k - 1))
            g.wait_ge(self.s_hi1, 2 * k + 2)
            g.tensor_tensor(self.val[:, k % 2, 1, SL // 2:SL, :], self.hi1[:, SL // 2:SL, :], self.tile_numbers(k, SL // 2),
                            ALU.mult).then_inc(self.s_val_pool, 1)

    def cols(self, k):
        return k // 2, slice(k % 2 * CW, (k % 2 + 1) * CW)

    def tile_numbers(self, k, n):
        return self.TV[:, self.cols(k)[1]].unsqueeze(1).to_broadcast([P, n, CW])

    def count(self, v, i):
        v.tensor_scalar(self.junk[:, :], self.SCT[:, :], self.cand[:, 0:1].bitcast(F32), 0.0, ALU.is_ge, ALU.add,
                        accum_out=self.cnt[:, 0:1]).then_inc(self.s_cnt, 1)

    def sum(self, pe, i):
        wait(pe, self.s_cnt, i + 1)
        pe.matmul(self.ps[:, 0, 0:1], self.same[:, :], self.cnt[:, 0:1], start=True, stop=True).then_inc(self.s_sum, 1)

    def update(self, v, i):
        wait(v, self.s_sum, i + 1)
        v.scalar_tensor_tensor(self.off[:, :], self.ps[:, 0, 0:1], float(CAP), self.BT[:, bass.ds(i, 1)], ALU.is_lt, ALU.mult)
        v.drain()
        v.scalar_tensor_tensor(self.cand[:, :], self.cand[:, :], self.BT[:, bass.ds(i + 1, 1)], self.off[:, :],
                               ALU.bitwise_or, ALU.bitwise_xor)
        v.drain()

    def vec_step(self, v, s):
        first, n = self.FIRST_COUNT, self.MASKS
        if not isinstance(s, int):
            self.update(v, s - first - 1)
            self.count(v, s - first)
            return
        if first < s < n:
            self.update(v, s - first - 1)
        if first <= s < n:
            self.count(v, s - first)
        self.run(self.vec, v, s)

    def pe_middle(self, pe, s):
        if not isinstance(s, int) or self.FIRST_COUNT < s - 1 < self.MASKS:
            self.sum(pe, s - self.FIRST_COUNT - 2)

    def pe_step(self, pe, s):
        if isinstance(s, int):
            self.run(self.pe, pe, s)

    def act_step(self, a, s):
        if isinstance(s, int):
            self.run(self.act, a, s)

    def p_sct(self, pe):
        for h in range(2):
            for j in range(4):
                i = pe.transpose(self.ps[:, h, j * P:(j + 1) * P], self.c.SC[:, j, 8 * h:8 * h + 8, :].rearrange("p u e -> p (u e)"),
                                 self.c.ident[:, :])
        i.then_inc(self.s_sct, 1)

    def a_sct(self, a):
        a.wait_ge(self.s_sct, 1)
        a.activation(self.SCT[:, :], self.ps[:, :, :].rearrange("p h c -> p (h c)"), ACT.Copy).then_inc(self.s_scv, 1)

    def v_const(self, v):
        v.wait_ge(self.s_const, 1)
        v.tensor_copy(self.mcolf[:, :], self.mcol[:, :])
        v.tensor_copy(self.mrowf[:, :], self.mrow[:, :])
        v.tensor_copy(self.pcol[:, :], self.pcol_i[:, :])
        v.tensor_copy(self.TV[:, :], self.TVi[:, :])
        v.tensor_copy(self.identb[:, :], self.c.ident[:, :])
        v.tensor_copy(self.cand[:, :], self.BT[:, 0:1])
        v.drain()
        v.tensor_scalar(self.incl[:, :], self.mcolf[:, :], self.mrowf[:, 0:1], None, ALU.is_ge)
        v.tensor_scalar(self.strict[:, :], self.mcolf[:, :], self.mrowf[:, 0:1], None, ALU.is_gt)
        v.tensor_scalar(self.mcol[:, :], self.mcol[:, :], E - 1, None, ALU.bitwise_and)
        v.tensor_scalar(self.mrow[:, :], self.mrow[:, :], E - 1, None, ALU.bitwise_and)
        v.drain()
        v.tensor_copy(self.mcolf[:, :], self.mcol[:, :])
        v.tensor_copy(self.mrowf[:, :], self.mrow[:, :])
        v.drain()
        v.tensor_scalar(self.same[:, :], self.mcolf[:, :], self.mrowf[:, 0:1], None, ALU.is_equal)
        v.wait_ge(self.s_scv, 1)
        v.drain()

    def v_masks(self, v):
        thr = self.cand[:, 0:1].bitcast(F32)
        v.tensor_scalar(self.MT[:, 0, :], self.SCT[:, :], thr, None, ALU.is_gt)
        v.tensor_scalar(self.MT[:, 1, :], self.SCT[:, :], thr, None, ALU.is_equal).then_inc(self.s_mask, 1)

    def p_masks(self, pe):
        pe.wait_ge(self.s_mask, 1)
        for k in range(2):
            out = self.ps[:, k, :].bitcast(BF16)
            for t in range(8):
                i = pe.transpose(out[:, t * P:(t + 1) * P], self.MT[:, k, t * P:(t + 1) * P], self.identb[:, :])
        i.then_inc(self.s_mt, 1)

    def a_mk(self, a):
        a.wait_ge(self.s_mt, 1)
        for k in range(2):
            for h in range(2):
                i = a.activation(self.MK[:, :, k, h * P:(h + 1) * P],
                                 self.ps[:, k, :].bitcast(BF16)[:, h * 512:(h + 1) * 512].rearrange("p (j q) -> p j q", j=4), ACT.Copy)
        i.then_inc(self.s_mk, 1)

    def mk(self, j):
        return self.MK[:, j, :, :].rearrange("p k n -> p (k n)")

    def p_tot(self, pe):
        pe.wait_ge(self.s_mk, 1)
        for j in range(4):
            i = pe.matmul(self.ps[:, 0, :], self.ones[:, :], self.mk(j), start=(j == 0), stop=(j == 3))
        i.then_inc(self.s_tot, 1)

    def a_tot(self, a):
        a.wait_ge(self.s_tot, 1)
        a.activation(self.tot[0][:, :, :, :].rearrange("p k u e -> p (k u e)"), self.ps[:, 0, :], ACT.Copy).then_inc(self.s_totc, 1)

    def p_rank(self, pe, js):
        for j in js:
            pe.wait_ge(self.s_totc, 1)
            if j >= 1:
                wait(pe, self.s_rkc, j - 1)
            for jj in range(4):
                i = pe.matmul(self.ps[:, (j + 1) % 2, :], (self.incl if jj < j else self.strict)[:, :], self.mk(jj),
                              start=(jj == 0), stop=(jj == 3))
            i.then_inc(self.s_rank, 1)

    def a_rank(self, a, js):
        for j in js:
            a.wait_ge(self.s_rank, j + 1)
            a.activation(self.RK[:, j, :, :].rearrange("p k n -> p (k n)"), self.ps[:, (j + 1) % 2, :], ACT.Copy).then_inc(self.s_rkc, 1)

    def v_prefix(self, v):
        v.wait_ge(self.s_totc, 1)
        cur, step = 0, 1
        while step < NU:
            a, b = self.tot[cur], self.tot[1 - cur]
            v.tensor_copy(b[:, :, 0:step, :], a[:, :, 0:step, :])
            v.tensor_tensor(b[:, :, step:NU, :], a[:, :, step:NU, :], a[:, :, 0:NU - step, :], ALU.add)
            v.drain()
            cur, step = 1 - cur, 2 * step
        self.inc = self.tot[cur]

    def v_ahead(self, v):
        pre, inc = self.PRE[:, :, :].rearrange("p k (u e) -> p k u e", e=E), self.inc
        v.memset(pre[:, :, 0:1, :], 0.0)
        v.tensor_copy(pre[:, :, 1:NU, :], inc[:, :, 0:NU - 1, :])
        v.drain()
        v.tensor_tensor(pre[:, 1, :, :], pre[:, 1, :, :], inc[:, 0, NU - 1:NU, :].to_broadcast([P, NU, E]), ALU.add)
        v.drain()

    def v_rank(self, v):
        v.wait_ge(self.s_rkc, 4)
        v.tensor_tensor(self.RK[:, :, :, :].rearrange("p j k n -> p j (k n)"), self.RK[:, :, :, :].rearrange("p j k n -> p j (k n)"),
                        self.PRE[:, :, :].rearrange("p k n -> p (k n)").unsqueeze(1).to_broadcast([P, 4, 2 * NG]), ALU.add)
        v.drain()

    def v_slot(self, v):
        for k in range(2):
            v.scalar_tensor_tensor(self.RK[:, :, k, :], self.RK[:, :, k, :], -4096.0, self.MK[:, :, k, :], ALU.add, ALU.mult)
        v.drain()

    def v_slot2(self, v):
        v.tensor_tensor(self.RK[:, :, 0, :], self.RK[:, :, 0, :], self.RK[:, :, 1, :], ALU.add)
        v.drain()
        v.tensor_scalar(self.SCT[:, :].bitcast(I32).rearrange("p (j n) -> p j n", j=4), self.RK[:, :, 0, :], 4096.0, None, ALU.add)
        v.drain()

    def v_digits(self, v):
        slot = self.SCT[:, :].bitcast(I32)
        v.tensor_scalar(self.digit[:, :], slot, 5, None, ALU.logical_shift_right)
        v.drain()
        v.tensor_scalar(slot, slot, SL - 1, None, ALU.bitwise_and).then_inc(self.s_dig, 1)

    def a_digits(self, a):
        a.wait_ge(self.s_dig, 1)
        for dst, src in ((self.LO, self.SCT[:, :].bitcast(I32)), (self.HI, self.digit[:, :])):
            i = a.activation(dst[:, :, :].rearrange("p g (t e) -> p g t e", e=GE),
                             src.rearrange("p (t g e) -> p g t e", g=GROUPS, e=GE), ACT.Copy).then_inc(self.s_digc, 1)

    def one_hot(self, v, out, digits, k, h):
        g, cols = self.cols(k)
        a, n = h * SL // 2, SL // 2
        return v.tensor_tensor(out[:, a:a + n, :], digits[:, g, cols].unsqueeze(1).to_broadcast([P, n, CW]),
                               self.VI[:, a:a + n, :], ALU.is_equal)

    def v_lo1(self, v, k, h):
        if h == 0:
            v.wait_ge(self.s_digc, 2)
            wait(v, self.s_mul, 2 * (k - 1))
        g, cols = self.cols(k)
        a, n = h * SL // 2, SL // 2
        split = lambda x: x.rearrange("p v (t e) -> p v t e", e=GE)
        v.tensor_tensor(self.lo1[:, k % 2, :, a:a + n, :].rearrange("p t v e -> p v t e"),
                        split(self.LO[:, g, cols].unsqueeze(1).to_broadcast([P, n, CW])),
                        split(self.VI[:, a:a + n, :]), ALU.is_equal).then_inc(self.s_lo1, 1)

    def v_hi1(self, v, k, h):
        if h == 0 and k:
            v.wait_ge(self.s_val, k)
            v.wait_ge(self.s_val_pool, k)
        self.one_hot(v, self.hi1, self.HI, k, h).then_inc(self.s_hi1, 1)

    def v_val(self, v, k):
        v.wait_ge(self.s_hi1, 2 * k + 2)
        wait(v, self.s_mul, 2 * (k - 1))
        v.tensor_scalar(self.val[:, k % 2, 0, :, :], self.hi1[:, :, :], self.pcol[:, 0:1], None, ALU.mult)
        v.tensor_tensor(self.val[:, k % 2, 1, 0:SL // 2, :], self.hi1[:, 0:SL // 2, :], self.tile_numbers(k, SL // 2),
                        ALU.mult).then_inc(self.s_val, 1)

    def p_lists(self, pe, k, h):
        g = k // 2
        if h == 0:
            pe.wait_ge(self.s_lo1, 2 * k + 2)
            pe.wait_ge(self.s_val, k + 1)
            pe.wait_ge(self.s_val_pool, k + 1)
            if k % 2 == 0:
                wait(pe, self.s_dec, g - 1)
        tiles = CW // GE
        for t in range(h * tiles // 2, (h + 1) * tiles // 2):
            cols = slice(t * GE, (t + 1) * GE)
            i = pe.matmul(self.ps[:, g % 2, 0:2 * SL * GE], self.lo1[:, k % 2, t, :, :].rearrange("p v e -> p (v e)"), self.val[:, k % 2, :, :, cols],
                          start=(k % 2 == 0 and t == 0), stop=(k % 2 == 1 and t == tiles - 1))
        i.then_inc(self.s_mul, 1)

    def a_dec(self, a, g):
        a.wait_ge(self.s_mul, 4 * (g + 1))
        wait(a, self.s_ls, g)
        a.activation(self.vi[:, :, :].rearrange("m a (e h) -> m a h e", e=GE),
                     self.ps[:, g % 2, 0:2 * SL * GE].rearrange("m (a h e) -> m a h e", a=2, e=GE), ACT.Copy).then_inc(self.s_dec, 1)

    def v_dec(self, v, g):
        v.wait_ge(self.s_dec, g + 1)
        u, j = self.vu[:, 0, :], self.vj[:, 0, :]
        v.tensor_scalar(u, self.vi[:, 1, :], NU - 1, None, ALU.bitwise_and)
        v.tensor_scalar(j, self.vi[:, 1, :], 4, None, ALU.logical_shift_right)
        v.drain()
        v.scalar_tensor_tensor(j, self.vi[:, 0, :], 4.0, j, ALU.mult, ALU.add)
        v.drain()
        v.scalar_tensor_tensor(self.LS[:, g, :, :].rearrange("m e h -> m (e h)"), u, 512.0, j, ALU.mult, ALU.add)
        v.drain().then_inc(self.s_ls, 1)

    def store(self, sp):
        sp.wait_ge(self.s_ls, GROUPS)
        for e in range(GE):
            sp.dma_start(self.io["LIST"].rearrange("(g e) (l h) -> e l g h", e=GE, l=SL)[e],
                         self.LS[e:e + GE * (SL - 1) + 1:GE, :, e, :]).then_inc(self.s_lst, 16)
        sp.wait_ge(self.s_lst, 16 * GE)
        sp.dma_start(self.c.IDX[:, :, :], self.io["LIST"].rearrange("e (p c) -> p e c", p=P)).then_inc(self.s_lst, 16)
        sp.wait_ge(self.s_lst, 16 * (GE + 1))


def mlp(nc, io, c, shared):
    NI = (I_SH if shared else I_EXP) // P
    N = NB if shared else E
    W_N = 1 if shared else 2
    SLOTS = NI + 2
    with ExitStack() as ctx:
        tag = "sh_" if shared else "ex_"
        sb = lambda n, s, d=F32: ctx.enter_context(nc.sbuf_tensor(tag + n, s, d))
        pair = lambda n, s: (sb(n + "_hi", s, F32R), sb(n + "_lo", s, F32R))
        if shared:
            wg, wu, wd = [c.sw["g"]], [c.sw["u"]], c.sw["d"]
        else:
            wg, wu = ([pair(f"{w}{i}", [P, KD, NI * P]) for i in range(W_N)] for w in ("wg", "wu"))
            wd = [t[:, :, :] for t in pair("wd", [P, NI, D])]
        XT = [pair(f"XT{i}", [P, KD, 512]) for i in range(2)]
        GL, HF = sb("GL", [P, 2, 512]), sb("HF", [P, 2, 512])
        H = pair("H", [P, SLOTS, 512])
        OUT = sb("OUT", [P, 8, D])
        lists = None
        psG = ctx.enter_context(nc.psum_tensor(tag + "psG", [P, 2, 512], F32))
        psU = ctx.enter_context(nc.psum_tensor(tag + "psU", [P, 2, 512], F32))
        psX = ctx.enter_context(nc.psum_tensor(tag + "psXT", [P, 2, 512], F32))
        psD = ctx.enter_context(nc.psum_tensor(tag + "psD", [P, 2, 512], F32))
        sem = lambda n: ctx.enter_context(nc.semaphore(tag + n))
        s_up, s_gelu, s_mul, s_hhi, s_hlo = (sem(n) for n in ("s_up", "s_gelu", "s_mul", "s_hhi", "s_hlo"))
        s_dn, s_ev = sem("s_dn"), sem("s_ev")
        s_xt, s_xhi, s_xlo = sem("s_xt"), sem("s_xhi"), sem("s_xlo")
        s_raw = {"g": c.s_raw[0], "u": c.s_raw[1], "d": sem("s_raw_d")}
        s_whi = {n: sem("s_whi_" + n) for n in "gud"}
        s_wlo = {n: sem("s_wlo_" + n) for n in "gud"}
        EV0 = 2
        if shared:
            XR, s_xr = [c.XR0, sb("XR1", [P, KD, 512])], [c.s_xr0, sem("s_xr1")]
            s_st = [sem("s_st0"), sem("s_st1")]
            lists = TopK(nc, io, c, sb, sem, psX)
        else:
            raw = {"g": c.X1a[:, 0, :], "u": c.X1a[:, 1, :], "d": c.X1b[:, 0, :]}
            XG = [sb(f"XG{i}", [P, 8, ROW]) for i in range(2)]
            GI = [sb(f"GI{i}", [P, 8], I32) for i in range(2)]
            TW = [sb(f"TW{i}", [P, 8]) for i in range(2)]
            s_gi, s_tw = sem("s_gi"), sem("s_tw")
            s_ga = [[sem(f"s_ga{q}{half}") for half in range(2)] for q in range(2)]
            s_sc = [sem("s_sc0"), sem("s_sc1")]
            s_x1 = sem("s_x1")
        blk = ctx.enter_context(nc.Block())

        def slot(tb, it):
            return it if tb == 0 or it >= 2 else NI + it

        def units(body):
            def run(eng):
                if shared:
                    body(0, 0, False)
                    with eng.Fori(1, 4) as n:
                        body(n, 0, False)
                    for n in range(4, N):
                        body(n, 0, n == N - 1)
                    return
                for q in range(2):
                    body(q, q, False)
                with eng.Fori(1, N // 2 - 1) as r:
                    for q in range(2):
                        body(2 * r + q, q, False)
                for q in range(2):
                    body(N - 2 + q, q, q == 1)
            return run

        def schedule(n, q, last, step, down):
            for tb in range(2):
                h = 2 * n + tb
                for it in range(2, NI):
                    step(n, h, q, tb, it)
                if not (last and tb):
                    n2, q2, tb2 = (n, q, 1) if tb == 0 else (n + 1, 1 - q, 0)
                    for it in range(2):
                        step(n2, h + 1, q2, tb2, it)
                down(n, h, q, tb)

        @blk.tensor
        def _(pe):
            def turn(n, h, q, tb, dk):
                if dk == 0:
                    wait(pe, s_ga[q][tb], 64 * (n // 2 + 1) if isinstance(n, int) else 32 * (n + 2 - q))
                wait(pe, s_xlo, 2 * h + dk - 1)
                for t in range(4):
                    i = pe.transpose(psX[:, dk, t * P:(t + 1) * P], XG[q][:, 4 * tb + t, dk * P:(dk + 1) * P], c.ident[:, :])
                i.then_inc(s_xt, 1)

            def step(n, h, q, tb, it):
                s = NI * h + it
                if not shared and tb == 0 and it % 2 == 0:
                    for w in "gu":
                        wait(pe, s_wlo[w], 4 * n + it // 2 + 1)
                if it == 0:
                    wait(pe, s_xlo, 2 * (h + 1))
                wait(pe, s_mul, s - 1)
                cols = slice(it * P, (it + 1) * P)
                for ps, w in ((psG, wg), (psU, wu)):
                    w_hi, w_lo = w[q % W_N]
                    for k in range(KD):
                        i = mm3(pe, ps[:, it % 2, :], w_hi[:, k, cols], w_lo[:, k, cols],
                                XT[tb][0][:, k, :], XT[tb][1][:, k, :], k == 0, k == KD - 1)
                    if lists and w is wg:
                        lists.pe_middle(pe, s)
                i.then_inc(s_up, 1)
                if not shared and it in (3, 4):
                    n2, q2, tb2 = (n, q, 1) if tb == 0 else (n + 1, 1 - q, 0)
                    if not (isinstance(n2, int) and n2 >= N):
                        turn(n2, h + 1, q2, tb2, it - 3)
                if lists:
                    lists.pe_step(pe, s)

            def down(n, h, q, tb):
                wait(pe, s_hlo, NI * (h + 1) - 2)
                if not shared and tb == 0:
                    wait(pe, s_wlo["d"], 4 * (n + 1))
                for t in range(4):
                    wait(pe, s_ev, EV0 + 4 * h + t - 1)
                    for it in range(NI):
                        if t == 0 and it >= NI - 2:
                            wait(pe, s_hlo, NI * h + it + 1)
                        z = slot(tb, it)
                        i = mm3(pe, psD[:, t % 2, 0:D], H[0][:, z, t * P:(t + 1) * P], H[1][:, z, t * P:(t + 1) * P],
                                wd[0][:, it, :], wd[1][:, it, :], it == 0, it == NI - 1)
                    i.then_inc(s_dn, 1)
                if lists and isinstance(h, int) and h < 2 * N - 1:
                    lists.run(lists.pe, pe, NI * (h + 1) + 1.5)

            if not shared:
                for dk in range(KD):
                    turn(0, 0, 0, 0, dk)
            for it in range(2):
                step(0, 0, 0, 0, it)
            units(lambda n, q, last: schedule(n, q, last, step, down))(pe)
            if lists:
                lists.run(lists.pe, pe, 2 * NI * N - 1, True)

        def weight_part(w, q, quarter):
            if w == "d":
                a = NI // 4
                cut = lambda t: t[:, quarter * a:(quarter + 1) * a, :]
                return cut(raw[w].rearrange("p (i n) -> p i n", n=D)), cut(wd[0]), cut(wd[1])
            a = NI * P // 4
            cut = lambda t: t[:, :, quarter * a:(quarter + 1) * a]
            hi, lo = (wg if w == "g" else wu)[q % W_N]
            return cut(raw[w].rearrange("p (k n) -> p k n", k=KD)), cut(hi), cut(lo)

        def w_hi(a, w, n, q, quarter):
            src, hi, _ = weight_part(w, q, quarter)
            if quarter == 0:
                wait(a, s_raw[w], 16 * (n + 1))
                if w == "d":
                    wait(a, s_dn, 8 * n)
                else:
                    wait(a, s_up, 2 * NI * (n - 1) if isinstance(n, int) else NI * 2 * (n - 1))
            a.activation(hi, src, ACT.Copy).then_inc(s_whi[w], 1)

        def w_lo(v, w, n, q, quarter):
            src, hi, lo = weight_part(w, q, quarter)
            wait(v, s_whi[w], 4 * n + quarter + 1)
            v.tensor_tensor(lo, src, hi.bitcast(F32), ALU.subtract).then_inc(s_wlo[w], 1)

        def weight_task(n, tb, it, last):
            if shared:
                return None
            if tb == 0:
                return ("d", 0, it - 2) if 2 <= it < 6 else None
            if last:
                return None
            return ("g", 1, it) if it < 4 else ("u", 1, it - 4)

        def x_part(h, tb, dk):
            src = XR[tb][:, dk, :] if shared else psX[:, dk, :]
            return src, XT[tb][0][:, dk, :], XT[tb][1][:, dk, :]

        def x_hi(a, n, h, tb, dk):
            src, hi, _ = x_part(h, tb, dk)
            if dk == 0:
                wait(a, s_up, NI * (h - 1))
                if shared:
                    wait(a, s_xr[tb], 16 * (n + 1))
            if not shared:
                wait(a, s_xt, 2 * h + dk + 1)
            a.activation(hi, src, ACT.Copy).then_inc(s_xhi, 1)

        def x_lo(v, n, h, tb, dk):
            src, hi, lo = x_part(h, tb, dk)
            wait(v, s_xhi, 2 * h + dk + 1)
            v.tensor_tensor(lo, src, hi.bitcast(F32), ALU.subtract).then_inc(s_xlo, 1)

        XAT = (0, 1) if shared else (3, 4)

        def next_x(f, eng, n, h, tb, it):
            if it in XAT:
                n2, tb2 = (n, 1) if tb == 0 else (n + 1, 0)
                if not (isinstance(n2, int) and n2 >= N):
                    f(eng, n2, h + 1, tb2, it - XAT[0])
                    return n2, tb2

        @blk.scalar
        def _(a):
            a.sem_inc(s_ev, EV0)

            def part_hi(h, tb, it):
                wait(a, s_mul, NI * h + it + 1)
                if it == 2:
                    wait(a, s_dn, 4 * h)
                a.activation(H[0][:, slot(tb, it), :], HF[:, it % 2, :], ACT.Copy).then_inc(s_hhi, 1)

            def step(n, h, q, tb, it, last=False):
                s = NI * h + it
                wait(a, s_up, s + 1)
                wait(a, s_mul, s - 1)
                a.activation(GL[:, it % 2, :], psG[:, it % 2, :], ACT.Gelu).then_inc(s_gelu, 1)
                if it:
                    part_hi(h, tb, it - 1)
                elif not (isinstance(s, int) and s == 0):
                    part_hi(h - 1, 1 - tb, NI - 1)
                task = weight_task(n, tb, it, isinstance(n, int) and n == N - 1)
                if task:
                    w_hi(a, task[0], n + task[1], (q + task[1]) % 2, task[2])
                next_x(x_hi, a, n, h, tb, it)
                if lists:
                    lists.act_step(a, s)

            def down(n, h, q, tb):
                if isinstance(h, int) and h == 2 * N - 1:
                    part_hi(h, tb, NI - 1)
                for t in range(4):
                    z = 4 * tb + t
                    wait(a, s_dn, 4 * h + t + 1)
                    if t == 0:
                        if shared:
                            wait(a, s_st[tb], 16 * n)
                        elif tb == 0:
                            wait(a, s_tw, n + 1)
                            wait(a, s_sc[1 - q], 64 * (n - q) + 128 * q)
                    scale = 1.0 if shared else TW[q][:, z:z + 1]
                    a.activation(OUT[:, z, :], psD[:, t % 2, 0:D], ACT.Copy, scale=scale).then_inc(s_ev, 1)
                if lists and isinstance(h, int) and h < 2 * N - 1:
                    lists.run(lists.act, a, NI * (h + 1) + 1.5)

            if not shared:
                for quarter in range(4):
                    for w in "gu":
                        w_hi(a, w, 0, 0, quarter)
            for dk in range(KD):
                x_hi(a, 0, 0, 0, dk)
            for it in range(2):
                step(0, 0, 0, 0, it)
            units(lambda n, q, last: schedule(n, q, last, step, down))(a)
            if lists:
                lists.run(lists.act, a, 2 * NI * N - 1, True)

        @blk.vector
        def _(v):
            def part_lo(h, tb, it):
                wait(v, s_hhi, NI * h + it + 1)
                v.tensor_tensor(H[1][:, slot(tb, it), :], HF[:, it % 2, :],
                                H[0][:, slot(tb, it), :].bitcast(F32), ALU.subtract).then_inc(s_hlo, 1)

            def scores_of(n, q):
                for half in range(2):
                    wait(v, s_ga[q][half], 64 * (n // 2 + 1) if isinstance(n, int) else 32 * (n + 2 - q))
                wait(v, s_ev, EV0 + 8 * (n - 1) if not (isinstance(n, int) and n < 2) else 0)
                v.tensor_copy(TW[q][:, :], XG[q][:, :, bass.ds(D + n, 1)].rearrange("p t o -> p (t o)")).then_inc(s_tw, 1)

            def step(n, h, q, tb, it):
                s = NI * h + it
                wait(v, s_gelu, s + 1)
                if not (isinstance(s, int) and s < 2):
                    wait(v, s_hlo, s - 1)
                v.tensor_tensor(HF[:, it % 2, :], psU[:, it % 2, :], GL[:, it % 2, :], ALU.mult).then_inc(s_mul, 1)
                if it:
                    part_lo(h, tb, it - 1)
                elif not (isinstance(s, int) and s == 0):
                    part_lo(h - 1, 1 - tb, NI - 1)
                task = weight_task(n, tb, it, isinstance(n, int) and n == N - 1)
                if task:
                    w_lo(v, task[0], n + task[1], (q + task[1]) % 2, task[2])
                got = next_x(x_lo, v, n, h, tb, it)
                if lists:
                    lists.vec_step(v, s)
                if got and not shared and it == XAT[1] and got[1] == 0:
                    scores_of(got[0], 1 - q)

            def down(n, h, q, tb):
                if isinstance(h, int) and h == 2 * N - 1:
                    part_lo(h, tb, NI - 1)
                if lists and isinstance(h, int) and h < 2 * N - 1:
                    lists.run(lists.vec, v, NI * (h + 1) + 1.5)

            if not shared:
                for quarter in range(4):
                    for w in "gu":
                        w_lo(v, w, 0, 0, quarter)
            for dk in range(KD):
                x_lo(v, 0, 0, 0, dk)
            if not shared:
                scores_of(0, 0)
            for it in range(2):
                step(0, 0, 0, 0, it)
            units(lambda n, q, last: schedule(n, q, last, step, down))(v)
            if lists:
                lists.run(lists.vec, v, 2 * NI * N - 1, True)

        if shared:
            @blk.sync
            def _(sp):
                def load(n, tb):
                    wait(sp, s_xlo, 2 * (2 * n + tb - 1))
                    sp.dma_start(XR[tb][:, :, :], io["XN2T"][n][:, :, tb * 512:(tb + 1) * 512]).then_inc(s_xr[tb], 16)

                load(0, 1)
                for i, (w, name) in enumerate((("g", "wg"), ("u", "wu"))):
                    sp.dma_start(c.X1a[:, i, :], io[name].rearrange("e p a n -> e p (a n)")[0]).then_inc(c.s_raw[i], 16)

                def store(n, tb):
                    wait(sp, s_ev, EV0 + 4 * (2 * n + tb + 1))
                    sp.dma_start(io["ACC"].rearrange("(n h p j) d -> n h p (j d)", n=NB, h=2, p=P)[n][tb],
                                 OUT[:, 4 * tb:4 * tb + 4, :].rearrange("p j d -> p (j d)")).then_inc(s_st[tb], 16)

                def body(n, q, last):
                    for tb in range(2):
                        if not last:
                            load(n + 1, tb)
                        store(n, tb)
                units(body)(sp)
                for tb in range(2):
                    sp.wait_ge(s_st[tb], 16 * N)
                    sp.wait_ge(c.s_raw[tb], 16)

            @blk.gpsimd
            def _(g):
                lists.pool(g)
                lists.store(g)
        else:
            @blk.sync
            def _(sp):
                def load(w, name, n):
                    wait(sp, s_wlo[w], 4 * n)
                    wait(sp, s_whi[w], 4 * n)
                    sp.dma_start(raw[w], io[name].rearrange("e p a n -> e p (a n)")[n]).then_inc(s_raw[w], 16)
                def load_x1(b):
                    dst = c.X1a[:, b, :] if b < 2 else c.X1b[:, b - 6, :]
                    sp.dma_start(dst.rearrange("p (h c) -> p h c", h=2), rows_of(io["X1"], b)).then_inc(s_x1, 16)

                for half in range(2):
                    sp.wait_ge(s_ga[0][half], 64)
                load("d", "wd", 0)
                load_x1(NB - 1)

                def body(n, q, last):
                    if not last:
                        load("g", "wg", n + 1)
                        load("u", "wu", n + 1)
                        load("d", "wd", n + 1)
                units(body)(sp)
                wait(sp, s_wlo["u"], 4 * N)
                load_x1(0)
                load_x1(1)
                wait(sp, s_wlo["d"], 4 * N)
                load_x1(6)
                sp.wait_ge(s_x1, 16 * 4)

            s_pass = sem("s_pass")

            @blk.gpsimd
            def _(g):
                def pass_wait(s, value):
                    wait(g, s, value)
                    g.sem_inc(s_pass, 1)

                def gather(n, q):
                    wait(g, s_xt, 4 * (n - 1))
                    wait(g, s_tw, n - 1)
                    if not (isinstance(n, int) and n < 2):
                        wait(g, s_sc[q], 64 * (n - q))
                    g.tensor_copy(GI[q][:, :], c.IDX[:, bass.ds(n, 1), :].rearrange("p o c -> p (o c)")).then_inc(s_gi, 1)
                    pass_wait(s_gi, n + 1)
                    for t in range(8):
                        g.indirect_dma_start(out=XG[q][:, t, :], out_offset=None, in_=io["XN"],
                                             in_offset=bass.IndirectOffsetOnAxis(ap=GI[q][:, t:t + 1], axis=0)).then_inc(s_ga[q][t // 4], 16)

                def scatter(n, q, tb):
                    for t in range(4 * tb, 4 * tb + 4):
                        if t == 0:
                            wait(g, s_sc[1 - q], 64 * (n - q) + 128 * q)
                        pass_wait(s_ev, EV0 + 8 * n + t + 1)
                        g.indirect_dma_start(out=io["ACC"], out_offset=bass.IndirectOffsetOnAxis(ap=GI[q][:, t:t + 1], axis=0),
                                             in_=OUT[:, t, :], in_offset=None, compute_op=ALU.add).then_inc(s_sc[q], 16)

                gather(0, 0)

                def body(n, q, last):
                    if not last:
                        gather(n + 1, 1 - q)
                    for tb in range(2):
                        scatter(n, q, tb)
                units(body)(g)
                for q in range(2):
                    g.wait_ge(s_sc[q], 64 * N)


def output(nc, io, c):
    NP = NB // 2
    with ExitStack() as ctx:
        sb = lambda n, s, d=F32: ctx.enter_context(nc.sbuf_tensor(n, s, d))
        F = sb("F", [P, NB, NT, D])
        xm = sb("x1_m", [P, 4, NT, D])
        xa, xb = (t[:, :, :].rearrange("p b (t d) -> p b t d", t=NT) for t in (c.X1a, c.X1b))
        st, mv = sb("fst", [P, 2 * NT, 6]), sb("fmv", [P, 2 * NT, 2])
        ve, tmp = sb("fve", [P, 2 * NT]), sb("ftmp", [P, 2 * NT])
        rs, shift = sb("frs", [P, NP, 2 * NT]), sb("fsh", [P, NP, 2 * NT])
        sem = lambda n: ctx.enter_context(nc.semaphore(n))
        s_f, s_st = ([sem(f"{n}{i}") for i in range(2)] for n in ("s_f", "s_fst"))
        s_x = sem("s_fx")
        s_r = sem("s_fr")
        s_n, s_a = sem("s_fn"), sem("s_fa")
        s_al = sem("s_fal")
        blk = ctx.enter_context(nc.Block())

        def half(t, b, h):
            return t[:, b, 4 * h:4 * h + 4, :].rearrange("p t d -> p (t d)")

        @blk.sync
        def _(sp):
            def rows(t, b):
                return t[:, b, :, :].rearrange("p (h j) d -> p h (j d)", h=2)

            def load(p, i):
                src = rows_of(io["ACC"], 2 * p + i)
                wait(sp, s_f[i], 16 * p)
                sp.dma_start(rows(F, 2 * p + i), src).then_inc(s_f[i], 16)

            def store(p, i, s, value):
                dst, src = rows_of(io["out"], 2 * p + i), rows(F, 2 * p + i)
                wait(sp, s_st[i], 16 * p)
                wait(sp, s, value)
                sp.dma_start(dst, src).then_inc(s_st[i], 16)

            def load_x1(b):
                wait(sp, s_x, 16 * (b - 2))
                sp.dma_start(rows(xm, b - 2), rows_of(io["X1"], b)).then_inc(s_x, 16)

            for p in range(NP):
                for i in range(2):
                    load(p, i)
                    if 0 < p < NP - 1:
                        load_x1(2 * p + i)
            def store_half(i, h, s, value):
                wait(sp, s, value)
                sp.dma_start(rows_of(io["out"], NB - 2 + i)[:, h, :], rows(F, NB - 2 + i)[:, h, :]).then_inc(s_st[i], 16)

            for b in range(NB - 2):
                store(b // 2, b % 2, s_a, 2 * (b + 1))
            for h in range(2):
                store_half(0, h, s_a, 2 * (NB - 2) + h + 1)
                store_half(1, h, s_al, h + 1)
            for i in range(2):
                sp.wait_ge(s_st[i], 16 * (NP + 1))

        @blk.vector
        def _(v):
            def body(p):
                for i in range(2):
                    wait(v, s_f[i], 16 * (p + 1))
                    for t in range(NT):
                        v.bn_stats(st[:, i * NT + t, :], F[:, 2 * p + i, t, :])
                v.drain()
                for t in range(2 * NT):
                    v.bn_aggr(mv[:, t, :], st[:, t, :])
                v.drain()
                for part in range(2):
                    last = layernorm_scale(v, part, mv, ve[:, :], rs[:, p, :], shift[:, p, :], tmp[:, :], 2 * NT)
                last.then_inc(s_r, 1)

            body(0)
            with v.Fori(1, NP - 1) as p:
                body(p)
            body(NP - 1)
            b, p = NB - 1, NP - 1
            v.drain()
            for h in range(2):
                for t in range(4 * h, 4 * h + 4):
                    v.tensor_scalar(F[:, b, t, :], F[:, b, t, :], rs[:, p, NT + t:NT + t + 1], shift[:, p, NT + t:NT + t + 1],
                                    ALU.mult, ALU.add)
                v.drain()
                v.tensor_tensor(half(F, b, h), half(F, b, h), half(xb, 1, h), ALU.add).then_inc(s_al, 1)

        @blk.scalar
        def _(a):
            def body(p, n=2):
                wait(a, s_r, p + 1)
                for i in range(n):
                    for h in range(2):
                        for t in range(4 * h, 4 * h + 4):
                            z = i * NT + t
                            j = a.activation(F[:, 2 * p + i, t, :], F[:, 2 * p + i, t, :], ACT.Identity,
                                             bias=shift[:, p, z:z + 1], scale=rs[:, p, z:z + 1])
                        j.then_inc(s_n, 1)
            body(0)
            with a.Fori(1, NP - 1) as p:
                body(p)
            body(NP - 1, 1)

        @blk.gpsimd
        def _(g):
            def body(b, x1, slot):
                for h in range(2):
                    wait(g, s_n, 2 * b + h + 1)
                    g.tensor_tensor(half(F, b, h), half(F, b, h), half(x1, slot, h), ALU.add).then_inc(s_a, 1)
            for b in range(2):
                body(b, xa, b)
            with g.Fori(2, 6) as b:
                wait(g, s_x, 16 * (b - 1))
                body(b, xm, b - 2)
            body(6, xb, 0)


class Kept:
    pass


def build(nc, io, phases="abcde"):
    with ExitStack() as ctx:
        c = Kept()
        sb = lambda n, s, d=F32: ctx.enter_context(nc.sbuf_tensor(n, s, d))
        c.ident = sb("ident", [P, P])
        c.SC = sb("SC", [P, 4, NU, E])
        c.IDX = sb("IDX", [P, E, CAP // P], I32)
        c.X1a = sb("x1_a", [P, 2, NT * D])
        c.s_raw = [ctx.enter_context(nc.semaphore(f"s_raw_{w}")) for w in "gu"]
        with ExitStack() as shared:
            ss = lambda n, s, d=F32: shared.enter_context(nc.sbuf_tensor(n, s, d))
            c.XR0 = ss("XR0", [P, KD, 512])
            c.s_xr0 = shared.enter_context(nc.semaphore("s_xr0"))
            c.sw = {w: [ss(f"s{w}_{z}", [P, I_SH // P if w == "d" else KD, D if w == "d" else I_SH], F32R)[:, :, :] for z in (0, 1)]
                    for w in "gud"}
            with ExitStack() as inner:
                sa = lambda n, s, d=F32: inner.enter_context(nc.sbuf_tensor(n, s, d))
                c.gw = sa("gw", [P, KD, E])
                c.bias = sa("bias", [P, D])
                c.wv, c.wp, c.m = ([sa(f"{n}{z}", [P, KD, D], F32R) for z in (0, 1)] for n in ("wv_", "wp_", "m_"))
                attention(nc, io, c)
            if "c" in phases:
                mlp(nc, io, c, shared=True)
        c.X1b = sb("x1_b", [P, 2, NT * D])
        if "d" in phases:
            mlp(nc, io, c, shared=False)
        if "e" in phases:
            output(nc, io, c)


def layouts(i):
    a = {k: np.asarray(v) for k, v in i.items()}
    wqkv = a["L0_attn_w_qkv"]
    tiles = lambda w: np.ascontiguousarray(w.reshape(-1, P, w.shape[-1]).transpose(1, 0, 2))
    etiles = lambda w: np.ascontiguousarray(w.transpose(0, 2, 1).reshape(E, -1, P, w.shape[1]).transpose(0, 2, 1, 3))
    return {
        "x": np.ascontiguousarray(a["L0_attn_x"].reshape(T, D)),
        "wq": tiles(wqkv[0:D]), "wk": tiles(wqkv[D:2 * D]), "wv": tiles(wqkv[2 * D:].T), "wp": tiles(a["L0_attn_w_proj"].T),
        "bias": np.ascontiguousarray(a["L0_attn_b_proj"]),
        "gate": tiles(a["L0_ffn_gate_w"].T),
        "wg": etiles(a["L0_ffn_Wg"]), "wu": etiles(a["L0_ffn_Wu"]), "wd": etiles(a["L0_ffn_Wd"]),
        "sg": tiles(a["L0_ffn_Sg"].T), "su": tiles(a["L0_ffn_Su"].T), "sd": tiles(a["L0_ffn_Sd"].T),
    }


def kernel(**inputs):
    import concourse.bacc as bacc
    from concourse.bass_utils import run_bass_kernel_spmd as run

    arrays = {f"{n}_in": v for n, v in layouts(inputs).items()}
    nc = bacc.Bacc("TRN2", target_bir_lowering=False, num_devices=1)
    io = {n[:-3]: nc.dram_tensor(n, v.shape, mybir.dt.from_np(v.dtype), kind="ExternalInput").ap() for n, v in arrays.items()}
    io["out"] = nc.dram_tensor("out_dram", (T, D), F32, kind="ExternalOutput").ap()
    for n, shape, dt in (("XN", (T, ROW), F32), ("X1", (T, D), F32), ("XN2T", (NB, P, KD, S), F32), ("ACC", (T, D), F32),
                         ("LIST", (E, CAP), I32)):
        io[n] = nc.dram_tensor(n, shape, dt).ap()
    build(nc, io)
    r = run(nc, [arrays], core_ids=[0])
    return r.results[0]["out_dram"].reshape(NB, S, D)
```
